# Optimizing a Trainium2 kernel written in Bass

```python
import numpy as np
import jax
import jax.numpy as jnp

def _softmax(x, axis=-1):
    return jax.nn.softmax(x, axis=axis)

def _gelu(x):
    return jax.nn.gelu(x, approximate=True)

def _silu(x):
    return jax.nn.silu(x)

def _sigmoid(x):
    return jax.nn.sigmoid(x)

def _layernorm(x, axis=-1, eps=1e-05):
    m = jnp.mean(x, axis=axis, keepdims=True)
    v = jnp.var(x, axis=axis, keepdims=True)
    return (x - m) / jnp.sqrt(v + eps)

def _scatter_add(tgt, idx, src, axis=0):
    return tgt.at[idx].add(src)

def _segment_sum(src, seg, n):
    return jax.ops.segment_sum(src, seg, n)
kernel_name = 'mk_seq_preln_d4_jaxref_r8_494400'

def setup_inputs(seed: int=0):
    np.random.seed(seed)
    _w = jnp.asarray

    def _L0_attn_setup():
        import math
        import jax, jax.numpy as jnp
        import numpy as np
        LN_EPS = 1e-05

        def _relative_sinusoidal(t, hd, dtype):
            pos = jnp.arange(-(t - 1), t, dtype=dtype)[:, None]
            div = jnp.exp(jnp.arange(0, hd, 2, dtype=dtype) * (-math.log(10000.0) / hd))
            pe = jnp.zeros((2 * t - 1, hd), dtype=dtype)
            pe = pe.at[:, 0::2].set(jnp.sin(pos * div))
            pe = pe.at[:, 1::2].set(jnp.cos(pos * div))
            return pe
        key = jax.random.key(seed)
        ks = jax.random.split(key, 4)
        b, t, dim, H = (2, 256, 128, 16)
        hd = dim // H
        s = 0.02
        return {'x': jax.random.normal(ks[0], (b, t, dim), jnp.float32), 'ln_g': jnp.ones((dim,), jnp.float32), 'ln_b': jnp.zeros((dim,), jnp.float32), 'w_qkv': jax.random.normal(ks[1], (dim, 3 * dim), jnp.float32) * s, 'b_qkv': jnp.zeros((3 * dim,), jnp.float32), 'w_rel': jax.random.normal(ks[2], (hd, H), jnp.float32) * s, 'w_out': jax.random.normal(ks[3], (dim, dim), jnp.float32) * s, 'b_out': jnp.zeros((dim,), jnp.float32)}
    _L0_attn_in = _L0_attn_setup()

    def _L0_ffn_setup():
        import math
        import jax, jax.numpy as jnp
        import numpy as np
        D_MODEL = 128
        D_FF = 512
        N_EXPERTS = 8
        CAPACITY_FACTOR = 1.25
        L, B = (64, 8)

        def _route(tokens, router_w):
            T = tokens.shape[0]
            E = router_w.shape[0]
            capacity = int(math.ceil(T / E * CAPACITY_FACTOR))
            logits = tokens @ router_w.T
            probs = jax.nn.softmax(logits, axis=-1)
            top1_idx = jnp.argmax(probs, axis=-1)
            top1_prob = jnp.max(probs, axis=-1)
            order = jnp.lexsort((-top1_prob, top1_idx))
            sorted_e = top1_idx[order]
            counts = jnp.bincount(top1_idx, length=E)
            start = jnp.cumsum(counts) - counts
            pos_in_group = jnp.arange(T) - start[sorted_e]
            keep_sorted = pos_in_group < capacity
            keep = jnp.zeros((T,), bool).at[order].set(keep_sorted)
            return jnp.where(keep, top1_idx, 0).astype(jnp.int32)
        key = jax.random.key(seed)
        ks = jax.random.split(key, 6)
        s_in = 1.0 / math.sqrt(D_MODEL)
        s_ff = 1.0 / math.sqrt(D_FF)
        return {'x': jax.random.normal(ks[0], (L, B, D_MODEL), dtype=jnp.float32), 'router_w': jax.random.uniform(ks[1], (N_EXPERTS, D_MODEL), minval=-s_in, maxval=s_in), 'W1': jax.random.uniform(ks[2], (N_EXPERTS, D_MODEL, D_FF), minval=-s_in, maxval=s_in), 'b1': jax.random.uniform(ks[3], (N_EXPERTS, D_FF), minval=-s_in, maxval=s_in), 'W2': jax.random.uniform(ks[4], (N_EXPERTS, D_FF, D_MODEL), minval=-s_ff, maxval=s_ff), 'b2': jax.random.uniform(ks[5], (N_EXPERTS, D_MODEL), minval=-s_ff, maxval=s_ff)}
    _L0_ffn_in = _L0_ffn_setup()

    def _L1_attn_setup():
        import jax, jax.numpy as jnp
        import numpy as np
        DIM = 128
        STATE = 128
        BATCH, SEQ = (4, 512)
        key = jax.random.key(seed)
        ks = jax.random.split(key, 12)
        s = 1.0 / np.sqrt(DIM)
        s4 = 1.0 / np.sqrt(DIM // 4)
        ss = 1.0 / np.sqrt(STATE)
        inp = {'x': jax.random.normal(ks[0], (BATCH, SEQ, DIM), dtype=jnp.float32), 'W_B': jax.random.uniform(ks[1], (DIM, STATE), minval=-s, maxval=s), 'b_B': jax.random.uniform(ks[2], (STATE,), minval=-s, maxval=s), 'W_C': jax.random.uniform(ks[3], (DIM, STATE), minval=-s, maxval=s), 'b_C': jax.random.uniform(ks[4], (STATE,), minval=-s, maxval=s), 'W_dt1': jax.random.uniform(ks[5], (DIM, DIM // 4), minval=-s, maxval=s), 'b_dt1': jax.random.uniform(ks[6], (DIM // 4,), minval=-s, maxval=s), 'W_dt2': jax.random.uniform(ks[7], (DIM // 4, STATE), minval=-s4, maxval=s4), 'b_dt2': jnp.full((STATE,), -4.0, dtype=jnp.float32), 'omega_base': jax.random.normal(ks[8], (STATE,)) * 0.1, 'D': jnp.ones((DIM,), dtype=jnp.float32), 'W_out': jax.random.uniform(ks[9], (STATE, DIM), minval=-ss, maxval=ss), 'b_out': jax.random.uniform(ks[10], (DIM,), minval=-ss, maxval=ss)}
        return inp
    _L1_attn_in = _L1_attn_setup()

    def _L1_ffn_setup():
        import jax, jax.numpy as jnp
        import numpy as np
        from jax import lax
        DIM = 128
        N_EXPERTS = 16
        TOPK = 4
        N_GROUPS = 4
        TOPK_GROUPS = 2
        ROUTE_SCALE = 1.0
        INTER = 64
        SHARED_INTER = 2 * INTER

        def _gate(x, gate_w):
            T = x.shape[0]
            logits = x @ gate_w.T
            scores = jax.nn.softmax(logits.astype(jnp.float32), axis=-1)
            original_scores = scores
            g = scores.reshape(T, N_GROUPS, N_EXPERTS // N_GROUPS)
            group_scores = g.max(axis=-1)
            _, gidx = lax.top_k(group_scores, TOPK_GROUPS)
            gmask = jnp.zeros_like(group_scores).at[jnp.arange(T)[:, None], gidx].set(1.0)
            masked = (g * gmask[..., None]).reshape(T, N_EXPERTS)
            _, indices = lax.top_k(masked, TOPK)
            weights = jnp.take_along_axis(original_scores, indices, axis=1)
            weights = weights * ROUTE_SCALE
            return (weights.astype(x.dtype), indices)
        key = jax.random.key(seed)
        ks = jax.random.split(key, 8)
        s = lambda fan_in: 1.0 / np.sqrt(fan_in)
        return {'x': jax.random.normal(ks[0], (2, 128, DIM), dtype=jnp.float32), 'gate_w': jax.random.normal(ks[1], (N_EXPERTS, DIM), dtype=jnp.float32) * s(DIM), 'w1': jax.random.normal(ks[2], (N_EXPERTS, DIM, INTER), dtype=jnp.float32) * s(DIM), 'w2': jax.random.normal(ks[3], (N_EXPERTS, INTER, DIM), dtype=jnp.float32) * s(INTER), 'w3': jax.random.normal(ks[4], (N_EXPERTS, DIM, INTER), dtype=jnp.float32) * s(DIM), 'ws1': jax.random.normal(ks[5], (DIM, SHARED_INTER), dtype=jnp.float32) * s(DIM), 'ws2': jax.random.normal(ks[6], (SHARED_INTER, DIM), dtype=jnp.float32) * s(SHARED_INTER), 'ws3': jax.random.normal(ks[7], (DIM, SHARED_INTER), dtype=jnp.float32) * s(DIM)}
    _L1_ffn_in = _L1_ffn_setup()

    def _L2_attn_setup():
        import jax, jax.numpy as jnp
        import numpy as np
        import math
        E = 128
        H = 64
        B = 4
        S = 256
        key = jax.random.key(seed)
        ks = jax.random.split(key, 9)
        x = jax.random.normal(ks[0], (B, S, E), dtype=jnp.float32)

        def he(k, fan_in, shape):
            return jax.random.normal(k, shape, dtype=jnp.float32) * jnp.sqrt(2.0 / fan_in)
        wq = he(ks[1], E, (E, H))
        bq = jnp.zeros((H,), jnp.float32)
        wk = he(ks[2], E, (E, H))
        bk = jnp.zeros((H,), jnp.float32)
        wv = he(ks[3], E, (E, H))
        bv = jnp.zeros((H,), jnp.float32)
        wo = he(ks[4], H, (H, E))
        bo = jnp.zeros((E,), jnp.float32)
        return {'x': x, 'wq': wq, 'bq': bq, 'wk': wk, 'bk': bk, 'wv': wv, 'bv': bv, 'wo': wo, 'bo': bo}
    _L2_attn_in = _L2_attn_setup()

    def _L2_ffn_setup():
        import jax, jax.numpy as jnp
        import numpy as np
        H = 128
        I = 128
        E = 8
        key = jax.random.key(seed)
        ks = jax.random.split(key, 8)
        s = 0.02
        x = jax.random.normal(ks[0], (4, 256, H), dtype=jnp.float32)
        Wg = jax.random.normal(ks[1], (H, E), dtype=jnp.float32) * s
        bg = jnp.zeros((E,), dtype=jnp.float32)
        W1 = jax.random.normal(ks[2], (E, H, I), dtype=jnp.float32) * s
        b1 = jnp.zeros((E, I), dtype=jnp.float32)
        W2 = jax.random.normal(ks[3], (E, I, H), dtype=jnp.float32) * s
        b2 = jnp.zeros((E, H), dtype=jnp.float32)
        return {'x': x, 'Wg': Wg, 'bg': bg, 'W1': W1, 'b1': b1, 'W2': W2, 'b2': b2}
    _L2_ffn_in = _L2_ffn_setup()

    def _L3_attn_setup():
        import jax, jax.numpy as jnp
        import numpy as np
        GAMMA_MIN, GAMMA_MAX = (0.15, 1.0)
        ALPHA_CAP = 1.0
        EPS_L2 = 1e-08
        EPS_RMS = 1e-06

        def _rmsnorm(x, w):
            return x * jax.lax.rsqrt(jnp.mean(x * x, axis=-1, keepdims=True) + EPS_RMS) * w

        def _l2norm(x):
            n = jnp.linalg.norm(x, axis=-1, keepdims=True)
            return x / jnp.maximum(n, EPS_L2)

        def _causal_conv(h, kernel):
            K = kernel.shape[0]
            S = h.shape[1]
            hp = jnp.pad(h, ((0, 0), (K - 1, 0), (0, 0)))
            out = jnp.zeros_like(h)
            for j in range(K):
                out = out + kernel[j] * hp[:, K - 1 - j:K - 1 - j + S, :]
            return out
        B, S, D, R, K = (8, 128, 128, 16, 4)
        key = jax.random.key(seed)
        ks = jax.random.split(key, 8)
        return {'h': jax.random.normal(ks[0], (B, S, D), dtype=jnp.float32), 'u': jax.random.normal(ks[1], (D, R), dtype=jnp.float32) * 0.05, 'v': jax.random.normal(ks[2], (D, R), dtype=jnp.float32) * 0.05, 'decay_logit': jnp.zeros((R,), jnp.float32), 'alpha_logit': jnp.zeros((R,), jnp.float32), 'k_base_gate_logit': jnp.float32(0.0), 'k_base_kernel': jax.random.normal(ks[3], (K,), dtype=jnp.float32) * 0.05, 'proj_w': jax.random.normal(ks[4], (D, D), dtype=jnp.float32) * 0.02, 'proj_b': jnp.zeros((D,), jnp.float32), 'norm1_w': jnp.ones((D,), jnp.float32), 'norm2_w': jnp.ones((D,), jnp.float32), 'mlp_w1': jax.random.normal(ks[5], (D, 4 * D), dtype=jnp.float32) * 0.02, 'mlp_b1': jnp.zeros((4 * D,), jnp.float32), 'mlp_w2': jax.random.normal(ks[6], (4 * D, D), dtype=jnp.float32) * 0.02, 'mlp_b2': jnp.zeros((D,), jnp.float32)}
    _L3_attn_in = _L3_attn_setup()

    def _L3_ffn_setup():
        import jax, jax.numpy as jnp
        import numpy as np
        H = 128
        E = 8
        B, S = (4, 256)
        key = jax.random.key(seed)
        k1, k2, k3, k4 = jax.random.split(key, 4)
        x = jax.random.normal(k1, (B, S, H), dtype=jnp.float32)
        wg = jax.random.normal(k2, (H, E), dtype=jnp.float32) * 0.02
        W = jax.random.normal(k3, (E, H, H), dtype=jnp.float32) * 0.02
        b = jax.random.normal(k4, (E, H), dtype=jnp.float32) * 0.02
        return {'x': x, 'wg': wg, 'W': W, 'b': b}
    _L3_ffn_in = _L3_ffn_setup()
    _d = {'L0_attn_x': _L0_attn_in['x'], 'L0_attn_ln_g': _L0_attn_in['ln_g'], 'L0_attn_ln_b': _L0_attn_in['ln_b'], 'L0_attn_w_qkv': _L0_attn_in['w_qkv'], 'L0_attn_b_qkv': _L0_attn_in['b_qkv'], 'L0_attn_w_rel': _L0_attn_in['w_rel'], 'L0_attn_w_out': _L0_attn_in['w_out'], 'L0_attn_b_out': _L0_attn_in['b_out'], 'L0_ffn_router_w': _L0_ffn_in['router_w'], 'L0_ffn_W1': _L0_ffn_in['W1'], 'L0_ffn_b1': _L0_ffn_in['b1'], 'L0_ffn_W2': _L0_ffn_in['W2'], 'L0_ffn_b2': _L0_ffn_in['b2'], 'L1_attn_W_B': _L1_attn_in['W_B'], 'L1_attn_b_B': _L1_attn_in['b_B'], 'L1_attn_W_C': _L1_attn_in['W_C'], 'L1_attn_b_C': _L1_attn_in['b_C'], 'L1_attn_W_dt1': _L1_attn_in['W_dt1'], 'L1_attn_b_dt1': _L1_attn_in['b_dt1'], 'L1_attn_W_dt2': _L1_attn_in['W_dt2'], 'L1_attn_b_dt2': _L1_attn_in['b_dt2'], 'L1_attn_omega_base': _L1_attn_in['omega_base'], 'L1_attn_D': _L1_attn_in['D'], 'L1_attn_W_out': _L1_attn_in['W_out'], 'L1_attn_b_out': _L1_attn_in['b_out'], 'L1_ffn_gate_w': _L1_ffn_in['gate_w'], 'L1_ffn_w1': _L1_ffn_in['w1'], 'L1_ffn_w2': _L1_ffn_in['w2'], 'L1_ffn_w3': _L1_ffn_in['w3'], 'L1_ffn_ws1': _L1_ffn_in['ws1'], 'L1_ffn_ws2': _L1_ffn_in['ws2'], 'L1_ffn_ws3': _L1_ffn_in['ws3'], 'L2_attn_wq': _L2_attn_in['wq'], 'L2_attn_bq': _L2_attn_in['bq'], 'L2_attn_wk': _L2_attn_in['wk'], 'L2_attn_bk': _L2_attn_in['bk'], 'L2_attn_wv': _L2_attn_in['wv'], 'L2_attn_bv': _L2_attn_in['bv'], 'L2_attn_wo': _L2_attn_in['wo'], 'L2_attn_bo': _L2_attn_in['bo'], 'L2_ffn_Wg': _L2_ffn_in['Wg'], 'L2_ffn_bg': _L2_ffn_in['bg'], 'L2_ffn_W1': _L2_ffn_in['W1'], 'L2_ffn_b1': _L2_ffn_in['b1'], 'L2_ffn_W2': _L2_ffn_in['W2'], 'L2_ffn_b2': _L2_ffn_in['b2'], 'L3_attn_u': _L3_attn_in['u'], 'L3_attn_v': _L3_attn_in['v'], 'L3_attn_decay_logit': _L3_attn_in['decay_logit'], 'L3_attn_alpha_logit': _L3_attn_in['alpha_logit'], 'L3_attn_k_base_gate_logit': _L3_attn_in['k_base_gate_logit'], 'L3_attn_k_base_kernel': _L3_attn_in['k_base_kernel'], 'L3_attn_proj_w': _L3_attn_in['proj_w'], 'L3_attn_proj_b': _L3_attn_in['proj_b'], 'L3_attn_norm1_w': _L3_attn_in['norm1_w'], 'L3_attn_norm2_w': _L3_attn_in['norm2_w'], 'L3_attn_mlp_w1': _L3_attn_in['mlp_w1'], 'L3_attn_mlp_b1': _L3_attn_in['mlp_b1'], 'L3_attn_mlp_w2': _L3_attn_in['mlp_w2'], 'L3_attn_mlp_b2': _L3_attn_in['mlp_b2'], 'L3_ffn_wg': _L3_ffn_in['wg'], 'L3_ffn_W': _L3_ffn_in['W'], 'L3_ffn_b': _L3_ffn_in['b']}
    _x0 = _d['L0_attn_x']
    _d['L0_attn_x'] = jax.random.normal(jax.random.fold_in(jax.random.key(seed), 1), (8, 512, 128), dtype=_x0.dtype)
    del _x0
    return _d

def reference(L0_attn_x, L0_attn_ln_g, L0_attn_ln_b, L0_attn_w_qkv, L0_attn_b_qkv, L0_attn_w_rel, L0_attn_w_out, L0_attn_b_out, L0_ffn_router_w, L0_ffn_W1, L0_ffn_b1, L0_ffn_W2, L0_ffn_b2, L1_attn_W_B, L1_attn_b_B, L1_attn_W_C, L1_attn_b_C, L1_attn_W_dt1, L1_attn_b_dt1, L1_attn_W_dt2, L1_attn_b_dt2, L1_attn_omega_base, L1_attn_D, L1_attn_W_out, L1_attn_b_out, L1_ffn_gate_w, L1_ffn_w1, L1_ffn_w2, L1_ffn_w3, L1_ffn_ws1, L1_ffn_ws2, L1_ffn_ws3, L2_attn_wq, L2_attn_bq, L2_attn_wk, L2_attn_bk, L2_attn_wv, L2_attn_bv, L2_attn_wo, L2_attn_bo, L2_ffn_Wg, L2_ffn_bg, L2_ffn_W1, L2_ffn_b1, L2_ffn_W2, L2_ffn_b2, L3_attn_u, L3_attn_v, L3_attn_decay_logit, L3_attn_alpha_logit, L3_attn_k_base_gate_logit, L3_attn_k_base_kernel, L3_attn_proj_w, L3_attn_proj_b, L3_attn_norm1_w, L3_attn_norm2_w, L3_attn_mlp_w1, L3_attn_mlp_b1, L3_attn_mlp_w2, L3_attn_mlp_b2, L3_ffn_wg, L3_ffn_W, L3_ffn_b):

    def _L0_attn_ref(x, ln_g, ln_b, w_qkv, b_qkv, w_rel, w_out, b_out):
        import math
        import jax, jax.numpy as jnp
        import numpy as np
        LN_EPS = 1e-05

        def _relative_sinusoidal(t, hd, dtype):
            pos = jnp.arange(-(t - 1), t, dtype=dtype)[:, None]
            div = jnp.exp(jnp.arange(0, hd, 2, dtype=dtype) * (-math.log(10000.0) / hd))
            pe = jnp.zeros((2 * t - 1, hd), dtype=dtype)
            pe = pe.at[:, 0::2].set(jnp.sin(pos * div))
            pe = pe.at[:, 1::2].set(jnp.cos(pos * div))
            return pe
        b, t, dim = x.shape
        hd, H = w_rel.shape
        scale = hd ** (-0.5)
        mu = jnp.mean(x, axis=-1, keepdims=True)
        var = jnp.mean(jnp.square(x - mu), axis=-1, keepdims=True)
        xn = (x - mu) * jax.lax.rsqrt(var + LN_EPS) * ln_g + ln_b
        qkv = (xn @ w_qkv + b_qkv).reshape(b, t, 3, H, hd)
        qkv = jnp.transpose(qkv, (2, 0, 3, 1, 4))
        q, k, v = (qkv[0], qkv[1], qkv[2])
        scores = jnp.einsum('bhqd,bhkd->bhqk', q, k) * scale
        rel_pe = _relative_sinusoidal(t, hd, scores.dtype)
        rel_bias = rel_pe @ w_rel
        idx = jnp.arange(t)[:, None] - jnp.arange(t)[None, :] + (t - 1)
        bias = jnp.transpose(rel_bias[idx], (2, 0, 1))[None]
        attn = jax.nn.softmax(scores + bias, axis=-1)
        out = jnp.einsum('bhqk,bhkd->bhqd', attn, v)
        out = jnp.transpose(out, (0, 2, 1, 3)).reshape(b, t, dim)
        return out @ w_out + b_out

    def _L0_ffn_ref(x, router_w, W1, b1, W2, b2):
        import math
        import jax, jax.numpy as jnp
        import numpy as np
        D_MODEL = 128
        D_FF = 512
        N_EXPERTS = 8
        CAPACITY_FACTOR = 1.25
        L, B = (64, 8)

        def _route(tokens, router_w):
            T = tokens.shape[0]
            E = router_w.shape[0]
            capacity = int(math.ceil(T / E * CAPACITY_FACTOR))
            logits = tokens @ router_w.T
            probs = jax.nn.softmax(logits, axis=-1)
            top1_idx = jnp.argmax(probs, axis=-1)
            top1_prob = jnp.max(probs, axis=-1)
            order = jnp.lexsort((-top1_prob, top1_idx))
            sorted_e = top1_idx[order]
            counts = jnp.bincount(top1_idx, length=E)
            start = jnp.cumsum(counts) - counts
            pos_in_group = jnp.arange(T) - start[sorted_e]
            keep_sorted = pos_in_group < capacity
            keep = jnp.zeros((T,), bool).at[order].set(keep_sorted)
            return jnp.where(keep, top1_idx, 0).astype(jnp.int32)
        Lx, Bx, D = x.shape
        T = Lx * Bx
        E = router_w.shape[0]
        tokens = x.reshape(T, D)
        final_e = _route(tokens, router_w)
        out = jnp.zeros_like(tokens)
        for e in range(E):
            h = jax.nn.relu(tokens @ W1[e] + b1[e])
            y = h @ W2[e] + b2[e]
            out = out + jnp.where((final_e == e)[:, None], y, 0.0)
        return out.reshape(Lx, Bx, D)

    def _L1_attn_ref(x, W_B, b_B, W_C, b_C, W_dt1, b_dt1, W_dt2, b_dt2, omega_base, D, W_out, b_out):
        import jax, jax.numpy as jnp
        import numpy as np
        DIM = 128
        STATE = 128
        BATCH, SEQ = (4, 512)
        Bm = x @ W_B + b_B
        Cm = x @ W_C + b_C
        dt = jax.nn.softplus((x @ W_dt1 + b_dt1) @ W_dt2 + b_dt2)
        omega = omega_base * dt
        phi = jnp.cumsum(omega, axis=1)
        content = Bm * x[..., :STATE]
        cphi, sphi = (jnp.cos(phi), jnp.sin(phi))
        memory_real = jnp.cumsum(content * cphi, axis=1)
        memory_imag = jnp.cumsum(content * sphi, axis=1)
        retrieved = Cm * (memory_real * cphi + memory_imag * sphi)
        y = retrieved @ W_out + b_out + D * x
        return y

    def _L1_ffn_ref(x, gate_w, w1, w2, w3, ws1, ws2, ws3):
        import jax, jax.numpy as jnp
        import numpy as np
        from jax import lax
        DIM = 128
        N_EXPERTS = 16
        TOPK = 4
        N_GROUPS = 4
        TOPK_GROUPS = 2
        ROUTE_SCALE = 1.0
        INTER = 64
        SHARED_INTER = 2 * INTER

        def _gate(x, gate_w):
            T = x.shape[0]
            logits = x @ gate_w.T
            scores = jax.nn.softmax(logits.astype(jnp.float32), axis=-1)
            original_scores = scores
            g = scores.reshape(T, N_GROUPS, N_EXPERTS // N_GROUPS)
            group_scores = g.max(axis=-1)
            _, gidx = lax.top_k(group_scores, TOPK_GROUPS)
            gmask = jnp.zeros_like(group_scores).at[jnp.arange(T)[:, None], gidx].set(1.0)
            masked = (g * gmask[..., None]).reshape(T, N_EXPERTS)
            _, indices = lax.top_k(masked, TOPK)
            weights = jnp.take_along_axis(original_scores, indices, axis=1)
            weights = weights * ROUTE_SCALE
            return (weights.astype(x.dtype), indices)
        shape = x.shape
        xt = x.reshape(-1, DIM)
        T = xt.shape[0]
        weights, indices = _gate(xt, gate_w)
        c = jnp.zeros((T, N_EXPERTS), dtype=xt.dtype)
        c = c.at[jnp.arange(T)[:, None], indices].add(weights)
        h1 = jnp.einsum('td,edi->tei', xt, w1)
        h3 = jnp.einsum('td,edi->tei', xt, w3)
        a = jax.nn.silu(h1) * h3
        y = jnp.einsum('tei,eid,te->td', a, w2, c)
        z = jax.nn.silu(xt @ ws1) * (xt @ ws3) @ ws2
        return (y + z).reshape(shape)

    def _L2_attn_ref(x, wq, bq, wk, bk, wv, bv, wo, bo):
        import jax, jax.numpy as jnp
        import numpy as np
        import math
        E = 128
        H = 64
        B = 4
        S = 256
        q = x @ wq + bq
        k = x @ wk + bk
        v = x @ wv + bv
        scale = 1.0 / math.sqrt(H)
        w = jnp.einsum('bqh,bkh->bqk', q, k) * scale
        seq = x.shape[1]
        mask = jnp.triu(jnp.ones((1, seq, seq), dtype=w.dtype), 1) * -100000000000.0
        w = w + mask
        w = jax.nn.softmax(w, axis=-1)
        z = jnp.einsum('bqk,bkh->bqh', w, v)
        z = z @ wo + bo
        return z

    def _L2_ffn_ref(x, Wg, bg, W1, b1, W2, b2):
        import jax, jax.numpy as jnp
        import numpy as np
        H = 128
        I = 128
        E = 8
        B, S, Hd = x.shape
        xf = x.reshape(-1, Hd)
        logits = xf @ Wg + bg
        gates = jax.nn.softmax(logits, axis=-1)
        idx = jnp.argmax(gates, axis=-1)
        h = jax.nn.gelu(jnp.einsum('th,ehi->tei', xf, W1) + b1, approximate=False)
        y = jnp.einsum('tei,eih->teh', h, W2) + b2
        out = jnp.take_along_axis(y, idx[:, None, None], axis=1)[:, 0, :]
        return out.reshape(B, S, Hd)

    def _L3_attn_ref(h, u, v, decay_logit, alpha_logit, k_base_gate_logit, k_base_kernel, proj_w, proj_b, norm1_w, norm2_w, mlp_w1, mlp_b1, mlp_w2, mlp_b2):
        import jax, jax.numpy as jnp
        import numpy as np
        GAMMA_MIN, GAMMA_MAX = (0.15, 1.0)
        ALPHA_CAP = 1.0
        EPS_L2 = 1e-08
        EPS_RMS = 1e-06

        def _rmsnorm(x, w):
            return x * jax.lax.rsqrt(jnp.mean(x * x, axis=-1, keepdims=True) + EPS_RMS) * w

        def _l2norm(x):
            n = jnp.linalg.norm(x, axis=-1, keepdims=True)
            return x / jnp.maximum(n, EPS_L2)

        def _causal_conv(h, kernel):
            K = kernel.shape[0]
            S = h.shape[1]
            hp = jnp.pad(h, ((0, 0), (K - 1, 0), (0, 0)))
            out = jnp.zeros_like(h)
            for j in range(K):
                out = out + kernel[j] * hp[:, K - 1 - j:K - 1 - j + S, :]
            return out
        B, S, D = h.shape
        R = u.shape[1]
        residual = h
        h_norm = _rmsnorm(h, norm1_w)
        gate = jax.nn.sigmoid(k_base_gate_logit)
        out = gate * _causal_conv(h_norm, k_base_kernel)
        alpha = ALPHA_CAP * jax.nn.sigmoid(alpha_logit)
        qk = h_norm @ jnp.concatenate((u, v), axis=1)
        q_raw, k_raw = (qk[..., :R], qk[..., R:])
        q = _l2norm(q_raw)
        k = _l2norm(k_raw)
        gamma = jnp.clip(jax.nn.sigmoid(decay_logit), GAMMA_MIN, GAMMA_MAX)
        pos = jnp.arange(S, dtype=h.dtype)
        diff = jnp.maximum(pos[:, None] - pos[None, :], 0.0)
        mask = jnp.tril(jnp.ones((S, S), dtype=h.dtype))
        w = gamma[:, None, None] ** diff * mask
        q_alpha = q * alpha
        A = jnp.einsum('bir,bjr,rij->bij', q_alpha, k, w)
        decay_out = jnp.einsum('bij,bjd->bid', A, h_norm)
        out = out + decay_out
        out = out @ proj_w.T + proj_b
        h2 = residual + out
        hn2 = _rmsnorm(h2, norm2_w)
        mlp_out = jax.nn.gelu(hn2 @ mlp_w1 + mlp_b1) @ mlp_w2 + mlp_b2
        return h2 + mlp_out

    def _L3_ffn_ref(x, wg, W, b):
        import jax, jax.numpy as jnp
        import numpy as np
        H = 128
        E = 8
        B, S = (4, 256)
        Bb, Ss, Hh = x.shape
        Ee = wg.shape[1]
        T = Bb * Ss
        C = T // Ee
        xt = x.reshape(T, Hh)
        logits = xt @ wg
        probs = jax.nn.softmax(logits, axis=-1)
        idx = jnp.argmax(probs, axis=-1)
        mask = jax.nn.one_hot(idx, Ee, dtype=xt.dtype)
        locations = jnp.cumsum(mask, axis=0) - mask
        mask = mask * (locations < C).astype(xt.dtype)
        gate = jnp.sum(probs * mask, axis=-1)
        loc_s = jnp.sum(locations * mask, axis=-1).astype(jnp.int32)
        loc_oh = jax.nn.one_hot(loc_s, C, dtype=xt.dtype)
        dispatch = mask[:, :, None] * loc_oh[:, None, :]
        combine = gate[:, None, None] * dispatch
        exp_in = jnp.einsum('tec,th->ech', dispatch, xt)
        exp_out = jnp.einsum('ech,efh->ecf', exp_in, W) + b[:, None, :]
        out = jnp.einsum('tec,ecf->tf', combine, exp_out)
        return out.reshape(Bb, Ss, Hh)
    x = L0_attn_x
    x = x + _L0_attn_ref(_layernorm(x, axis=-1), L0_attn_ln_g, L0_attn_ln_b, L0_attn_w_qkv, L0_attn_b_qkv, L0_attn_w_rel, L0_attn_w_out, L0_attn_b_out)
    x = x + _L0_ffn_ref(_layernorm(x, axis=-1), L0_ffn_router_w, L0_ffn_W1, L0_ffn_b1, L0_ffn_W2, L0_ffn_b2)
    x = x + _L1_attn_ref(_layernorm(x, axis=-1), L1_attn_W_B, L1_attn_b_B, L1_attn_W_C, L1_attn_b_C, L1_attn_W_dt1, L1_attn_b_dt1, L1_attn_W_dt2, L1_attn_b_dt2, L1_attn_omega_base, L1_attn_D, L1_attn_W_out, L1_attn_b_out)
    x = x + _L1_ffn_ref(_layernorm(x, axis=-1), L1_ffn_gate_w, L1_ffn_w1, L1_ffn_w2, L1_ffn_w3, L1_ffn_ws1, L1_ffn_ws2, L1_ffn_ws3)
    x = x + _L2_attn_ref(_layernorm(x, axis=-1), L2_attn_wq, L2_attn_bq, L2_attn_wk, L2_attn_bk, L2_attn_wv, L2_attn_bv, L2_attn_wo, L2_attn_bo)
    x = x + _L2_ffn_ref(_layernorm(x, axis=-1), L2_ffn_Wg, L2_ffn_bg, L2_ffn_W1, L2_ffn_b1, L2_ffn_W2, L2_ffn_b2)
    x = x + _L3_attn_ref(_layernorm(x, axis=-1), L3_attn_u, L3_attn_v, L3_attn_decay_logit, L3_attn_alpha_logit, L3_attn_k_base_gate_logit, L3_attn_k_base_kernel, L3_attn_proj_w, L3_attn_proj_b, L3_attn_norm1_w, L3_attn_norm2_w, L3_attn_mlp_w1, L3_attn_mlp_b1, L3_attn_mlp_w2, L3_attn_mlp_b2)
    x = x + _L3_ffn_ref(_layernorm(x, axis=-1), L3_ffn_wg, L3_ffn_W, L3_ffn_b)
    return x

_drawn_inputs = setup_inputs


def setup_inputs(seed=0):
    import zlib

    import numpy as np

    out = dict(_drawn_inputs(seed))
    spreads = {'L0_attn_ln_g': (1.0, 0.6),
     'L0_attn_ln_b': (0.0, 0.1),
     'L0_attn_b_qkv': (0.0, 0.1),
     'L0_attn_b_out': (0.0, 0.1),
     'L1_attn_b_dt2': (-4.0, 0.2),
     'L1_attn_D': (1.0, 0.2),
     'L2_attn_bq': (0.0, 0.769),
     'L2_attn_bk': (0.0, 2.0),
     'L2_attn_bv': (0.0, 0.414),
     'L2_attn_bo': (0.0, 0.443),
     'L2_ffn_bg': (0.0, 0.512),
     'L2_ffn_b1': (0.0, 0.8),
     'L2_ffn_b2': (0.0, 0.46),
     'L3_attn_decay_logit': (0.0, 0.8),
     'L3_attn_alpha_logit': (0.0, 0.8),
     'L3_attn_proj_b': (0.0, 0.601),
     'L3_attn_norm1_w': (1.0, 0.6),
     'L3_attn_norm2_w': (1.0, 0.6),
     'L3_attn_mlp_b1': (0.0, 0.8),
     'L3_attn_mlp_b2': (0.0, 0.588)}
    factors = {'L0_attn_w_rel': 8.0,
     'L1_attn_W_dt1': 4.405,
     'L1_attn_b_dt1': 4.53,
     'L1_attn_W_dt2': 2.913,
     'L1_attn_b_out': 4.525,
     'L2_ffn_Wg': 3.429,
     'L2_ffn_W1': 8.0,
     'L2_ffn_W2': 8.0,
     'L3_attn_u': 8.0,
     'L3_attn_v': 8.0,
     'L3_attn_k_base_kernel': 8.0,
     'L3_attn_proj_w': 8.0,
     'L3_attn_mlp_w1': 7.094,
     'L3_attn_mlp_w2': 6.577,
     'L3_ffn_wg': 8.0,
     'L3_ffn_W': 8.0,
     'L3_ffn_b': 44.87}
    for name, (base, spread) in spreads.items():
        noise = np.random.default_rng([zlib.crc32(name.encode()), seed]).standard_normal(out[name].shape)
        drawn = base * np.exp(spread * noise) if base else spread * noise
        out[name] = jnp.asarray(drawn.astype(out[name].dtype))
    for name, factor in factors.items():
        out[name] = (out[name] * factor).astype(out[name].dtype)
    return out
```

```python
import numpy as np
import concourse.bass as bass
from concourse import mybir
from contextlib import ExitStack

FP = mybir.dt.float32
BF = mybir.dt.bfloat16
I32 = mybir.dt.int32
ACT = mybir.ActivationFunctionType
ALU = mybir.AluOpType
AX = mybir.AxisListType

B, S, D = 8, 512, 128
P = 128
NT = B * S // P
TC = S // P
LN_EPS = 1e-5


class Net:

    def __init__(self, nc, ctx):
        self.nc = nc
        sb = lambda n, s, d=FP: ctx.enter_context(nc.sbuf_tensor(n, s, d))
        self.x = sb("x_resid", [P, NT, D])
        self.stat = sb("x_stat", [P, NT, 2])
        self.rstd = sb("x_rstd", [P, NT])
        self.ident = sb("ident", [P, P])
        self.ones = sb("ones_sq", [P, P])
        self.xT = sb("x_normT", [P, B * S])
        self.epst = sb("eps_col", [P, 2])


class Scope:

    used = []

    def __init__(self, nc, ctx, tag):
        self.nc, self.ctx, self.tag = nc, ctx, tag

    def sb(self, name, shape, dt=FP):
        return self.ctx.enter_context(self.nc.sbuf_tensor(f"{self.tag}_{name}", shape, dt))

    def ps(self, name, shape=(P, 512), dt=FP):
        return self.ctx.enter_context(self.nc.psum_tensor(f"{self.tag}_{name}", list(shape), dt))

    def sem(self, name):
        handle = self.nc.alloc_semaphore(name=f"{self.tag}_{name}")
        Scope.used.append(handle)
        return handle


def renew_semaphores(nc):
    nc.clear_and_free_semaphores(Scope.used)
    nc.all_engine_barrier()
    Scope.used = []


def row(v):
    return v.rearrange("(a n) -> a n", a=1)


def col(v):
    return v.rearrange("(n a) -> n a", a=1)


def token_stats(nc, v, net, bst, tile, k):
    nc.vector.bn_stats(bst[:, k, :], net.x[:, tile, :])


def load_and_measure(nc, net, x_dram):
    with ExitStack() as ctx:
        p = Scope(nc, ctx, "in")
        loaded = [p.sem(f"loaded{i}") for i in range(4)]
        zeroed, ready = p.sem("ident_zeroed"), p.sem("ident_ready")
        bst = p.sb("bst", [P, 8, 6])
        block = ctx.enter_context(nc.Block())
        xv = x_dram.rearrange("b (t p) d -> p (b t) d", p=P)

        @block.sync
        def _(sp):
            for q in range(4):
                sp.dma_start(net.x[:, 8 * q:8 * q + 8, :], xv[:, 8 * q:8 * q + 8, :]).then_inc(loaded[q], 16)

        @block.gpsimd
        def _(pool):
            nc.gpsimd.memset(net.ident[:, :], 0.0).then_inc(zeroed, 1)
            nc.gpsimd.memset(net.ones[:, :], 1.0)
            nc.gpsimd.memset(net.epst[:, 0:1], LN_EPS)
            nc.gpsimd.memset(net.epst[:, 1:2], 1e-6)
            pool.wait_ge(zeroed, 1)
            nc.gpsimd.affine_select(out=net.ident[:, :], in_=net.ident[:, :], compare_op=ALU.not_equal, fill=1.0,
                                    base=0, pattern=[[-1, P]], channel_multiplier=1).then_inc(ready, 1)

        @block.vector
        def _(v):
            for q in range(4):
                v.wait_ge(loaded[q], 16)
                for k in range(8):
                    nc.vector.bn_stats(bst[:, k, :], net.x[:, 8 * q + k, :])
                v.drain()
                for k in range(8):
                    nc.vector.bn_aggr(net.stat[:, 8 * q + k, :], bst[:, k, :])
                v.drain()


def normalise(nc, net, tag, src=None, g=None, b=None):
    with ExitStack() as ctx:
        p = Scope(nc, ctx, tag + "_ln")
        xn = [p.sb(f"xn{i}", [P, TC, D]) for i in range(2)]
        gcol, bcol = p.sb("gcol", [P, 1]), p.sb("bcol", [P, 1])
        w_loaded = p.sem("w_loaded")
        std = p.sb("std", [P, NT])
        tps = [p.ps(f"tps{i}") for i in range(2)]
        std_done, xn_done = p.sem("std_done"), p.sem("xn_done")
        t_done, t_free = p.sem("t_done"), p.sem("t_free")
        block = ctx.enter_context(nc.Block())
        src = net.x if src is None else src

        @block.sync
        def _(sp):
            if g is not None:
                sp.dma_start(gcol[:, :], col(g)).then_inc(w_loaded, 16)
                sp.dma_start(bcol[:, :], col(b)).then_inc(w_loaded, 16)

        @block.vector
        def _(v):
            v.wait_ge(std_done, 1)
            nc.vector.reciprocal(net.rstd[:, :], std[:, :])
            v.drain()
            with v.Fori(0, B // 2) as i:
                for par in range(2):
                    c = 2 * i + par
                    v.wait_ge(t_done, c + 1)
                    for k in range(TC):
                        last = nc.vector.tensor_scalar(xn[par][:, k, :], src[:, 4 * c + k, :], net.stat[:, 4 * c + k, 0:1],
                                                       net.rstd[:, bass.ds(4 * c + k, 1)], ALU.subtract, ALU.mult)
                    last.then_inc(xn_done, 1)

        @block.tensor
        def _(pe):
            pe.sem_inc(t_done, 2)
            with pe.Fori(0, B // 2) as i:
                for par in range(2):
                    c = 2 * i + par
                    pe.wait_ge(xn_done, c + 1)
                    pe.wait_ge(t_free, c + 1)
                    for k in range(TC):
                        last = nc.tensor.transpose(tps[par][:, k * P:(k + 1) * P], xn[par][:, k, :], net.ident[:, :])
                    last.then_inc(t_done, 1)

        @block.scalar
        def _(act):
            nc.scalar.activation(std[:, :], net.stat[:, :, 1], ACT.Sqrt, bias=net.epst[:, 0:1]).then_inc(std_done, 1)
            act.sem_inc(t_free, 2)
            if g is not None:
                act.wait_ge(w_loaded, 32)
            with act.Fori(0, B // 2) as i:
                for par in range(2):
                    c = 2 * i + par
                    act.wait_ge(t_done, c + 3)
                    sc = {} if g is None else dict(scale=gcol[:, :], bias=bcol[:, :])
                    nc.scalar.activation(net.xT[:, bass.ts(c, S)], tps[par][:, :],
                                         ACT.Identity, **sc).then_inc(t_free, 1)


def store(nc, net, out):
    with ExitStack() as ctx:
        p = Scope(nc, ctx, "out")
        stored = p.sem("stored")
        block = ctx.enter_context(nc.Block())
        ov = out.rearrange("b (t p) d -> p (b t) d", p=P)

        @block.sync
        def _(sp):
            for q in range(4):
                sp.dma_start(ov[:, 8 * q:8 * q + 8, :], net.x[:, 8 * q:8 * q + 8, :]).then_inc(stored, 16)
            sp.wait_ge(stored, 64)


def one_chunk_ahead(eng, front, back):
    front(0, 0)
    with eng.Fori(0, B // 2 - 1) as i:
        front(2 * i + 1, 1)
        back(2 * i, 0)
        front(2 * i + 2, 0)
        back(2 * i + 1, 1)
    front(B - 1, 1)
    back(B - 2, 0)
    back(B - 1, 1)


def expert_pairs(eng, n):
    if n == 1:
        yield 0, 0
        return
    with eng.Fori(0, n // 2) as j:
        for ep in range(2):
            yield j, ep


def experts(nc, net, tag, n, nf, func, gate, w1, w2, b1=None, w3=None, nb=1):
    glu = w3 is not None
    with ExitStack() as ctx:
        p = Scope(nc, ctx, tag)
        w1t = [p.sb(f"w1_{i}", [P, nf * P]) for i in range(2)]
        w3t = [p.sb(f"w3_{i}", [P, P]) for i in range(2)] if glu else None
        w2t = [p.sb(f"w2_{i}", [P, nf, nb * P]) for i in range(2)]
        b1t = [p.sb(f"b1_{i}", [P, nf]) for i in range(2)]
        h = [p.sb(f"h{i}", [P, nf, S]) for i in range(2)]
        act_h = [p.sb(f"act{i}", [P, S]) for i in range(2)] if glu else None
        nh = 4 if nf == 4 else 2
        hps = [p.ps(f"hps{i}") for i in range(nh)]
        gps = [p.ps(f"gps{i}") for i in range(2)] if glu else None
        yps = [p.ps(f"yps{i}", [P, TC, nb * P]) for i in range(2)]
        loaded = [p.sem(f"loaded{i}") for i in range(2)]
        zeroed = p.sem("zeroed")
        h_done = p.sem("h_done")
        act_done = p.sem("act_done")
        glu_done = p.sem("glu_done")
        y_done = p.sem("y_done")
        y_used = p.sem("y_used")
        n_load = len(w1(0)) + len(w2(0)) + (len(w3(0)) if glu else 0) + (1 if b1 else 0)
        H0, Y0, U0 = nh, 2, 2
        block = ctx.enter_context(nc.Block())

        @block.sync
        def _(sp):
            def load(e, par):
                for dst, src in w1(e):
                    sp.dma_start(dst(w1t[par]), src).then_inc(loaded[par], 16)
                for dst, src in w3(e) if glu else ():
                    sp.dma_start(dst(w3t[par]), src).then_inc(loaded[par], 16)
                for dst, src in w2(e):
                    sp.dma_start(dst(w2t[par]), src).then_inc(loaded[par], 16)
                if b1:
                    sp.dma_start(b1t[par][:, :], b1(e)).then_inc(loaded[par], 16)
            sp.wait_ge(zeroed, 1)
            load(0, 0)
            if n > 1:
                load(1, 1)
            if n > 2:
                with sp.Fori(1, n // 2) as j:
                    for par in range(2):
                        sp.wait_ge(y_done, Y0 + 8 * (2 * j + par) - 8)
                        load(2 * j + par, par)

        @block.gpsimd
        def _(pool):
            for i in range(2):
                last = nc.gpsimd.memset(w2t[i][:, :, :], 0.0)
            last.then_inc(zeroed, 1)

        @block.tensor
        def _(pe):
            pe.sem_inc(y_done, Y0)
            for j, ep in expert_pairs(pe, n):
                    s0 = 8 * (2 * j + ep)
                    pe.wait_ge(loaded[ep], 16 * n_load * (j + 1))

                    def front(c, par):
                        for f in range(nf):
                            bank = f if nf == 4 else par
                            pe.wait_ge(act_done, (s0 + c) * nf + f + 1)
                            if glu:
                                pe.wait_ge(glu_done, s0 + c + 1)
                            last = nc.tensor.matmul(hps[bank][:, :], w1t[ep][:, f * P:(f + 1) * P],
                                                    net.xT[:, bass.ts(c, S)], start=True, stop=True)
                            if glu:
                                last = nc.tensor.matmul(gps[par][:, :], w3t[ep][:, :],
                                                        net.xT[:, bass.ts(c, S)], start=True, stop=True)
                            last.then_inc(h_done, 1)

                    def back(c, par):
                        if glu:
                            pe.wait_ge(glu_done, 2 + s0 + c + 1)
                        else:
                            pe.wait_ge(act_done, H0 + (s0 + c + 1) * nf)
                        pe.wait_ge(y_used, s0 + c + 1)
                        for k in range(TC):
                            for f in range(nf):
                                last = nc.tensor.matmul(yps[par][:, k, :], h[par][:, f, k * P:(k + 1) * P],
                                                        w2t[ep][:, f, :], start=(f == 0), stop=(f == nf - 1))
                        last.then_inc(y_done, 1)

                    one_chunk_ahead(pe, front, back)

        @block.scalar
        def _(act):
            act.sem_inc(act_done, H0)
            for j, ep in expert_pairs(act, n):
                    act.wait_ge(loaded[ep], 16 * n_load * (j + 1))
                    with act.Fori(0, B // 2) as i:
                        for par in range(2):
                            s = 8 * (2 * j + ep) + 2 * i + par
                            act.wait_ge(y_done, s + 1)
                            for f in range(nf):
                                act.wait_ge(h_done, s * nf + f + 1)
                                bank = f if nf == 4 else par
                                o = act_h[par][:, :] if glu else h[par][:, f, :]
                                bias = dict(bias=b1t[ep][:, f:f + 1]) if b1 else {}
                                nc.scalar.activation(o, hps[bank][:, :], func, **bias).then_inc(act_done, 1)

        @block.vector
        def _(v):
            v.sem_inc(y_used, U0)
            if glu:
                v.sem_inc(glu_done, 2)
            for j, ep in expert_pairs(v, n):
                    e = 2 * j + ep

                    def product(c, par):
                        if glu:
                            v.wait_ge(act_done, H0 + 8 * e + c + 1)
                            nc.vector.tensor_tensor(h[par][:, 0, :], act_h[par][:, :], gps[par][:, :],
                                                    ALU.mult).then_inc(glu_done, 1)

                    def gather(c, par):
                        v.wait_ge(y_done, Y0 + 8 * e + c + 1)
                        for q in range(nb):
                            for k in range(TC):
                                xt = net.x[:, 4 * c + k, :]
                                last = nc.vector.scalar_tensor_tensor(
                                    xt, yps[par][:, k, q * P:(q + 1) * P], gate(4 * c + k, e, q), xt,
                                    ALU.mult, ALU.add)
                            if q == nb - 1:
                                last.then_inc(y_used, 1)
                            v.drain()

                    if glu:
                        one_chunk_ahead(v, product, gather)
                    else:
                        with v.Fori(0, B // 2) as i:
                            for par in range(2):
                                gather(2 * i + par, par)


def gated_bias(nc, net, tag, gate, b2):
    with ExitStack() as ctx:
        p = Scope(nc, ctx, tag + "_gb")
        gT = [p.sb(f"gT{i}", [32, P]) for i in range(2)]
        b2d = p.sb("b2d", [32, TC, D])
        tps = [p.ps(f"tps{i}") for i in range(2)]
        bps = [p.ps(f"bps{i}") for i in range(2)]
        loaded, zeroed, t_done, gT_done = p.sem("loaded"), p.sem("zeroed"), p.sem("t_done"), p.sem("gT_done")
        b_done, b_used = p.sem("b_done"), p.sem("b_used")
        block = ctx.enter_context(nc.Block())

        @block.gpsimd
        def _(pool):
            nc.gpsimd.memset(b2d[:, :, :], 0.0).then_inc(zeroed, 1)

        @block.sync
        def _(sp):
            sp.wait_ge(zeroed, 1)
            for k in range(TC):
                sp.dma_start(b2d[8 * k:8 * k + 8, k, :], b2).then_inc(loaded, 16)

        @block.tensor
        def _(pe):
            pe.wait_ge(loaded, 16 * TC)
            for c in range(B):
                if c >= 2:
                    pe.wait_ge(gT_done, c - 1)
                nc.tensor.transpose(tps[c % 2][0:32, 0:P], gate[:, 4 * c:4 * c + 4, :].rearrange("p a b -> p (a b)"),
                                    net.ident[:, :]).then_inc(t_done, 1)
                pe.wait_ge(gT_done, c + 1)
                if c >= 2:
                    pe.wait_ge(b_used, c - 1)
                nc.tensor.matmul(bps[c % 2][:, :], gT[c % 2][:, :], b2d[:, :, :].rearrange("p a b -> p (a b)"),
                                 start=True, stop=True).then_inc(b_done, 1)

        @block.scalar
        def _(act):
            for c in range(B):
                act.wait_ge(t_done, c + 1)
                if c >= 2:
                    act.wait_ge(b_done, c - 1)
                nc.scalar.activation(gT[c % 2][:, :], tps[c % 2][0:32, 0:P], ACT.Copy).then_inc(gT_done, 1)

        @block.vector
        def _(v):
            for c in range(B):
                v.wait_ge(b_done, c + 1)
                xt = net.x[:, 4 * c:4 * c + 4, :].rearrange("p a b -> p (a b)")
                nc.vector.tensor_tensor(xt, xt, bps[c % 2][:, :], ALU.add).then_inc(b_used, 1)


def measure(nc, net, tag):
    with ExitStack() as ctx:
        p = Scope(nc, ctx, tag + "_st")
        bst, agg = p.sb("bst", [P, 8, 6]), p.sb("agg", [P, 8, 2])
        block = ctx.enter_context(nc.Block())

        @block.vector
        def _(v):
            with v.Fori(0, NT // 8) as i:
                for k in range(8):
                    nc.vector.bn_stats(bst[:, k, :], net.x[:, 8 * i + k, :])
                v.drain()
                for k in range(8):
                    nc.vector.bn_aggr(agg[:, k, :], bst[:, k, :])
                v.drain()
                nc.vector.tensor_copy(net.stat[:, bass.ts(i, 8), :], agg[:, :, :])
                v.drain()


def router_logits(nc, net, tag, w, E, lg, bias=None):
    with ExitStack() as ctx:
        p = Scope(nc, ctx, tag + "_rl")
        lT = [p.sb(f"lT{i}", [E, S]) for i in range(2)]
        wt = p.sb("w", [P, E])
        bt = p.sb("b", [E, 1])
        lps = [p.ps(f"lps{i}") for i in range(2)]
        tps = [p.ps(f"tps{i}", [P, TC, E]) for i in range(2)]
        parts = w if isinstance(w, tuple) else (w,)
        n_loaded = 16 * (len(parts) + (bias is not None))
        loaded, l_done, lT_done, t_done, lg_done = (p.sem(n) for n in ("loaded", "l_done", "lT_done", "t_done", "lg_done"))
        block = ctx.enter_context(nc.Block())

        @block.sync
        def _(sp):
            for i, part in enumerate(parts):
                n = E // len(parts)
                sp.dma_start(wt[:, i * n:(i + 1) * n], part).then_inc(loaded, 16)
            if bias is not None:
                sp.dma_start(bt[:, :], col(bias)).then_inc(loaded, 16)

        @block.tensor
        def _(pe):
            pe.wait_ge(loaded, n_loaded)

            def logits(c, par):
                if isinstance(c, int) and c < 2:
                    pass
                else:
                    pe.wait_ge(lT_done, c - 1)
                nc.tensor.matmul(lps[par][0:E, :], wt[:, :], net.xT[:, bass.ts(c, S)],
                                 start=True, stop=True).then_inc(l_done, 1)

            def turn(c, par):
                pe.wait_ge(lT_done, c + 1)
                if not (isinstance(c, int) and c < 2):
                    pe.wait_ge(lg_done, c - 1)
                for k in range(TC):
                    last = nc.tensor.transpose(tps[par][:, k, :], lT[par][:, k * P:(k + 1) * P], net.ident[0:E, 0:E])
                last.then_inc(t_done, 1)

            for c in range(2):
                logits(c, c)
            for c in range(B):
                turn(c, c % 2)
                if c + 2 < B:
                    logits(c + 2, c % 2)

        @block.scalar
        def _(act):
            act.wait_ge(loaded, n_loaded)
            for c in range(B):
                act.wait_ge(l_done, c + 1)
                if c >= 2:
                    act.wait_ge(t_done, c - 1)
                kw = {} if bias is None else dict(bias=bt[:, :])
                nc.scalar.activation(lT[c % 2][:, :], lps[c % 2][0:E, :], ACT.Identity, **kw).then_inc(lT_done, 1)

        @block.vector
        def _(v):
            for c in range(B):
                v.wait_ge(t_done, c + 1)
                nc.vector.tensor_copy(lg[:, 4 * c:4 * c + 4, :], tps[c % 2][:, :, :]).then_inc(lg_done, 1)


def bcast(ap, n):
    return ap.unsqueeze(len(ap.shape)).to_broadcast(list(ap.shape) + [n])


def first_best(nc, v, lg, m, eq, idx, onehot, iota, E):
    nc.vector.tensor_reduce(m[:, :], lg[:, :, :], AX.X, ALU.max)
    v.drain()
    nc.vector.tensor_tensor(eq[:, :, :], lg[:, :, :], bcast(m[:, :], E), ALU.is_equal)
    v.drain()
    nc.vector.scalar_tensor_tensor(eq[:, :, :], eq[:, :, :], float(-E), iota[:, :, :], ALU.mult, ALU.add)
    v.drain()
    nc.vector.tensor_reduce(idx[:, :], eq[:, :, :], AX.X, ALU.min)
    v.drain()
    nc.vector.tensor_tensor(onehot[:, :, :], eq[:, :, :], bcast(idx[:, :], E), ALU.is_equal)
    v.drain()


class Router:

    def __init__(self, nc, ctx, tag, E):
        p = Scope(nc, ctx, tag)
        self.E = E
        self.lg, self.eq, self.oh = p.sb("lg", [P, NT, E]), p.sb("eq", [P, NT, E]), p.sb("onehot", [P, NT, E])
        self.gate, self.iota = p.sb("gate", [P, NT, E]), p.sb("iota", [P, NT, E])
        self.m, self.idx, self.prob = p.sb("m", [P, NT]), p.sb("idx", [P, NT]), p.sb("prob", [P, NT])


def top1_prob(nc, r, tag):
    with ExitStack() as ctx:
        p = Scope(nc, ctx, tag + "_t1")
        iota_done, shifted, exped = p.sem("iota_done"), p.sem("shifted"), p.sem("exped")
        sh = p.sb("sh", [P, NT, r.E])
        block = ctx.enter_context(nc.Block())

        @block.gpsimd
        def _(pool):
            nc.gpsimd.iota(r.iota[:, :, :], pattern=[[0, NT], [1, r.E]], base=0, channel_multiplier=0,
                           allow_small_or_imprecise_dtypes=True).then_inc(iota_done, 1)

        @block.scalar
        def _(act):
            act.wait_ge(shifted, 1)
            nc.scalar.activation(sh[:, :, :], sh[:, :, :], ACT.Exp).then_inc(exped, 1)

        @block.vector
        def _(v):
            v.wait_ge(iota_done, 1)
            first_best(nc, v, r.lg, r.m, r.eq, r.idx, r.oh, r.iota, r.E)
            nc.vector.tensor_tensor(sh[:, :, :], r.lg[:, :, :], bcast(r.m[:, :], r.E), ALU.subtract).then_inc(shifted, 1)
            v.wait_ge(exped, 1)
            nc.vector.tensor_reduce(r.idx[:, :], sh[:, :, :], AX.X, ALU.add)
            v.drain()
            nc.vector.reciprocal(r.prob[:, :], r.idx[:, :])


def over_tiles(v, n):
    return v.unsqueeze(1).to_broadcast([v.shape[0], n, v.shape[1]])


def prefix_steps(nc, p, E):
    tri = p.sb("tri", [P, P])
    tot, scan, one = p.sb("tot", [P, NT, E]), p.sb("scan", [P, NT, E]), p.sb("one", [P, NT])
    wps, tps = p.ps("wps", [P, NT, E]), p.ps("tps", [P, NT, E])
    tri_zeroed, tri_ready = p.sem("tri_zeroed"), p.sem("tri_ready")
    mask_ready, counted = p.sem("mask_ready"), p.sem("counted")

    def on_pool(pool):
        nc.gpsimd.memset(tri[:, :], 1.0)
        nc.gpsimd.memset(one[:, :], 1.0).then_inc(tri_zeroed, 1)
        pool.wait_ge(tri_zeroed, 1)
        nc.gpsimd.affine_select(out=tri[:, :], in_=tri[:, :], compare_op=ALU.is_ge, fill=0.0,
                                base=-1, pattern=[[1, P]], channel_multiplier=-1).then_inc(tri_ready, 1)

    def on_tensor(pe, net, mask):
        pe.wait_ge(tri_ready, 1)
        pe.wait_ge(mask_ready, 1)
        flat = mask.rearrange("p t e -> p (t e)")
        nc.tensor.matmul(wps[:, :, :].rearrange("p t e -> p (t e)"), tri[:, :], flat, start=True, stop=True)
        nc.tensor.matmul(tps[:, :, :].rearrange("p t e -> p (t e)"), net.ones[:, :], flat,
                         start=True, stop=True).then_inc(counted, 1)

    def on_vector(v, loc):
        v.drain()
        v.sem_inc(mask_ready, 1)
        v.wait_ge(tri_ready, 1)
        v.wait_ge(counted, 1)
        nc.vector.tensor_copy(tot[:, :, :], tps[:, :, :])
        v.drain()
        for e in range(E):
            nc.vector.tensor_tensor_scan(scan[:, :, e], one[:, :], tot[:, :, e], 0.0, ALU.mult, ALU.add)
        v.drain()
        nc.vector.tensor_tensor(scan[:, :, :], scan[:, :, :], tot[:, :, :], ALU.subtract)
        v.drain()
        nc.vector.tensor_tensor(loc, scan[:, :, :], wps[:, :, :], ALU.add)
        v.drain()

    return on_pool, on_tensor, on_vector


def capacity_by_probability(nc, net, r, cap, tag):
    E = r.E
    steps = 28
    with ExitStack() as ctx:
        p = Scope(nc, ctx, tag + "_cap")
        key, cmp = p.sb("key", [P, NT, E]), p.sb("cmp", [P, NT, E])
        gt, loc = p.sb("gt", [P, NT, E]), p.sb("loc", [P, NT, E])
        t, cand, part, take = (p.sb(n, [P, E]) for n in ("t", "cand", "part", "take"))
        step, drop = p.sb("step", [P, 1]), p.sb("drop", [P, NT])
        cps = p.ps("cps", [P, E])
        part_done, total_done = p.sem("part_done"), p.sem("total_done")
        on_pool, on_tensor, on_vector = prefix_steps(nc, p, E)
        block = ctx.enter_context(nc.Block())

        @block.gpsimd
        def _(pool):
            on_pool(pool)

        @block.tensor
        def _(pe):
            with pe.Fori(0, steps + 1) as i:
                pe.wait_ge(part_done, i + 1)
                nc.tensor.matmul(cps[:, :], net.ones[:, :], part[:, :], start=True, stop=True).then_inc(total_done, 1)
            on_tensor(pe, net, r.eq[:, :, :])

        @block.vector
        def _(v):
            def count(op, thr):
                nc.vector.tensor_tensor(cmp[:, :, :], key[:, :, :], over_tiles(thr, NT), op)
                v.drain()
                nc.vector.tensor_reduce(part[:, :], cmp[:, :, :].rearrange("p t e -> p e t"),
                                        AX.X, ALU.add).then_inc(part_done, 1)

            nc.vector.memset(t[:, :], 0.0)
            nc.vector.memset(step[:, :], 1.0)
            nc.vector.tensor_tensor(key[:, :, :], r.oh[:, :, :], bcast(r.prob[:, :], E), ALU.mult)
            v.drain()
            with v.Fori(0, steps) as i:
                nc.vector.tensor_scalar(cand[:, :], t[:, :], step[:, :], None, ALU.add)
                v.drain()
                count(ALU.is_ge, cand[:, :])
                v.wait_ge(total_done, i + 1)
                nc.vector.tensor_scalar(take[:, :], cps[:, :], float(cap), None, ALU.is_ge)
                v.drain()
                nc.vector.tensor_tensor(cand[:, :], cand[:, :], t[:, :], ALU.subtract)
                nc.vector.tensor_scalar(step[:, :], step[:, :], 0.5, None, ALU.mult)
                v.drain()
                nc.vector.tensor_tensor(take[:, :], take[:, :], cand[:, :], ALU.mult)
                v.drain()
                nc.vector.tensor_tensor(t[:, :], t[:, :], take[:, :], ALU.add)
                v.drain()
            count(ALU.is_gt, t[:, :])
            v.wait_ge(total_done, steps + 1)
            nc.vector.tensor_copy(gt[:, :, :], cmp[:, :, :])
            nc.vector.tensor_tensor(r.eq[:, :, :], key[:, :, :], over_tiles(t[:, :], NT), ALU.is_equal)
            nc.vector.tensor_scalar(take[:, :], cps[:, :], -1.0, float(cap), ALU.mult, ALU.add)
            on_vector(v, loc[:, :, :])
            nc.vector.tensor_tensor(cmp[:, :, :], loc[:, :, :], over_tiles(take[:, :], NT), ALU.is_lt)
            v.drain()
            nc.vector.tensor_tensor(cmp[:, :, :], cmp[:, :, :], r.eq[:, :, :], ALU.mult)
            v.drain()
            nc.vector.tensor_tensor(cmp[:, :, :], cmp[:, :, :], gt[:, :, :], ALU.add)
            v.drain()
            nc.vector.tensor_tensor(r.gate[:, :, :], cmp[:, :, :], r.oh[:, :, :], ALU.mult)
            v.drain()
            nc.vector.tensor_reduce(drop[:, :], r.gate[:, :, :], AX.X, ALU.add)
            v.drain()
            nc.vector.tensor_scalar(drop[:, :], drop[:, :], -1.0, 1.0, ALU.mult, ALU.add)
            v.drain()
            nc.vector.tensor_tensor(r.gate[:, :, 0], r.gate[:, :, 0], drop[:, :], ALU.add)


def capacity_by_order(nc, net, r, cap, tag):
    E = r.E
    with ExitStack() as ctx:
        p = Scope(nc, ctx, tag + "_cap")
        loc = p.sb("loc", [P, NT, E])
        on_pool, on_tensor, on_vector = prefix_steps(nc, p, E)
        block = ctx.enter_context(nc.Block())

        @block.gpsimd
        def _(pool):
            on_pool(pool)

        @block.tensor
        def _(pe):
            on_tensor(pe, net, r.oh[:, :, :])

        @block.vector
        def _(v):
            on_vector(v, loc[:, :, :])
            nc.vector.tensor_scalar(loc[:, :, :], loc[:, :, :], float(cap), None, ALU.is_lt)
            v.drain()
            nc.vector.tensor_tensor(loc[:, :, :], loc[:, :, :], r.oh[:, :, :], ALU.mult)
            v.drain()
            nc.vector.tensor_tensor(r.gate[:, :, :], loc[:, :, :], bcast(r.prob[:, :], E), ALU.mult)


def split3(nc, eng, e, src, dst, rest, drain):
    e.tensor_copy(dst[0], src)
    drain()
    e.tensor_tensor(rest, src, dst[0], ALU.subtract)
    drain()
    e.tensor_copy(dst[1], rest)
    drain()
    e.tensor_tensor(rest, rest, dst[1], ALU.subtract)
    drain()
    return e.tensor_copy(dst[2], rest)


def relative_attention(nc, net, d):
    a = lambda n: d[f"L0_attn_{n}"]
    HD, NH = a("w_rel").shape
    qd, kd = (nc.dram_tensor(n, (3, P, B * S), BF, kind="Internal").ap() for n in ("q_parts", "k_parts"))
    ad = nc.dram_tensor("rel_q_parts", (3, P, S), BF, kind="Internal").ap()
    td = nc.dram_tensor("rel_k_parts", (3, HD, S), BF, kind="Internal").ap()
    with ExitStack() as ctx:
        h = Scope(nc, ctx, "a0h").sb("h", [P, NT, D])
        token_rstd(nc, net, "a0")
        layernorm_tokens(nc, net, h)
        normalise(nc, net, "a0", src=h, g=a("ln_g"), b=a("ln_b"))
    with ExitStack() as ctx:
        V = Scope(nc, ctx, "a0v").sb("V", [P, NT, NH, HD + 1])
        project_parts(nc, net, a, HD, NH, V, qd, kd)
        relative_parts(nc, d, a, HD, NH, ad, td)
        heads(nc, net, a, HD, NH, V, qd, kd, ad, td)
    measure(nc, net, "a0")


def layernorm_tokens(nc, net, h):
    with ExitStack() as ctx:
        p = Scope(nc, ctx, "a0n")
        bst = p.sb("bst", [P, NT, 6])
        block = ctx.enter_context(nc.Block())

        @block.vector
        def _(v):
            for t in range(NT):
                nc.vector.tensor_scalar(h[:, t, :], net.x[:, t, :], net.stat[:, t, 0:1], net.rstd[:, t:t + 1],
                                        ALU.subtract, ALU.mult)
            v.drain()
            for t in range(NT):
                nc.vector.bn_stats(bst[:, t, :], h[:, t, :])
            v.drain()
            for t in range(NT):
                nc.vector.bn_aggr(net.stat[:, t, :], bst[:, t, :])


def project_parts(nc, net, a, HD, NH, V, qd, kd):
    with ExitStack() as ctx:
        p = Scope(nc, ctx, "a0p")
        w, bv = p.sb("w", [P, 3, P]), p.sb("bv", [P, P])
        bias, tick = p.sb("bias", [P, 2]), p.sb("tick", [P, 2])
        f = [[p.sb(f"f{t}{i}", [P, S]) for i in range(2)] for t in "qk"]
        parts = [[p.sb(f"parts{t}{i}", [P, 3, S], BF) for i in range(2)] for t in "qk"]
        rest = [p.sb(f"rest{t}", [P, S]) for t in "qk"]
        xc = [p.sb(f"xc{i}", [P, S]) for i in range(2)]
        qkps = [[p.ps(f"ps{t}{i}") for i in range(2)] for t in "qk"]
        vps = [p.ps(f"vps{i}") for i in range(2)]
        loaded, k_split, xc_done, pj_ready, f_done, v_done = (
            p.sem(n) for n in ("loaded", "k_split", "xc_done", "pj_ready", "f_done", "v_done"))
        split_done = [p.sem(f"split_{t}") for t in "qk"]
        stored = [[p.sem(f"stored_{t}{i}") for i in range(2)] for t in "qk"]
        block = ctx.enter_context(nc.Block())
        scale = HD ** -0.5

        @block.sync
        def _(sp):
            sp.dma_start(w[:, :, :], a("w_qkv")).then_inc(loaded, 16)
            for t in range(2):
                sp.dma_start(bias[:, t:t + 1], col(a("b_qkv")[t, :])).then_inc(loaded, 16)
            sp.dma_start(bv[:, :], row(a("b_qkv")[2, :]).to_broadcast([P, P])).then_inc(loaded, 16)
            for t in range(2):
                for par in range(2):
                    sp.sem_inc(stored[t][par], 16)
            with sp.Fori(0, B // 2) as i:
                for par in range(2):
                    c = 2 * i + par
                    for t, dst in enumerate((qd, kd)):
                        sp.wait_ge(split_done[t], c + 1)
                        sp.dma_start(dst[:, :, bass.ts(c, S)].rearrange("s p n -> p s n"),
                                     parts[t][par][:, :, :]).then_inc(stored[t][par], 16)
            for t in range(2):
                for par in range(2):
                    sp.wait_ge(stored[t][par], 16 + 16 * (B // 2))

        @block.tensor
        def _(pe):
            pe.wait_ge(loaded, 64)
            pe.sem_inc(pj_ready, 2)
            with pe.Fori(0, B // 2) as i:
                for par in range(2):
                    c = 2 * i + par
                    pe.wait_ge(f_done, c + 1)
                    for t in range(2):
                        nc.tensor.matmul(qkps[t][par][:, :], w[:, t, :], net.xT[:, bass.ts(c, S)], start=True, stop=True)
                    pe.wait_ge(xc_done, c + 1)
                    pe.wait_ge(v_done, c + 1)
                    for k in range(TC):
                        last = nc.tensor.matmul(vps[par][:, k * P:(k + 1) * P], xc[par][:, k * P:(k + 1) * P], w[:, 2, :],
                                                start=True, stop=True)
                    last.then_inc(pj_ready, 1)

        @block.scalar
        def _(act):
            act.wait_ge(loaded, 64)
            nc.scalar.activation(bias[:, 0:1], bias[:, 0:1], ACT.Copy, scale=scale)
            act.drain()
            act.sem_inc(f_done, 2)
            with act.Fori(0, B // 2) as i:
                for par in range(2):
                    c = 2 * i + par
                    act.wait_ge(pj_ready, c + 1)
                    nc.scalar.activation(xc[par][:, :], net.xT[:, bass.ts(c, S)], ACT.Copy).then_inc(xc_done, 1)
                    act.wait_ge(pj_ready, c + 3)
                    act.wait_ge(v_done, c + 1)
                    act.wait_ge(k_split, c + 1)
                    nc.scalar.activation(f[0][par][:, :], qkps[0][par][:, :], ACT.Identity, bias=bias[:, 0:1], scale=scale)
                    nc.scalar.activation(f[1][par][:, :], qkps[1][par][:, :], ACT.Identity, bias=bias[:, 1:2]).then_inc(f_done, 1)

        @block.vector
        def _(v):
            nc.vector.memset(V[:, :, :, HD:HD + 1], 1.0)
            v.wait_ge(loaded, 64)
            v.sem_inc(v_done, 2)
            with v.Fori(0, B // 2) as i:
                for par in range(2):
                    c = 2 * i + par
                    v.wait_ge(f_done, c + 3)
                    v.wait_ge(stored[0][par], 16 * i + 16)
                    split3(nc, v, nc.vector, f[0][par][:, :], [parts[0][par][:, s, :] for s in range(3)],
                           rest[0][:, :], v.drain).then_inc(split_done[0], 1)
                    for k in range(TC):
                        last = nc.vector.tensor_tensor(V[:, 4 * c + k, :, 0:HD],
                                                       vps[par][:, k * P:(k + 1) * P].rearrange("p (h d) -> p h d", d=HD),
                                                       bv[:, :].rearrange("p (h d) -> p h d", d=HD), ALU.add)
                    last.then_inc(v_done, 1)

        @block.gpsimd
        def _(pool):
            pool.sem_inc(k_split, 2)
            nc.gpsimd.memset(tick[:, :], 1.0)
            pool.drain()
            with pool.Fori(0, B // 2) as i:
                for par in range(2):
                    c = 2 * i + par
                    pool.wait_ge(f_done, c + 3)
                    pool.wait_ge(stored[1][par], 16 * i + 16)
                    nc.gpsimd.tensor_tensor(tick[:, 1:2], tick[:, 0:1], tick[:, 0:1], ALU.mult)
                    split3(nc, pool, nc.gpsimd, f[1][par][:, :], [parts[1][par][:, s, :] for s in range(3)],
                           rest[1][:, :], pool.drain).then_inc(split_done[1], 1)
                    pool.drain()
                    pool.sem_inc(k_split, 1)


def relative_parts(nc, d, a, HD, NH, ad, td):
    with ExitStack() as ctx:
        p = Scope(nc, ctx, "a0r")
        t, m1, m2 = p.sb("t", [HD, S]), p.sb("m1", [HD, HD]), p.sb("m2", [HD, HD])
        wr, ws = p.sb("wr", [HD, NH]), p.sb("ws", [HD, NH])
        L, L2 = p.sb("L", [HD, HD, NH]), p.sb("L2", [HD, HD, NH])
        qf, qp, kp = p.sb("qf", [P, S]), p.sb("qp", [P, 3, S], BF), p.sb("kp", [HD, 3, S], BF)
        rest = p.sb("rest", [P, S])
        ps = p.ps("ps")
        loaded, L_done, q_done, split_done, stored = (p.sem(n) for n in ("loaded", "L_done", "q_done", "split_done", "stored"))
        block = ctx.enter_context(nc.Block())

        @block.sync
        def _(sp):
            for dst, src in ((t, d["rel_t"]), (m1, d["rel_m1"]), (m2, d["rel_m2"]), (wr, a("w_rel"))):
                sp.dma_start(dst[:, :], src).then_inc(loaded, 16)
            for r in range(HD):
                sp.dma_start(ws[r:r + 1, :], a("w_rel")[r ^ 1:(r ^ 1) + 1, :]).then_inc(loaded, 16)
            sp.wait_ge(split_done, 1)
            sp.dma_start(td.rearrange("s r n -> r s n"), kp[:, :, :]).then_inc(stored, 16)
            sp.wait_ge(split_done, 2)
            sp.dma_start(ad.rearrange("s p n -> p s n"), qp[:, :, :]).then_inc(stored, 16)
            sp.wait_ge(stored, 32)

        @block.tensor
        def _(pe):
            pe.wait_ge(L_done, 1)
            nc.tensor.matmul(ps[:, :], L[:, :, :].rearrange("a r h -> a (r h)"), t[:, :], start=True, stop=True).then_inc(q_done, 1)

        @block.vector
        def _(v):
            v.wait_ge(loaded, 16 * (4 + HD))
            nc.vector.tensor_tensor(L[:, :, :], over_tiles(wr[:, :], HD), bcast(m1[:, :], NH), ALU.mult)
            nc.vector.tensor_tensor(L2[:, :, :], over_tiles(ws[:, :], HD), bcast(m2[:, :], NH), ALU.mult)
            v.drain()
            nc.vector.tensor_tensor(L[:, :, :], L[:, :, :], L2[:, :, :], ALU.add).then_inc(L_done, 1)
            split3(nc, v, nc.vector, t[:, :], [kp[:, s, :] for s in range(3)], rest[0:HD, :], v.drain).then_inc(split_done, 1)
            v.wait_ge(q_done, 1)
            nc.vector.tensor_copy(qf[:, :], ps[:, :])
            v.drain()
            split3(nc, v, nc.vector, qf[:, :], [qp[:, s, :] for s in range(3)], rest[:, :], v.drain).then_inc(split_done, 1)


def heads(nc, net, a, HD, NH, V, qd, kd, ad, td):
    GH = 4
    NG = NH // GH
    QP, KP = (0, 0, 0, 1, 1, 2), (0, 1, 2, 0, 1, 0)
    DYN, REL, MAX = 0, len(QP) * HD, 2 * len(QP) * HD
    KB = MAX + 3
    SLOTS = 4 * GH + 1
    N_DMA = len(QP) + 3
    LQ = 16 * N_DMA
    with ExitStack() as ctx:
        p = Scope(nc, ctx, "a0")
        Q, K = p.sb("Q", [P, 2 * NH, S], BF), p.sb("K", [P, 2 * NH, S], BF)
        prob = [p.sb(f"prob{i}", [P, GH, TC, S]) for i in range(2)]
        Vg = [p.sb(f"Vg{i}", [P, TC, GH, 32]) for i in range(2)]
        OT = [p.sb(f"OT{i}", [P, S]) for i in range(2)]
        nm = [p.sb(f"nm{i}", [P, 4 * GH]) for i in range(2)]
        mr, ms = p.sb("mr", [4 * GH, P]), [p.sb(f"ms{i}", [4 * GH, 3, P], BF) for i in range(2)]
        mrest = p.sb("mrest", [4 * GH, P])
        den, O, OTn = p.sb("den", [P, TC, GH]), p.sb("O", [P, TC, NH * HD]), p.sb("OTn", [P, S])
        wo, bo, tick = p.sb("wo", [P, D]), p.sb("bo", [P, D]), p.sb("tick", [P, 2])
        aps = [p.ps(f"aps{i}") for i in range(2)]
        sps = [p.ps(f"sps{i}", [P, 2, S]) for i in range(2)]
        ops, mps = p.ps("ops"), p.ps("mps")
        statics, bias_added, zeroed = p.sem("statics"), p.sem("bias_added"), p.sem("zeroed")
        qk_loaded = [p.sem(f"qk_loaded{i}") for i in range(2)]
        max_loaded = [p.sem(f"max_loaded{i}") for i in range(2)]
        a_ready, a_used, ms_done = p.sem("a_ready"), p.sem("a_used"), p.sem("ms_done")
        s_ready, p_done, vg_ready, av_done = p.sem("s_ready"), p.sem("p_done"), p.sem("vg_ready"), p.sem("av_done")
        ot_copied, ott_done, o_done = p.sem("ot_copied"), p.sem("ott_done"), p.sem("o_done")
        on_turned, otn_done, y_done, y_added = p.sem("on_turned"), p.sem("otn_done"), p.sem("y_done"), p.sem("y_added")
        block = ctx.enter_context(nc.Block())
        AV0 = 2 * NG
        N_STATIC = 16 * (2 * (len(QP) + 3) + 2)

        def units(eng, maxima, both, probs, post):
            def groups(f):
                with eng.Fori(0, NG // 2) as g2:
                    for gp in range(2):
                        f(2 * g2 + gp, g2, gp)
            if maxima is not None:
                groups(lambda g, g2, gp: maxima(0, g, g2, gp))
            with eng.Fori(0, B - 1) as b:
                groups(lambda g, g2, gp: both(b, g, g2, gp))
                post(b)
            groups(lambda g, g2, gp: probs(B - 1, g, g2, gp))
            post(B - 1)

        hs = lambda b, g: bass.ds((b % 2) * NH + GH * g, GH)
        head = lambda b, g, j: bass.ds((b % 2) * NH + GH * g + j, 1)

        @block.sync
        def _(sp):
            sp.wait_ge(zeroed, 1)
            for par in range(2):
                hh = slice(par * NH, (par + 1) * NH)
                for n, s in enumerate(QP):
                    sp.dma_start(Q[REL + n * HD:REL + (n + 1) * HD, hh, :],
                                 ad[s, :, :].rearrange("(r h) n -> r h n", h=NH)).then_inc(statics, 16)
                for first, s in ((0, 3), (3, 2), (5, 1)):
                    src = td[0:s, :, :].rearrange("s r n -> (s r) n")
                    sp.dma_start(K[REL + first * HD:REL + (first + s) * HD, hh, :],
                                 over_tiles(src, NH)).then_inc(statics, 16)
            sp.dma_start(wo[:, :], a("w_out")).then_inc(statics, 16)
            sp.dma_start(bo[:, :], row(a("b_out")).to_broadcast([P, D])).then_inc(statics, 16)

            qv = qd.rearrange("s (r h) n -> s r h n", h=NH)
            kv = kd.rearrange("s (r h) n -> s r h n", h=NH)

            def load(b, g, gp):
                for n, s in enumerate(QP):
                    sp.dma_start(Q[DYN + n * HD:DYN + (n + 1) * HD, hs(b, g), :],
                                 qv[s, :, bass.ts(g, GH), bass.ts(b, S)]).then_inc(qk_loaded[gp], 16)
                for first, s in ((0, 3), (3, 2), (5, 1)):
                    sp.dma_start(K[DYN + first * HD:DYN + (first + s) * HD, hs(b, g), :],
                                 kv[0:s, :, bass.ts(g, GH), bass.ts(b, S)].rearrange("s r h n -> (s r) h n"))\
                      .then_inc(qk_loaded[gp], 16)

            def store_max(b, g, g2, gp):
                sp.wait_ge(ms_done, NG * b + g + 1)
                sp.wait_ge(av_done, NG * b + g + 1)
                for s in range(3):
                    sp.dma_start(Q[MAX + s:MAX + s + 1, hs(b, g), :].rearrange("o h (q t) -> o (h q) t", t=P),
                                 ms[gp][:, s, :]).then_inc(max_loaded[gp], 16)

            for i in range(2):
                sp.sem_inc(max_loaded[i], 48)
            load(0, 0, 0)
            load(0, 1, 1)
            for b, g in ((0, 2), (0, 3), (1, 0), (1, 1), (1, 2), (1, 3)):
                sp.wait_ge(qk_loaded[g % 2], LQ * (2 * b + g // 2))
                load(b, g, g % 2)
            with sp.Fori(0, NG // 2) as g2:
                for gp in range(2):
                    store_max(0, 2 * g2 + gp, g2, gp)
            with sp.Fori(0, B - 2) as b:
                with sp.Fori(0, NG // 2) as g2:
                    for gp in range(2):
                        g = 2 * g2 + gp
                        store_max(b + 1, g, g2, gp)
                        sp.wait_ge(av_done, AV0 + NG * b + g + 1)
                        sp.wait_ge(qk_loaded[gp], LQ * (2 * (b + 2) + g2))
                        load(b + 2, g, gp)
            with sp.Fori(0, NG // 2) as g2:
                for gp in range(2):
                    store_max(B - 1, 2 * g2 + gp, g2, gp)

        @block.gpsimd
        def _(pool):
            nc.gpsimd.memset(K[:, :, :], 1.0).then_inc(zeroed, 1)
            nc.gpsimd.memset(tick[:, :], 1.0)
            for i in range(2):
                nc.gpsimd.memset(Vg[i][:, :, :, :], 0.0)
            pool.drain()
            pool.wait_ge(statics, N_STATIC)
            nc.gpsimd.tensor_tensor(net.x[:, :, :], net.x[:, :, :], over_tiles(bo[:, :], NT), ALU.add).then_inc(bias_added, 1)
            with pool.Fori(0, B) as b:
                with pool.Fori(0, NG // 2) as g2:
                    for gp in range(2):
                        g = 2 * g2 + gp
                        pool.drain()
                        pool.wait_ge(av_done, NG * b + g + AV0 - 1)
                        nc.gpsimd.tensor_tensor(tick[:, 1:2], tick[:, 0:1], tick[:, 0:1], ALU.mult)
                        for k in range(TC):
                            last = nc.gpsimd.tensor_copy(Vg[gp][:, k, :, 0:HD + 1], V[:, 4 * b + k, bass.ts(g, GH), :])
                        last.then_inc(vg_ready, 1)

        @block.tensor
        def _(pe):
            pe.wait_ge(statics, N_STATIC)
            pe.sem_inc(av_done, AV0)
            pe.sem_inc(ott_done, 2)
            pe.sem_inc(on_turned, 1)
            pe.sem_inc(y_done, 1)

            def max_scores(b, g, j):
                U = SLOTS * (NG * b + g)
                for q in range(TC):
                    s = 4 * j + q
                    pe.wait_ge(a_used, U + max(s + 1, 2))
                    nc.tensor.matmul(aps[s % 2][:, :],
                                     Q[0:MAX, head(b, g, j), q * P:(q + 1) * P].rearrange("k a n -> k (a n)"),
                                     K[0:MAX, head(b, g, j), :].rearrange("k a n -> k (a n)"),
                                     start=True, stop=True).then_inc(a_ready, 1)

            def turn_maxima(b, g, gp):
                U = SLOTS * (NG * b + g)
                pe.wait_ge(a_used, U + SLOTS + 1)
                nc.tensor.transpose(aps[0][0:4 * GH, 0:P], nm[gp][:, :], net.ident[:, :]).then_inc(a_ready, 1)

            def key_scores(b, g, j):
                for half in range(2):
                    pe.wait_ge(p_done, 8 * (NG * b + g) + 2 * j + half + 1)
                    for t in range(2):
                        k = 2 * half + t
                        last = nc.tensor.matmul(sps[half][:, t, :],
                                                K[0:KB, head(b, g, j), k * P:(k + 1) * P].rearrange("k a n -> k (a n)"),
                                                Q[0:KB, head(b, g, j), :].rearrange("k a n -> k (a n)"),
                                                start=True, stop=True)
                    last.then_inc(s_ready, 1)

            def values(b, g, gp):
                u = NG * b + g
                pe.wait_ge(p_done, 2 + 8 * (u + 1))
                pe.wait_ge(vg_ready, u + 1)
                pe.wait_ge(ot_copied, u + 1)
                for k in range(TC):
                    for j in range(GH):
                        last = nc.tensor.matmul(ops[32 * j:32 * j + 32, :], Vg[gp][:, k, j, :], prob[gp][:, j, k, :],
                                                start=(k == 0), stop=(k == TC - 1))
                last.then_inc(av_done, 1)

            def turn_outputs(b, g, gp):
                u = NG * b + g
                pe.wait_ge(ot_copied, u + 2)
                pe.wait_ge(o_done, u + 1)
                pe.wait_ge(y_added, b + 1)
                for q in range(TC):
                    last = nc.tensor.transpose(mps[:, q * P:(q + 1) * P], OT[gp][:, q * P:(q + 1) * P], net.ident[:, :])
                last.then_inc(ott_done, 1)

            def maxima(b, g, g2, gp):
                pe.wait_ge(qk_loaded[gp], LQ * (2 * b + g2 + 1))
                for j in range(GH):
                    max_scores(b, g, j)
                turn_maxima(b, g, gp)

            def both(b, g, g2, gp):
                pe.wait_ge(max_loaded[gp], 48 * (2 * b + g2 + 2))
                pe.wait_ge(qk_loaded[gp], LQ * (2 * (b + 1) + g2 + 1))
                key_scores(b, g, 0)
                max_scores(b + 1, g, 0)
                key_scores(b, g, 1)
                key_scores(b, g, 2)
                max_scores(b + 1, g, 1)
                key_scores(b, g, 3)
                max_scores(b + 1, g, 2)
                values(b, g, gp)
                max_scores(b + 1, g, 3)
                turn_outputs(b, g, gp)
                turn_maxima(b + 1, g, gp)

            def probs(b, g, g2, gp):
                pe.wait_ge(max_loaded[gp], 48 * (2 * b + g2 + 2))
                for j in range(GH):
                    key_scores(b, g, j)
                values(b, g, gp)
                turn_outputs(b, g, gp)

            def post(b):
                pe.wait_ge(o_done, NG * b + NG + 1)
                for q in range(TC):
                    last = nc.tensor.transpose(mps[:, q * P:(q + 1) * P], O[:, q, :], net.ident[:, :])
                last.then_inc(on_turned, 1)
                pe.wait_ge(otn_done, b + 1)
                for q in range(TC):
                    last = nc.tensor.matmul(mps[:, q * P:(q + 1) * P], OTn[:, q * P:(q + 1) * P], wo[:, :],
                                            start=True, stop=True)
                last.then_inc(y_done, 1)

            units(pe, maxima, both, probs, post)

        @block.scalar
        def _(act):
            act.sem_inc(p_done, 2)
            act.sem_inc(ot_copied, 1)

            def probs(b, g, g2, gp):
                u = NG * b + g
                act.wait_ge(av_done, u + AV0 - 1)
                for j in range(GH):
                    for half in range(2):
                        act.wait_ge(s_ready, 8 * u + 2 * j + half + 1)
                        nc.scalar.activation(prob[gp][:, j, 2 * half:2 * half + 2, :].rearrange("p a b -> p (a b)"),
                                             sps[half][:, :, :].rearrange("p a b -> p (a b)"), ACT.Exp).then_inc(p_done, 1)
                act.wait_ge(av_done, u + AV0 + 1)
                act.wait_ge(ott_done, u + 1)
                nc.scalar.activation(OT[gp][:, :], ops[:, :], ACT.Copy).then_inc(ot_copied, 1)

            def post(b):
                act.wait_ge(on_turned, b + 2)
                act.wait_ge(y_done, b + 1)
                nc.scalar.activation(OTn[:, :], mps[:, :], ACT.Copy).then_inc(otn_done, 1)

            units(act, None, probs, probs, post)

        @block.vector
        def _(v):
            v.sem_inc(a_used, 2)
            v.sem_inc(o_done, 1)
            v.sem_inc(y_added, 1)
            v.wait_ge(bias_added, 1)

            def maxima(b, g, g2, gp):
                u = NG * b + g
                for s in range(4 * GH):
                    v.wait_ge(a_ready, SLOTS * u + s + 1)
                    nc.vector.tensor_reduce(nm[gp][:, s:s + 1], aps[s % 2][:, :], AX.X, ALU.max, negate=True).then_inc(a_used, 1)

            def split_maxima(b, g, g2, gp):
                u = NG * b + g
                v.wait_ge(a_ready, SLOTS * (u + 1))
                v.wait_ge(max_loaded[gp], 48 * (2 * b + g2 + 1))
                nc.vector.tensor_copy(mr[:, :], aps[0][0:4 * GH, 0:P]).then_inc(a_used, 1)
                v.drain()
                split3(nc, v, nc.vector, mr[:, :], [ms[gp][:, s, :] for s in range(3)], mrest[:, :], v.drain).then_inc(ms_done, 1)
                v.drain()

            def outputs(b, g, g2, gp):
                u = NG * b + g
                v.wait_ge(ott_done, u + 3)
                v.wait_ge(on_turned, b + 1)
                m = mps[:, :].rearrange("p (q j e) -> p q j e", q=TC, j=GH)
                nc.vector.reciprocal(den[:, :, :], m[:, :, :, HD])
                v.drain()
                for q in range(TC):
                    last = nc.vector.tensor_tensor(O[:, q, bass.ts(g, GH * HD)].rearrange("p (j e) -> p j e", e=HD),
                                                   m[:, q, :, 0:HD], bcast(den[:, q, :], HD), ALU.mult)
                last.then_inc(o_done, 1)

            def first(b, g, g2, gp):
                maxima(b, g, g2, gp)
                split_maxima(b, g, g2, gp)

            def both(b, g, g2, gp):
                maxima(b + 1, g, g2, gp)
                outputs(b, g, g2, gp)
                split_maxima(b + 1, g, g2, gp)

            def post(b):
                v.wait_ge(y_done, b + 2)
                xt = net.x[:, bass.ts(b, 4), :].rearrange("p a b -> p (a b)")
                nc.vector.tensor_tensor(xt, xt, mps[:, :], ALU.add).then_inc(y_added, 1)

            units(v, first, both, outputs, post)


def moe_capacity_relu(nc, net, d):
    E, _, nf = d["L0_ffn_b1"].shape
    cap = -(-(B * S) * 5 // (E * 4))
    with ExitStack() as ctx:
        r = Router(nc, ctx, "m0", E)
        normalise(nc, net, "m0")
        router_logits(nc, net, "m0", d["L0_ffn_router_w"], E, r.lg)
        top1_prob(nc, r, "m0")
        capacity_by_probability(nc, net, r, cap, "m0")
        gated_bias(nc, net, "m0", r.gate, d["L0_ffn_b2"])
        W1 = d["L0_ffn_W1"].rearrange("e d f -> d e f")
        W2 = d["L0_ffn_W2"].rearrange("e (g f) d -> f e g d", f=P)
        b1 = d["L0_ffn_b1"].rearrange("e f g -> f e g")
        experts(nc, net, "m0e", E, nf, ACT.Relu, lambda t, e, k: r.gate[:, t, bass.ds(e, 1)],
                lambda e: [(lambda t: t[:, :], W1[:, bass.ds(e, 1), :].rearrange("d a f -> d (a f)"))],
                lambda e: [(lambda t: t[:, :, :], W2[:, bass.ds(e, 1), :, :].rearrange("f a g d -> f (a g) d"))],
                b1=lambda e: b1[:, bass.ds(e, 1), :].rearrange("f a g -> f (a g)"))
    measure(nc, net, "m0")


def phase_memory(nc, net, d):
    import math
    T1 = d["L1_attn_W_dt1"].shape[1]
    TWO_PI_HI = 6.28125
    TWO_PI_LO = 2 * math.pi - TWO_PI_HI
    ROUND = 1.5 * 2.0 ** 23
    normalise(nc, net, "a1")
    with ExitStack() as ctx:
        p = Scope(nc, ctx, "a1")
        WB, WC, Wo, Dg = (p.sb(n, [P, P]) for n in ("WB", "WC", "Wo", "Dg"))
        W1, W2 = p.sb("W1", [P, T1]), p.sb("W2", [T1, P])
        bB, bC, b2, om0, Dc, b1 = (p.sb(n, [P, 1]) for n in ("bB", "bC", "b2", "om0", "Dc", "b1"))
        half_pi, one, bo = p.sb("half_pi", [P, 1]), p.sb("one", [P, S]), p.sb("bo", [P, D])
        two = lambda n, s=S, q=P: [p.sb(f"{n}{i}", [q, s]) for i in range(2)]
        xc, t1, rz, l, ph, sn, cn, r = (two("xc"), two("t1", S, T1), two("rz"), two("l"), two("ph"), two("sn"),
                                        two("cn"), two("r"))
        az, om, k, content, cc, cs = (p.sb(n, [P, S]) for n in ("az", "om", "k", "content", "cc", "cs"))
        t1ps, t2ps = p.ps("t1ps"), p.ps("t2ps")
        bps, cps, yps = ([p.ps(f"{n}{i}") for i in range(2)] for n in ("bps", "cps", "yps"))
        loaded, consts, diag, bias_added = p.sem("loaded"), p.sem("consts"), p.sem("diag"), p.sem("bias_added")
        xc_done, t1_ready, t1_done, t2_ready, sp_done, phi_done, trig_done, bc_ready, r_done, y_done, y_used = (
            p.sem(n) for n in ("xc_done", "t1_ready", "t1_done", "t2_ready", "sp_done", "phi_done", "trig_done",
                               "bc_ready", "r_done", "y_done", "y_used"))
        block = ctx.enter_context(nc.Block())
        a = lambda n: d[f"L1_attn_{n}"]
        loads = [(WB, a("W_B")), (WC, a("W_C")), (Wo, a("W_out")), (W1, a("W_dt1")), (W2, a("W_dt2")),
                 (bB, col(a("b_B"))), (bC, col(a("b_C"))), (b2, col(a("b_dt2"))), (om0, col(a("omega_base"))),
                 (Dc, col(a("D")))]

        @block.sync
        def _(sp):
            for t, src in loads:
                sp.dma_start(t[:, :], src).then_inc(loaded, 16)
            sp.dma_start(b1[0:T1, :], col(a("b_dt1"))).then_inc(loaded, 16)
            sp.dma_start(bo[:, :], row(a("b_out")).to_broadcast([P, D])).then_inc(loaded, 16)

        N_LOADED = 16 * (len(loads) + 2)

        @block.gpsimd
        def _(pool):
            nc.gpsimd.memset(one[:, :], 1.0)
            nc.gpsimd.memset(half_pi[:, :], math.pi / 2).then_inc(consts, 1)
            pool.wait_ge(loaded, N_LOADED)
            nc.gpsimd.tensor_scalar(Dg[:, :], net.ident[:, :], Dc[:, :], None, ALU.mult).then_inc(diag, 1)
            nc.gpsimd.tensor_tensor(net.x[:, :, :], net.x[:, :, :], over_tiles(bo[:, :], NT), ALU.add).then_inc(bias_added, 1)

        @block.tensor
        def _(pe):
            pe.wait_ge(loaded, N_LOADED)
            pe.wait_ge(diag, 1)
            pe.sem_inc(t2_ready, 2)
            pe.sem_inc(y_done, 2)

            def inner(c, par):
                pe.wait_ge(xc_done, c + 1)
                pe.wait_ge(t1_done, c + 1)
                nc.tensor.matmul(t1ps[0:T1, :], W1[:, :], xc[par][:, :], start=True, stop=True).then_inc(t1_ready, 1)
                pe.wait_ge(r_done, c + 1)
                nc.tensor.matmul(bps[par][:, :], WB[:, :], xc[par][:, :], start=True, stop=True)
                nc.tensor.matmul(cps[par][:, :], WC[:, :], xc[par][:, :], start=True, stop=True).then_inc(bc_ready, 1)
                pe.wait_ge(t1_done, c + 2)
                pe.wait_ge(sp_done, c + 1)
                nc.tensor.matmul(t2ps[:, :], W2[:, :], t1[par][0:T1, :], start=True, stop=True).then_inc(t2_ready, 1)

            def outer(c, par):
                pe.wait_ge(r_done, c + 3)
                pe.wait_ge(y_used, c + 1)
                for q in range(TC):
                    tok = slice(q * P, (q + 1) * P)
                    nc.tensor.matmul(yps[par][:, tok], r[par][:, tok], Wo[:, :], start=True, stop=False)
                    last = nc.tensor.matmul(yps[par][:, tok], xc[par][:, tok], Dg[:, :], start=False, stop=True)
                last.then_inc(y_done, 1)

            one_chunk_ahead(pe, inner, outer)

        @block.scalar
        def _(act):
            act.wait_ge(loaded, N_LOADED)
            act.wait_ge(consts, 1)
            act.sem_inc(t1_done, 1)
            act.sem_inc(sp_done, 1)
            act.sem_inc(trig_done, 2)

            def softplus(c, par):
                act.wait_ge(y_done, c + 1)
                nc.scalar.activation(xc[par][:, :], net.xT[:, bass.ts(c, S)], ACT.Copy).then_inc(xc_done, 1)
                act.wait_ge(t1_ready, c + 1)
                act.wait_ge(t2_ready, c + 1)
                nc.scalar.activation(t1[par][0:T1, :], t1ps[0:T1, :], ACT.Identity, bias=b1[0:T1, :]).then_inc(t1_done, 1)
                act.wait_ge(t2_ready, c + 3)
                act.wait_ge(phi_done, c + 1)
                nc.scalar.activation(rz[par][:, :], t2ps[:, :], ACT.Relu, bias=b2[:, :])
                nc.scalar.activation(az[:, :], t2ps[:, :], ACT.Abs, bias=b2[:, :])
                act.drain()
                nc.scalar.activation(az[:, :], az[:, :], ACT.Exp, scale=-1.0)
                act.drain()
                nc.scalar.activation(l[par][:, :], az[:, :], ACT.Ln, bias=1.0).then_inc(sp_done, 1)

            def trig(c, par):
                act.wait_ge(phi_done, c + 3)
                act.wait_ge(r_done, c + 1)
                nc.scalar.activation(sn[par][:, :], ph[par][:, :], ACT.Sin)
                nc.scalar.activation(cn[par][:, :], ph[par][:, :], ACT.Abs)
                act.drain()
                nc.scalar.activation(cn[par][:, :], cn[par][:, :], ACT.Sin, bias=half_pi[:, :], scale=-1.0).then_inc(trig_done, 1)

            one_chunk_ahead(act, softplus, trig)

        @block.vector
        def _(v):
            tt, ts, stt = nc.vector.tensor_tensor, nc.vector.tensor_scalar, nc.vector.scalar_tensor_tensor
            v.sem_inc(phi_done, 2)
            v.sem_inc(r_done, 2)
            v.sem_inc(y_used, 2)
            v.wait_ge(loaded, N_LOADED)
            v.wait_ge(consts, 1)
            v.wait_ge(bias_added, 1)

            def phase(c, par):
                v.wait_ge(sp_done, c + 2)
                tt(om[:, :], rz[par][:, :], l[par][:, :], ALU.add)
                v.drain()
                ts(om[:, :], om[:, :], om0[:, :], None, ALU.mult)
                v.drain()
                v.wait_ge(trig_done, c + 1)
                nc.vector.tensor_tensor_scan(ph[par][:, :], one[:, :], om[:, :], 0.0, ALU.mult, ALU.add)
                v.drain()
                ts(k[:, :], ph[par][:, :], 1 / (2 * math.pi), ROUND, ALU.mult, ALU.add)
                v.drain()
                ts(k[:, :], k[:, :], -ROUND, None, ALU.add)
                v.drain()
                stt(ph[par][:, :], k[:, :], -TWO_PI_HI, ph[par][:, :], ALU.mult, ALU.add)
                v.drain()
                stt(ph[par][:, :], k[:, :], -TWO_PI_LO, ph[par][:, :], ALU.mult, ALU.add)
                v.drain()
                ts(ph[par][:, :], ph[par][:, :], 3.1415925, -3.1415925, ALU.min, ALU.max).then_inc(phi_done, 1)

            def memory(c, par):
                v.wait_ge(bc_ready, c + 1)
                v.wait_ge(trig_done, c + 3)
                stt(content[:, :], bps[par][:, :], bB[:, :], xc[par][:, :], ALU.add, ALU.mult)
                v.drain()
                tt(cc[:, :], content[:, :], cn[par][:, :], ALU.mult)
                tt(cs[:, :], content[:, :], sn[par][:, :], ALU.mult)
                v.drain()
                nc.vector.tensor_tensor_scan(content[:, :], one[:, :], cc[:, :], 0.0, ALU.mult, ALU.add)
                nc.vector.tensor_tensor_scan(k[:, :], one[:, :], cs[:, :], 0.0, ALU.mult, ALU.add)
                v.drain()
                tt(cc[:, :], content[:, :], cn[par][:, :], ALU.mult)
                tt(cs[:, :], k[:, :], sn[par][:, :], ALU.mult)
                v.drain()
                tt(cc[:, :], cc[:, :], cs[:, :], ALU.add)
                v.drain()
                v.wait_ge(y_done, c + 1)
                stt(r[par][:, :], cps[par][:, :], bC[:, :], cc[:, :], ALU.add, ALU.mult).then_inc(r_done, 1)
                v.wait_ge(y_done, c + 3)
                xt = net.x[:, bass.ts(c, 4), :].rearrange("p a b -> p (a b)")
                tt(xt, xt, yps[par][:, :], ALU.add).then_inc(y_used, 1)

            one_chunk_ahead(v, phase, memory)
    measure(nc, net, "a1")


def best_groups_gate(nc, net, r, scores, groups, keep_groups, top, tag):
    E, size = r.E, r.E // groups
    with ExitStack() as ctx:
        p = Scope(nc, ctx, tag + "_bg")
        iota_done, shifted, exped = p.sem("iota_done"), p.sem("shifted"), p.sem("exped")
        giota, gs, geq, goh, gsel = (p.sb(n, [P, NT, groups]) for n in ("giota", "gs", "geq", "goh", "gsel"))
        gm, total = p.sb("gm", [P, NT]), p.sb("total", [P, NT])
        cur, sel = p.sb("cur", [P, NT, E]), p.sb("sel", [P, NT, E])
        block = ctx.enter_context(nc.Block())

        @block.gpsimd
        def _(pool):
            nc.gpsimd.iota(giota[:, :, :], pattern=[[0, NT], [1, groups]], base=0, channel_multiplier=0,
                           allow_small_or_imprecise_dtypes=True).then_inc(iota_done, 1)
            nc.gpsimd.iota(r.iota[:, :, :], pattern=[[0, NT], [1, E]], base=0, channel_multiplier=0,
                           allow_small_or_imprecise_dtypes=True).then_inc(iota_done, 1)

        @block.scalar
        def _(act):
            act.wait_ge(shifted, 1)
            nc.scalar.activation(scores[:, :, :], scores[:, :, :], ACT.Exp).then_inc(exped, 1)

        @block.vector
        def _(v):
            def pick(cur, m, eq, oh, iota, sel, n, times):
                nc.vector.memset(sel, 0.0)
                for _ in range(times):
                    first_best(nc, v, cur, m, eq, r.idx, oh, iota, n)
                    nc.vector.tensor_tensor(sel, sel, oh[:, :, :], ALU.add)
                    nc.vector.scalar_tensor_tensor(cur[:, :, :], oh[:, :, :], -4.0, cur[:, :, :], ALU.mult, ALU.add)
                    v.drain()

            v.wait_ge(iota_done, 2)
            nc.vector.tensor_reduce(r.m[:, :], r.lg[:, :, :], AX.X, ALU.max)
            v.drain()
            nc.vector.tensor_tensor(scores[:, :, :], r.lg[:, :, :], bcast(r.m[:, :], E), ALU.subtract).then_inc(shifted, 1)
            v.wait_ge(exped, 1)
            nc.vector.tensor_reduce(total[:, :], scores[:, :, :], AX.X, ALU.add)
            v.drain()
            nc.vector.reciprocal(total[:, :], total[:, :])
            v.drain()
            nc.vector.tensor_tensor(scores[:, :, :], scores[:, :, :], bcast(total[:, :], E), ALU.mult)
            v.drain()
            nc.vector.tensor_reduce(gs[:, :, :], scores[:, :, :].rearrange("p t (g s) -> p t g s", s=size), AX.X, ALU.max)
            v.drain()
            pick(gs, gm, geq, goh, giota, gsel[:, :, :], groups, keep_groups)
            v4 = lambda a: a.rearrange("p t (g s) -> p (t g) s", s=size)
            nc.vector.tensor_tensor(v4(cur[:, :, :]), v4(scores[:, :, :]),
                                    bcast(gsel[:, :, :].rearrange("p t g -> p (t g)"), size), ALU.mult)
            v.drain()
            pick(cur, r.m, r.eq, r.oh, r.iota, sel[:, :, :], E, top)
            nc.vector.tensor_tensor(r.gate[:, :, :], sel[:, :, :], scores[:, :, :], ALU.mult)


def moe_grouped_swiglu(nc, net, d):
    E, _, I = d["L1_ffn_w1"].shape
    with ExitStack() as ctx:
        r = Router(nc, ctx, "m1", E)
        scores = Scope(nc, ctx, "m1s").sb("scores", [P, NT, E])
        normalise(nc, net, "m1")
        router_logits(nc, net, "m1", d["L1_ffn_gate_w"], E, r.lg)
        best_groups_gate(nc, net, r, scores, 4, 2, 4, "m1")
        w1, w3 = (d[f"L1_ffn_{n}"].rearrange("e d i -> d e i") for n in ("w1", "w3"))
        w2 = d["L1_ffn_w2"].rearrange("e i d -> i e d")
        one = Scope(nc, ctx, "m1o").sb("one", [P, 1])
        pair = lambda w: lambda e: [(lambda t: t[:, :].rearrange("d (e i) -> d e i", e=2), w[:, bass.ds(2 * e, 2), :])]
        down = lambda e: [(lambda t, q=q: t[q * I:(q + 1) * I, 0, q * P:(q + 1) * P],
                           w2[:, bass.ds(2 * e + q, 1), :].rearrange("i a d -> i (a d)")) for q in range(2)]
        experts(nc, net, "m1e", E // 2, 1, ACT.Silu, lambda t, e, q: r.gate[:, t, bass.ds(2 * e + q, 1)],
                pair(w1), down, w3=pair(w3), nb=2)
        whole = lambda n: lambda e: [(lambda t: t[:, :], d[f"L1_ffn_{n}"])]
        experts(nc, net, "m1sh", 1, 1, ACT.Silu, lambda t, e, q: net.ones[:, 0:1],
                whole("ws1"), lambda e: [(lambda t: t[:, 0, :], d["L1_ffn_ws2"])], w3=whole("ws3"))
    measure(nc, net, "m1")


def causal_attention(nc, net, d):
    H = d["L2_attn_wq"].shape[1]
    scale = H ** -0.5
    a = lambda n: d[f"L2_attn_{n}"]
    PLACE = [(0, 0), (1, 0), (0, P), (2, 0)]
    POFF = [0, P, 3 * P, 6 * P]
    PV0 = 10
    normalise(nc, net, "a2")
    with ExitStack() as ctx:
        p = Scope(nc, ctx, "a2")
        wq, wk, wv = (p.sb(n, [P, H]) for n in ("wq", "wk", "wv"))
        wo, bq, bk = p.sb("wo", [P, D]), p.sb("bq", [H, 1]), p.sb("bk", [H, 1])
        bv, bo, mask = p.sb("bv", [P, H]), p.sb("bo", [P, D]), p.sb("mask", [P, P])
        two = lambda n, s: [p.sb(f"{n}{i}", [P, *s]) for i in range(2)]
        xc, qT, kT, V = two("xc", [S]), two("qT", [S]), two("kT", [S]), two("V", [TC, H])
        prob, nb, sums, ri = two("prob", [10 * P]), two("nb", [TC]), two("sums", [TC]), two("ri", [TC])
        PT, z = two("PT", [S]), p.sb("z", [P, TC, P])
        pj, zps, yps = p.ps("pj"), p.ps("zps", [P, TC, H]), p.ps("yps")
        sps, tps = [p.ps(f"sps{i}") for i in range(3)], [p.ps(f"tps{i}") for i in range(2)]
        wo_zeroed = p.sem("wo_zeroed")
        loaded, zeroed, bias_added = p.sem("loaded"), p.sem("zeroed"), p.sem("bias_added")
        xc_done, pj_ready, pj_used, s_ready, nb_done, p_done = (
            p.sem(n) for n in ("xc_done", "pj_ready", "pj_used", "s_ready", "nb_done", "p_done"))
        t_ready, t_used, pv_done, z_ready, z_done, y_used = (
            p.sem(n) for n in ("t_ready", "t_used", "pv_done", "z_ready", "z_done", "y_used"))
        block = ctx.enter_context(nc.Block())
        N_LOADED = 16 * 8

        @block.sync
        def _(sp):
            sp.wait_ge(wo_zeroed, 1)
            for t, src in ((wq, a("wq")), (wk, a("wk")), (wv, a("wv")), (wo, a("wo")), (bq, col(a("bq"))),
                           (bk, col(a("bk"))), (bv, row(a("bv")).to_broadcast([P, H])),
                           (bo, row(a("bo")).to_broadcast([P, D]))):
                sp.dma_start(t[:, :] if t is not wo else wo[0:H, :], src).then_inc(loaded, 16)

        @block.gpsimd
        def _(pool):
            nc.gpsimd.memset(wo[:, :], 0.0).then_inc(wo_zeroed, 1)
            nc.gpsimd.memset(z[:, :, H:P], 0.0)
            for i in range(2):
                nc.gpsimd.memset(qT[i][:, :], 0.0)
                nc.gpsimd.memset(kT[i][:, :], 0.0)
            nc.gpsimd.memset(mask[:, :], 0.0).then_inc(zeroed, 1)
            pool.wait_ge(zeroed, 1)
            nc.gpsimd.affine_select(out=mask[:, :], in_=mask[:, :], compare_op=ALU.is_ge, fill=-1e11 / scale,
                                    base=0, pattern=[[-1, P]], channel_multiplier=1).then_inc(zeroed, 1)
            pool.wait_ge(loaded, N_LOADED)
            nc.gpsimd.tensor_tensor(net.x[:, :, :], net.x[:, :, :], over_tiles(bo[:, :], NT), ALU.add).then_inc(bias_added, 1)

        @block.tensor
        def _(pe):
            pe.wait_ge(loaded, N_LOADED)
            pe.wait_ge(zeroed, 2)
            pe.sem_inc(pv_done, PV0)

            def scores(c, par):
                pe.wait_ge(xc_done, c + 1)
                pe.wait_ge(pj_used, 3 * c + 1)
                nc.tensor.matmul(pj[0:H, :], wq[:, :], xc[par][:, :], start=True, stop=True).then_inc(pj_ready, 1)
                pe.wait_ge(pj_used, 3 * c + 2)
                nc.tensor.matmul(pj[0:H, :], wk[:, :], xc[par][:, :], start=True, stop=True).then_inc(pj_ready, 1)
                pe.wait_ge(pj_used, 3 * c + 3)
                for k in range(TC):
                    last = nc.tensor.matmul(pj[:, k * H:(k + 1) * H], xc[par][:, k * P:(k + 1) * P], wv[:, :],
                                            start=True, stop=True)
                last.then_inc(pj_ready, 1)
                for q in range(TC):
                    bank, off = PLACE[q]
                    pe.wait_ge(p_done, 4 * c + (3 if bank == 0 else q + 1))
                    n = (q + 1) * P
                    nc.tensor.matmul(sps[bank][:, off:off + n], qT[par][:, q * P:n], kT[par][:, 0:n],
                                     start=True, stop=True).then_inc(s_ready, 1)

            def values(c, par):
                def turn(q):
                    u = 5 * c + q
                    b = (par + q) % 2
                    pe.wait_ge(p_done, 4 * c + q + 5)
                    pe.wait_ge(t_used, u + 1)
                    for k in range(q + 1):
                        last = nc.tensor.transpose(tps[b][:, k * P:(k + 1) * P],
                                                   prob[par][:, POFF[q] + k * P:POFF[q] + (k + 1) * P], net.ident[:, :])
                    last.then_inc(t_ready, 1)

                def pv(q):
                    pe.wait_ge(t_used, 5 * c + q + 3)
                    for k in range(q + 1):
                        last = nc.tensor.matmul(zps[:, q, :], PT[(par + q) % 2][:, k * P:(k + 1) * P], V[par][:, k, :],
                                                start=(k == 0), stop=(k == q))
                    last.then_inc(pv_done, 1)

                turn(0)
                turn(1)
                pe.wait_ge(z_done, c + 1)
                pv(0)
                turn(2)
                pv(1)
                turn(3)
                pv(2)
                pv(3)
                b = par % 2
                pe.wait_ge(z_done, c + 2)
                pe.wait_ge(t_used, 5 * c + 5)
                for k in range(TC):
                    last = nc.tensor.transpose(tps[b][:, k * P:(k + 1) * P], z[:, k, :], net.ident[:, :])
                last.then_inc(t_ready, 1)
                pe.wait_ge(t_used, 5 * c + 7)
                pe.wait_ge(y_used, c + 1)
                for k in range(TC):
                    last = nc.tensor.matmul(yps[:, k * P:(k + 1) * P], PT[b][:, k * P:(k + 1) * P], wo[:, :],
                                            start=True, stop=True)
                last.then_inc(pv_done, 1)

            one_chunk_ahead(pe, scores, values)

        @block.scalar
        def _(act):
            act.wait_ge(loaded, N_LOADED)
            act.wait_ge(zeroed, 2)
            act.sem_inc(pj_used, 1)
            act.sem_inc(p_done, 4)
            with act.Fori(0, B // 2) as i:
                for par in range(2):
                    c = 2 * i + par
                    act.wait_ge(pv_done, PV0 + 5 * c - 5)
                    nc.scalar.activation(xc[par][:, :], net.xT[:, bass.ts(c, S)], ACT.Copy).then_inc(xc_done, 1)
                    for n, (t, bias) in enumerate(((qT, bq), (kT, bk))):
                        act.wait_ge(pj_ready, 3 * c + n + 1)
                        nc.scalar.activation(t[par][0:H, :], pj[0:H, :], ACT.Identity, bias=bias[:, :]).then_inc(pj_used, 1)
                    act.wait_ge(pj_ready, 3 * c + 3)
                    nc.scalar.activation(V[par][:, :, :].rearrange("p a b -> p (a b)"), pj[:, 0:TC * H], ACT.Copy).then_inc(pj_used, 1)
                    for q in range(TC):
                        bank, off = PLACE[q]
                        act.wait_ge(nb_done, 4 * c + (3 if bank == 0 else q + 1))
                        nc.scalar.activation(prob[par][:, POFF[q]:POFF[q] + (q + 1) * P], sps[bank][:, off:off + (q + 1) * P],
                                             ACT.Exp, bias=nb[par][:, q:q + 1], scale=scale,
                                             accum_out=sums[par][:, q:q + 1]).then_inc(p_done, 1)

        @block.vector
        def _(v):
            v.sem_inc(t_used, 2)
            v.sem_inc(z_done, 1)
            v.sem_inc(y_used, 1)
            v.wait_ge(zeroed, 2)
            v.wait_ge(bias_added, 1)

            def maxima(c, par):
                for q in range(TC):
                    bank, off = PLACE[q]
                    n = (q + 1) * P
                    v.wait_ge(s_ready, 4 * c + (3 if bank == 0 else q + 1))
                    dg = sps[bank][:, off + q * P:off + n]
                    nc.vector.tensor_tensor(dg, dg, mask[:, :], ALU.add)
                    v.drain()
                    nc.vector.tensor_reduce(nb[par][:, q:q + 1], sps[bank][:, off:off + n], AX.X, ALU.max)
                    v.drain()
                    nc.vector.tensor_scalar(nb[par][:, q:q + 1], nb[par][:, q:q + 1], -scale, None, ALU.mult).then_inc(nb_done, 1)

            def outputs(c, par):
                def copy(q, rows, n):
                    u = 5 * c + q
                    v.wait_ge(t_ready, u + 1)
                    v.wait_ge(pv_done, PV0 + u - 1)
                    nc.vector.tensor_copy(PT[(par + q) % 2][0:rows, 0:n], tps[(par + q) % 2][0:rows, 0:n]).then_inc(t_used, 1)

                v.wait_ge(p_done, 4 * c + 8)
                nc.vector.reciprocal(ri[par][:, :], sums[par][:, :])
                for q in range(TC):
                    copy(q, P, (q + 1) * P)
                v.drain()
                v.wait_ge(pv_done, PV0 + 5 * c + 4)
                for q in range(TC):
                    last = nc.vector.scalar_tensor_tensor(z[:, q, 0:H], zps[:, q, :], ri[par][:, q:q + 1], bv[:, :],
                                                          ALU.mult, ALU.add)
                last.then_inc(z_done, 1)
                copy(4, P, S)
                v.wait_ge(pv_done, PV0 + 5 * c + 5)
                xt = net.x[:, bass.ts(c, 4), :].rearrange("p a b -> p (a b)")
                nc.vector.tensor_tensor(xt, xt, yps[:, :], ALU.add).then_inc(y_used, 1)

            one_chunk_ahead(v, maxima, outputs)
    measure(nc, net, "a2")


def moe_top1_gelu(nc, net, d):
    E = 8
    with ExitStack() as ctx:
        p = Scope(nc, ctx, "m2")
        lg, eq, oh = p.sb("lg", [P, NT, E]), p.sb("eq", [P, NT, E]), p.sb("onehot", [P, NT, E])
        m, idx, iota = p.sb("m", [P, NT]), p.sb("idx", [P, NT]), p.sb("iota", [P, NT, E])
        normalise(nc, net, "m2")
        router_logits(nc, net, "m2", d["L2_ffn_Wg"], E, lg, bias=d["L2_ffn_bg"])
        with ExitStack() as c2:
            iota_done = Scope(nc, c2, "m2r").sem("iota_done")
            block = c2.enter_context(nc.Block())

            @block.gpsimd
            def _(pool):
                nc.gpsimd.iota(iota[:, :, :], pattern=[[0, NT], [1, E]], base=0, channel_multiplier=0,
                               allow_small_or_imprecise_dtypes=True).then_inc(iota_done, 1)

            @block.vector
            def _(v):
                v.wait_ge(iota_done, 1)
                first_best(nc, v, lg, m, eq, idx, oh, iota, E)
        gated_bias(nc, net, "m2", oh, d["L2_ffn_b2"])
        W1 = d["L2_ffn_W1"].rearrange("e d f -> d e f")
        W2 = d["L2_ffn_W2"].rearrange("e f d -> f e d")
        b1 = d["L2_ffn_b1"].rearrange("e f a -> f e a")
        experts(nc, net, "m2e", E, 1, ACT.Gelu, lambda t, e, k: oh[:, t, bass.ds(e, 1)],
                lambda e: [(lambda t: t[:, :], W1[:, bass.ds(e, 1), :].rearrange("d a f -> d (a f)"))],
                lambda e: [(lambda t: t[:, 0, :], W2[:, bass.ds(e, 1), :].rearrange("d a f -> d (a f)"))],
                b1=lambda e: b1[:, bass.ds(e, 1), :].rearrange("f a b -> f (a b)"))
    measure(nc, net, "m2")


def root_mean_square(nc, net, tag, h, r, weight=None, out=None, first=None):
    with ExitStack() as ctx:
        p = Scope(nc, ctx, tag)
        junk, ss = p.sb("junk", [P, D]), p.sb("ss", [P, NT])
        h_done, ss_done, w_loaded = p.sem("h_done"), p.sem("ss_done"), p.sem("w_loaded")
        wb = p.sb("wb", [P, D])
        block = ctx.enter_context(nc.Block())

        @block.sync
        def _(sp):
            if weight is not None:
                sp.dma_start(wb[:, :], row(weight).to_broadcast([P, D])).then_inc(w_loaded, 16)

        @block.scalar
        def _(act):
            for t in range(NT):
                if first is not None and t % 4 == 0:
                    act.wait_ge(h_done, t // 4 + 1)
                nc.scalar.activation(junk[:, :], h[:, t, :], ACT.Square, accum_out=ss[:, t:t + 1])
                act.drain()
            nc.scalar.activation(ss[:, :], ss[:, :], ACT.Sqrt, scale=1.0 / D, bias=net.epst[:, 1:2]).then_inc(ss_done, 1)

        @block.vector
        def _(v):
            if first is not None:
                for t in range(NT):
                    last = first(t)
                    if t % 4 == 3:
                        last.then_inc(h_done, 1)
            v.wait_ge(ss_done, 1)
            nc.vector.reciprocal(r[:, :], ss[:, :])
            if out is not None:
                v.drain()
                v.wait_ge(w_loaded, 16)
                for t in range(NT):
                    nc.vector.scalar_tensor_tensor(out[:, t, :], h[:, t, :], r[:, t:t + 1], wb[:, :], ALU.mult, ALU.mult)


def turn_tokens(nc, net, tag, src, scale=None, weight=None):
    with ExitStack() as ctx:
        p = Scope(nc, ctx, tag)
        xn = [p.sb(f"xn{i}", [P, TC, D]) for i in range(2)]
        tps = [p.ps(f"tps{i}") for i in range(2)]
        wcol = p.sb("wcol", [P, 1])
        xn_done, t_done, t_free, w_loaded = p.sem("xn_done"), p.sem("t_done"), p.sem("t_free"), p.sem("w_loaded")
        block = ctx.enter_context(nc.Block())

        @block.sync
        def _(sp):
            if weight is not None:
                sp.dma_start(wcol[:, :], col(weight)).then_inc(w_loaded, 16)

        @block.vector
        def _(v):
            with v.Fori(0, B // 2) as i:
                for par in range(2):
                    c = 2 * i + par
                    v.wait_ge(t_done, c + 1)
                    if scale is None:
                        nc.vector.tensor_copy(xn[par][:, :, :], src[:, bass.ts(c, 4), :]).then_inc(xn_done, 1)
                    else:
                        nc.vector.tensor_tensor(xn[par][:, :, :], src[:, bass.ts(c, 4), :],
                                                bcast(scale[:, bass.ts(c, 4)], D), ALU.mult).then_inc(xn_done, 1)

        @block.tensor
        def _(pe):
            pe.sem_inc(t_done, 2)
            with pe.Fori(0, B // 2) as i:
                for par in range(2):
                    c = 2 * i + par
                    pe.wait_ge(xn_done, c + 1)
                    pe.wait_ge(t_free, c + 1)
                    for k in range(TC):
                        last = nc.tensor.transpose(tps[par][:, k * P:(k + 1) * P], xn[par][:, k, :], net.ident[:, :])
                    last.then_inc(t_done, 1)

        @block.scalar
        def _(act):
            act.sem_inc(t_free, 2)
            if weight is not None:
                act.wait_ge(w_loaded, 16)
            with act.Fori(0, B // 2) as i:
                for par in range(2):
                    c = 2 * i + par
                    act.wait_ge(t_done, c + 3)
                    kw = {} if weight is None else dict(scale=wcol[:, :])
                    nc.scalar.activation(net.xT[:, bass.ts(c, S)], tps[par][:, :], ACT.Identity if kw else ACT.Copy,
                                         **kw).then_inc(t_free, 1)


def decay_attention(nc, net, d):
    a = lambda n: d[f"L3_attn_{n}"]
    R = a("u").shape[1]
    K = a("k_base_kernel").shape[0]
    SUB = 32
    with ExitStack() as ctx:
        p = Scope(nc, ctx, "a3")
        h, hn = p.sb("h", [P, NT, D]), p.sb("hn", [P, NT, D])
        qk, rn = p.sb("qk", [P, NT, 2 * R]), p.sb("rn", [P, NT, 2])
        r1, g = p.sb("r1", [P, NT]), p.sb("g", [P, K])
        NB = P // SUB
        tQ, tQ2, tK, gP = p.sb("tQ", [R, P]), p.sb("tQ2", [R, P]), p.sb("tK", [R, NB, P]), p.sb("gP", [R, 1])
        tK2, causal = p.sb("tK2", [P, R]), p.sb("causal", [P, P])

        normalise_only = lambda t: nc.vector.tensor_scalar(h[:, t, :], net.x[:, t, :], net.stat[:, t, 0:1],
                                                           net.rstd[:, t:t + 1], ALU.subtract, ALU.mult)
        token_rstd(nc, net, "a3")
        root_mean_square(nc, net, "a3r1", h, r1, weight=a("norm1_w"), out=hn, first=normalise_only)
        turn_tokens(nc, net, "a3t", hn)
        router_logits(nc, net, "a3", (a("u"), a("v")), 2 * R, qk)
        decay_tables(nc, net, a, R, K, SUB, qk, rn, g, tQ, tQ2, tK, gP, tK2, causal)
        decay_mix(nc, net, a, R, K, SUB, h, hn, qk, rn, g, tQ, tQ2, tK, gP, tK2, causal)
        root_mean_square(nc, net, "a3r2", h, r1)
        turn_tokens(nc, net, "a3t2", h, scale=r1, weight=a("norm2_w"))
    F = a("mlp_w1").shape[1]
    experts(nc, net, "a3m", 1, F // P, ACT.Gelu_apprx_tanh, lambda t, e, q: net.ones[:, 0:1],
            lambda e: [(lambda t: t[:, :], a("mlp_w1"))],
            lambda e: [(lambda t: t[:, :, :], a("mlp_w2").rearrange("(g f) d -> f g d", f=P))],
            b1=lambda e: a("mlp_b1"))
    measure(nc, net, "a3")


def token_rstd(nc, net, tag):
    with ExitStack() as ctx:
        p = Scope(nc, ctx, tag + "_rs")
        std, std_done = p.sb("std", [P, NT]), p.sem("std_done")
        block = ctx.enter_context(nc.Block())

        @block.scalar
        def _(act):
            nc.scalar.activation(std[:, :], net.stat[:, :, 1], ACT.Sqrt, bias=net.epst[:, 0:1]).then_inc(std_done, 1)

        @block.vector
        def _(v):
            v.wait_ge(std_done, 1)
            nc.vector.reciprocal(net.rstd[:, :], std[:, :])


def decay_tables(nc, net, a, R, K, SUB, qk, rn, g, tQ, tQ2, tK, gP, tK2, causal):
    NB = P // SUB
    with ExitStack() as ctx:
        p = Scope(nc, ctx, "a3tab")
        dl, al = p.sb("dl", [R, 1]), p.sb("al", [R, 1])
        dlb, jcol = p.sb("dlb", [P, R]), p.sb("jcol", [P, 1])
        gate, sq = p.sb("gate", [P, 1]), p.sb("sq", [P, NT, 2 * R])
        loaded, counted, sig, clipped, lned, ready, squared, rooted = (
            p.sem(n) for n in ("loaded", "counted", "sig", "clipped", "lned", "ready", "squared", "rooted"))
        block = ctx.enter_context(nc.Block())

        @block.sync
        def _(sp):
            sp.dma_start(dl[:, :], col(a("decay_logit"))).then_inc(loaded, 16)
            sp.dma_start(al[:, :], col(a("alpha_logit"))).then_inc(loaded, 16)
            sp.dma_start(dlb[:, :], row(a("decay_logit")).to_broadcast([P, R])).then_inc(loaded, 16)
            sp.dma_start(gate[:, :], row(a("k_base_gate_logit")).to_broadcast([P, 1])).then_inc(loaded, 16)
            sp.dma_start(g[:, :], row(a("k_base_kernel")).to_broadcast([P, K])).then_inc(loaded, 16)

        @block.gpsimd
        def _(pool):
            io = dict(base=0, channel_multiplier=0, allow_small_or_imprecise_dtypes=True)
            nc.gpsimd.iota(tQ[:, :], pattern=[[0, NB], [1, SUB]], **io)
            nc.gpsimd.iota(tQ2[:, :], pattern=[[1, P]], **io)
            nc.gpsimd.iota(tK[:, :, :], pattern=[[SUB, NB], [-1, P]], **io)
            nc.gpsimd.memset(gP[:, :], float(P))
            nc.gpsimd.iota(jcol[:, :], pattern=[[0, 1]], base=P, channel_multiplier=-1,
                           allow_small_or_imprecise_dtypes=True)
            nc.gpsimd.memset(causal[:, :], 1.0).then_inc(counted, 1)
            pool.wait_ge(counted, 1)
            nc.gpsimd.affine_select(out=causal[:, :], in_=causal[:, :], compare_op=ALU.is_ge, fill=0.0,
                                    base=0, pattern=[[1, P]], channel_multiplier=-1).then_inc(counted, 1)

        @block.scalar
        def _(act):
            act.wait_ge(loaded, 80)
            act.wait_ge(squared, 1)
            nc.scalar.activation(rn[:, :, :], rn[:, :, :], ACT.Sqrt).then_inc(rooted, 1)
            for t in (dl, al, dlb, gate):
                last = nc.scalar.activation(t[:, :], t[:, :], ACT.Sigmoid)
            last.then_inc(sig, 1)
            act.wait_ge(clipped, 1)
            nc.scalar.activation(dl[:, :], dl[:, :], ACT.Ln)
            nc.scalar.activation(dlb[:, :], dlb[:, :], ACT.Ln).then_inc(lned, 1)
            act.wait_ge(ready, 1)
            act.drain()
            for t in (tQ[:, :], tQ2[:, :], tK[:, :, :], gP[:, :]):
                nc.scalar.activation(t, t, ACT.Exp, scale=dl[:, :])
            nc.scalar.activation(tK2[:, :], tK2[:, :], ACT.Exp)
            act.drain()
            for t in (tQ, tQ2):
                nc.scalar.activation(t[:, :], t[:, :], ACT.Copy, scale=al[:, :])

        @block.vector
        def _(v):
            nc.vector.tensor_tensor(sq[:, :, :], qk[:, :, :], qk[:, :, :], ALU.mult)
            v.drain()
            nc.vector.tensor_reduce(rn[:, :, :], sq[:, :, :].rearrange("p t (s r) -> p t s r", s=2), AX.X,
                                    ALU.add).then_inc(squared, 1)
            v.wait_ge(sig, 1)
            for t in (dl, dlb):
                last = nc.vector.tensor_scalar(t[:, :], t[:, :], 0.15, 1.0, ALU.max, ALU.min)
            last.then_inc(clipped, 1)
            v.wait_ge(counted, 2)
            nc.vector.tensor_scalar(tK[:, :, :], tK[:, :, :], float(1 - SUB), None, ALU.max)
            v.wait_ge(lned, 1)
            nc.vector.tensor_scalar(tK2[:, :], dlb[:, :], jcol[:, :], None, ALU.mult).then_inc(ready, 1)
            nc.vector.tensor_scalar(g[:, :], g[:, :], gate[:, :], None, ALU.mult)
            v.wait_ge(rooted, 1)
            nc.vector.tensor_scalar(rn[:, :, :], rn[:, :, :], 1e-8, None, ALU.max)
            v.drain()
            nc.vector.reciprocal(rn[:, :, :], rn[:, :, :])


def decay_mix(nc, net, a, R, K, SUB, h, hn, qk, rn, g, tQ, tQ2, tK, gP, tK2, causal):
    NB = P // SUB
    with ExitStack() as ctx:
        p = Scope(nc, ctx, "a3x")
        two = lambda n, s, q=P: [p.sb(f"{n}{i}", [q, *s]) for i in range(2)]
        proj, pb, mb = p.sb("proj", [P, D]), p.sb("pb", [P, D]), p.sb("mb", [P, D])
        hc, qc, kk = two("hc", [TC, D]), two("qc", [TC, 2 * R]), two("kk", [TC, R])
        Qp, Qpp, Kp = two("Qp", [S], R), two("Qpp", [S], R), two("Kp", [NB, S], R)
        AT, SS, T = two("AT", [S]), two("SS", [TC, D], R), two("T", [S])
        tq, tk, aps, sps = p.ps("tq"), p.ps("tk"), p.ps("aps"), p.ps("sps", [P, TC, D])
        dps, ops = [p.ps(f"dps{i}") for i in range(2)], [p.ps(f"ops{i}") for i in range(2)]
        loaded, bias_added, hc_done, qc_done, t_ready, tab_done = (
            p.sem(n) for n in ("loaded", "bias_added", "hc_done", "qc_done", "t_ready", "tab_done"))
        a_done, am_done, dec_done, conv_done, proj_done, add_done = (
            p.sem(n) for n in ("a_done", "am_done", "dec_done", "conv_done", "proj_done", "add_done"))
        block = ctx.enter_context(nc.Block())

        @block.sync
        def _(sp):
            sp.dma_start(proj[:, :], a("proj_w")).then_inc(loaded, 16)
            sp.dma_start(pb[:, :], row(a("proj_b")).to_broadcast([P, D])).then_inc(loaded, 16)
            sp.dma_start(mb[:, :], row(a("mlp_b2")).to_broadcast([P, D])).then_inc(loaded, 16)

        @block.gpsimd
        def _(pool):
            pool.wait_ge(loaded, 48)
            nc.gpsimd.tensor_tensor(h[:, :, :], h[:, :, :], over_tiles(pb[:, :], NT), ALU.add).then_inc(bias_added, 1)
            nc.gpsimd.tensor_tensor(net.x[:, :, :], net.x[:, :, :], over_tiles(mb[:, :], NT), ALU.add).then_inc(bias_added, 1)
            pool.wait_ge(bias_added, 2)
            with pool.Fori(0, B) as c:
                pool.wait_ge(add_done, c + 3)
                xt = net.x[:, bass.ts(c, 4), :]
                nc.gpsimd.tensor_tensor(xt, xt, h[:, bass.ts(c, 4), :], ALU.add)

        @block.scalar
        def _(act):
            with act.Fori(0, B // 2) as i:
                for par in range(2):
                    c = 2 * i + par
                    act.wait_ge(dec_done, c + 1)
                    nc.scalar.activation(hc[par][:, :, :], hn[:, bass.ts(c, 4), :], ACT.Copy).then_inc(hc_done, 1)

        @block.tensor
        def _(pe):
            pe.wait_ge(loaded, 48)
            pe.sem_inc(t_ready, 2)
            pe.sem_inc(a_done, 2)
            pe.sem_inc(dec_done, 2)
            pe.sem_inc(proj_done, 2)

            def inside(c, par):
                pe.wait_ge(qc_done, c + 1)
                pe.wait_ge(tab_done, c + 1)
                for k in range(TC):
                    tok = slice(k * P, (k + 1) * P)
                    nc.tensor.transpose(tq[0:R, tok], qc[par][:, k, 0:R], net.ident[:, :])
                    last = nc.tensor.transpose(tk[0:R, tok], qc[par][:, k, R:2 * R], net.ident[:, :])
                last.then_inc(t_ready, 1)
                pe.wait_ge(hc_done, c + 1)
                pe.wait_ge(am_done, c + 1)
                pe.wait_ge(tab_done, c + 2)
                for k in range(TC - 1):
                    nc.tensor.matmul(sps[0:R, k, :], kk[par][:, k, :], hc[par][:, k, :], start=True, stop=True)
                for k in range(TC):
                    for b in range(NB):
                        sub = slice(k * P + b * SUB, k * P + (b + 1) * SUB)
                        last = nc.tensor.matmul(aps[:, sub], Kp[par][0:R, b, k * P:(k + 1) * P], Qp[par][0:R, sub],
                                                start=True, stop=True)
                last.then_inc(a_done, 1)

            def across(c, par):
                pe.wait_ge(am_done, c + 2)
                pe.wait_ge(conv_done, c + 1)
                for k in range(TC):
                    tok = slice(k * P, (k + 1) * P)
                    last = nc.tensor.matmul(dps[par][:, tok], hc[par][:, k, :], AT[par][:, tok], start=True, stop=(k == 0))
                    if k > 0:
                        last = nc.tensor.matmul(dps[par][:, tok], SS[par][0:R, k, :], Qpp[par][0:R, tok],
                                                start=False, stop=True)
                last.then_inc(dec_done, 1)
                pe.wait_ge(conv_done, c + 3)
                pe.wait_ge(add_done, c + 1)
                for k in range(TC):
                    tok = slice(k * P, (k + 1) * P)
                    last = nc.tensor.matmul(ops[par][:, tok], T[par][:, tok], proj[:, :], start=True, stop=True)
                last.then_inc(proj_done, 1)

            one_chunk_ahead(pe, inside, across)

        @block.vector
        def _(v):
            tt, stt = nc.vector.tensor_tensor, nc.vector.scalar_tensor_tensor
            v.sem_inc(tab_done, 1)
            v.sem_inc(am_done, 1)
            v.sem_inc(conv_done, 2)
            v.sem_inc(add_done, 2)

            def inside(c, par):
                v.wait_ge(t_ready, c + 1)
                tt(qc[par][:, :, :].rearrange("p t (s r) -> p (t s) r", s=2),
                   qk[:, bass.ts(c, 4), :].rearrange("p t (s r) -> p (t s) r", s=2),
                   bcast(rn[:, bass.ts(c, 4), :].rearrange("p t s -> p (t s)"), R), ALU.mult).then_inc(qc_done, 1)
                v.drain()
                v.wait_ge(a_done, c + 1)
                tt(kk[par][:, :, :], qc[par][:, :, R:2 * R], over_tiles(tK2[:, :], TC), ALU.mult)
                v.wait_ge(t_ready, c + 3)
                v.wait_ge(dec_done, c + 1)
                tiles = lambda t: t.rearrange("r (t i) -> r t i", i=P)
                tt(tiles(Qp[par][:, :]), tiles(tq[0:R, :]), over_tiles(tQ[:, :], TC), ALU.mult)
                tt(tiles(Qpp[par][:, :]), tiles(tq[0:R, :]), over_tiles(tQ2[:, :], TC), ALU.mult)
                for b in range(NB):
                    last = tt(tiles(Kp[par][:, b, :]), tiles(tk[0:R, :]), over_tiles(tK[:, b, :], TC), ALU.mult)
                last.then_inc(tab_done, 1)
                v.wait_ge(a_done, c + 3)
                tt(AT[par][:, :].rearrange("j (t i) -> j t i", i=P), aps[:, :].rearrange("j (t i) -> j t i", i=P),
                   over_tiles(causal[:, :], TC), ALU.mult)
                nc.vector.tensor_copy(SS[par][:, 1, :], sps[0:R, 0, :])
                v.drain()
                stt(SS[par][:, 2, :], SS[par][:, 1, :], gP[:, :], sps[0:R, 1, :], ALU.mult, ALU.add)
                v.drain()
                stt(SS[par][:, 3, :], SS[par][:, 2, :], gP[:, :], sps[0:R, 2, :], ALU.mult, ALU.add).then_inc(am_done, 1)

            def across(c, par):
                v.wait_ge(dec_done, c + 3)
                v.wait_ge(proj_done, c + 1)
                t = T[par]
                stt(t[:, :], net.xT[:, bass.ts(c, S)], g[:, 0:1], dps[par][:, :], ALU.mult, ALU.add)
                v.drain()
                for j in range(1, K):
                    last = stt(t[:, j:], net.xT[:, bass.ds(c * S, S - j)], g[:, j:j + 1], t[:, j:], ALU.mult, ALU.add)
                    if j == K - 1:
                        last.then_inc(conv_done, 1)
                    v.drain()
                v.wait_ge(proj_done, c + 3)
                v.wait_ge(bias_added, 2)
                ht = h[:, bass.ts(c, 4), :].rearrange("p a b -> p (a b)")
                tt(ht, ht, ops[par][:, :], ALU.add).then_inc(add_done, 1)

            one_chunk_ahead(v, inside, across)


def moe_linear(nc, net, d):
    E = d["L3_ffn_b"].shape[0]
    with ExitStack() as ctx:
        r = Router(nc, ctx, "m3", E)
        normalise(nc, net, "m3")
        router_logits(nc, net, "m3", d["L3_ffn_wg"], E, r.lg)
        top1_prob(nc, r, "m3")
        capacity_by_order(nc, net, r, B * S // E, "m3")
        moe_linear_products(nc, net, d, r, E)
        gated_bias(nc, net, "m3", r.gate, d["L3_ffn_b"])


def moe_linear_products(nc, net, d, r, E):
    with ExitStack() as ctx:
        p = Scope(nc, ctx, "m3e")
        WT = p.sb("WT", [P, E, D])
        xn = [p.sb(f"xn{i}", [P, TC, D]) for i in range(2)]
        xc = [p.sb(f"xc{i}", [P, S]) for i in range(2)]
        tps = [p.ps(f"tps{i}") for i in range(2)]
        yps = [p.ps(f"yps{i}", [P, E, D]) for i in range(2)]
        loaded = p.sem("loaded")
        xn_done = p.sem("xn_done")
        t_done = p.sem("t_done")
        xc_done = p.sem("xc_done")
        y_done = p.sem("y_done")
        y_used = p.sem("y_used")
        block = ctx.enter_context(nc.Block())

        @block.sync
        def _(sp):
            sp.dma_start(WT[:, :, :], d["L3_ffn_W"]).then_inc(loaded, 16)

        @block.tensor
        def _(pe):
            pe.wait_ge(loaded, 16)
            pe.sem_inc(t_done, 2)
            pe.sem_inc(y_done, 5)

            def turn(c, par):
                pe.wait_ge(xn_done, c + 1)
                pe.wait_ge(xc_done, c + 1)
                for k in range(TC):
                    last = nc.tensor.transpose(tps[par][:, k * P:(k + 1) * P], xn[par][:, k, :], net.ident[:, :])
                last.then_inc(t_done, 1)

            def products(c, par):
                pe.wait_ge(xc_done, c + 3)
                for k in range(TC):
                    pe.wait_ge(y_used, 4 * c + k + 1)
                    for q in range(2):
                        last = nc.tensor.matmul(yps[k % 2][:, 4 * q:4 * q + 4, :].rearrange("p e d -> p (e d)"),
                                                xc[par][:, k * P:(k + 1) * P],
                                                WT[:, 4 * q:4 * q + 4, :].rearrange("p e d -> p (e d)"),
                                                start=True, stop=True)
                    last.then_inc(y_done, 1)

            one_chunk_ahead(pe, turn, products)

        @block.scalar
        def _(act):
            act.sem_inc(xc_done, 2)
            with act.Fori(0, B // 2) as i:
                for par in range(2):
                    c = 2 * i + par
                    act.wait_ge(t_done, c + 3)
                    act.wait_ge(y_done, 4 * c + 1)
                    nc.scalar.activation(xc[par][:, :], tps[par][:, :], ACT.Copy).then_inc(xc_done, 1)

        @block.vector
        def _(v):
            v.sem_inc(y_used, 2)

            def norm(c, par):
                v.wait_ge(t_done, c + 1)
                for k in range(TC):
                    last = nc.vector.tensor_scalar(xn[par][:, k, :], net.x[:, 4 * c + k, :],
                                                   net.stat[:, 4 * c + k, 0:1],
                                                   net.rstd[:, bass.ds(4 * c + k, 1)], ALU.subtract, ALU.mult)
                last.then_inc(xn_done, 1)

            def gather(c, par):
                for k in range(TC):
                    v.wait_ge(y_done, 4 * c + k + 6)
                    for e in range(E):
                        xt = net.x[:, 4 * c + k, :]
                        last = nc.vector.scalar_tensor_tensor(xt, yps[k % 2][:, e, :], r.gate[:, 4 * c + k, e:e + 1],
                                                              xt, ALU.mult, ALU.add)
                        if e == E - 1:
                            last.then_inc(y_used, 1)
                        v.drain()

            one_chunk_ahead(v, norm, gather)


def program(nc, d, out):
    Scope.used = []
    with ExitStack() as ctx:
        net = Net(nc, ctx)
        load_and_measure(nc, net, d["L0_attn_x"])
        relative_attention(nc, net, d)
        renew_semaphores(nc)
        moe_capacity_relu(nc, net, d)
        renew_semaphores(nc)
        phase_memory(nc, net, d)
        renew_semaphores(nc)
        moe_grouped_swiglu(nc, net, d)
        renew_semaphores(nc)
        causal_attention(nc, net, d)
        renew_semaphores(nc)
        moe_top1_gelu(nc, net, d)
        renew_semaphores(nc)
        decay_attention(nc, net, d)
        renew_semaphores(nc)
        moe_linear(nc, net, d)
        store(nc, net, out)


def tables():
    import numpy as np
    HD = 8
    div = np.exp(np.arange(0, HD, 2, dtype=np.float64) * (-np.log(10000.0) / HD))
    angle = np.arange(512)[None, :] * div[:, None]
    t = np.stack([np.sin(angle), np.cos(angle)], axis=1).reshape(HD, 512)
    m1, m2 = np.zeros((HD, HD)), np.zeros((HD, HD))
    for m in range(HD // 2):
        s, c = 2 * m, 2 * m + 1
        m1[s, c] = m1[c, c] = 1
        m2[s, s], m2[c, s] = 1, -1
    return {"rel_t": t.astype(np.float32), "rel_m1": m1.astype(np.float32), "rel_m2": m2.astype(np.float32)}


def laid_out(name, a):
    import numpy as np
    if name in ("L0_ffn_router_w", "L1_ffn_gate_w", "L3_attn_proj_w"):
        a = a.T
    elif name in ("L0_attn_w_qkv", "L0_attn_b_qkv"):
        a = a.reshape(a.shape[:-1] + (3, 16, 8))
        a = np.stack([np.swapaxes(a[..., 0, :, :], -1, -2).reshape(a.shape[:-3] + (128,)),
                      np.swapaxes(a[..., 1, :, :], -1, -2).reshape(a.shape[:-3] + (128,)),
                      a[..., 2, :, :].reshape(a.shape[:-3] + (128,))], axis=-2)
    elif name == "L3_ffn_W":
        a = a.transpose(2, 0, 1)
    elif name in ("L0_ffn_b1", "L2_ffn_b1"):
        a = a.reshape(a.shape[0], -1, 128).transpose(0, 2, 1)
    elif name == "L3_attn_mlp_b1":
        a = a.reshape(-1, 128).T
    elif a.ndim == 0:
        a = a.reshape(1)
    return np.ascontiguousarray(a)


def kernel(**inputs):
    import numpy as _np
    import concourse.bacc as _bacc
    from concourse import mybir as _mybir
    from concourse.bass_utils import run_bass_kernel_spmd as _run

    nc = _bacc.Bacc("TRN2", target_bir_lowering=False, num_devices=1)
    arrays, dram = {}, {}
    for name in inputs:
        a = laid_out(name, _np.asarray(inputs[name]))
        arrays[f"in_{name}"] = a
        dram[name] = nc.dram_tensor(f"in_{name}", a.shape, _mybir.dt.from_np(a.dtype), kind="ExternalInput").ap()
    for name, a in tables().items():
        arrays[f"tab_{name}"] = a
        dram[name] = nc.dram_tensor(f"tab_{name}", a.shape, _mybir.dt.from_np(a.dtype), kind="ExternalInput").ap()
    out = nc.dram_tensor("out_x", (B, S, D), _mybir.dt.float32, kind="ExternalOutput").ap()
    program(nc, dram, out)
    return _run(nc, [arrays], core_ids=[0]).results[0]["out_x"]
```

```python
import numpy as np
import concourse.bass as bass
from concourse import mybir
from contextlib import ExitStack

FP = mybir.dt.float32
BF = mybir.dt.bfloat16
I32 = mybir.dt.int32
ACT = mybir.ActivationFunctionType
ALU = mybir.AluOpType
AX = mybir.AxisListType

B, S, D = 8, 512, 128
P = 128
NT = B * S // P
TC = S // P
LN_EPS = 1e-5


class Net:

    def __init__(self, nc, ctx):
        self.nc = nc
        sb = lambda n, s, d=FP: ctx.enter_context(nc.sbuf_tensor(n, s, d))
        self.x = sb("x_resid", [P, NT, D])
        self.stat = sb("x_stat", [P, NT, 2])
        self.rstd = sb("x_rstd", [P, NT])
        self.ident = sb("ident", [P, P])
        self.ones = sb("ones_sq", [P, P])
        self.xT = sb("x_normT", [P, B * S])
        self.epst = sb("eps_col", [P, 2])


class Scope:

    used = []

    def __init__(self, nc, ctx, tag):
        self.nc, self.ctx, self.tag = nc, ctx, tag

    def sb(self, name, shape, dt=FP):
        return self.ctx.enter_context(self.nc.sbuf_tensor(f"{self.tag}_{name}", shape, dt))

    def ps(self, name, shape=(P, 512), dt=FP):
        return self.ctx.enter_context(self.nc.psum_tensor(f"{self.tag}_{name}", list(shape), dt))

    def sem(self, name):
        handle = self.nc.alloc_semaphore(name=f"{self.tag}_{name}")
        Scope.used.append(handle)
        return handle


def renew_semaphores(nc):
    nc.clear_and_free_semaphores(Scope.used)
    nc.all_engine_barrier()
    Scope.used = []


def row(v):
    return v.rearrange("(a n) -> a n", a=1)


def col(v):
    return v.rearrange("(n a) -> n a", a=1)


def token_stats(nc, v, net, bst, tile, k):
    nc.vector.bn_stats(bst[:, k, :], net.x[:, tile, :])


def load_and_measure(nc, net, x_dram):
    with ExitStack() as ctx:
        p = Scope(nc, ctx, "in")
        loaded = [p.sem(f"loaded{i}") for i in range(4)]
        zeroed, ready = p.sem("ident_zeroed"), p.sem("ident_ready")
        bst = p.sb("bst", [P, 8, 6])
        block = ctx.enter_context(nc.Block())
        xv = x_dram.rearrange("b (t p) d -> p (b t) d", p=P)

        @block.sync
        def _(sp):
            for q in range(4):
                sp.dma_start(net.x[:, 8 * q:8 * q + 8, :], xv[:, 8 * q:8 * q + 8, :]).then_inc(loaded[q], 16)

        @block.gpsimd
        def _(pool):
            nc.gpsimd.memset(net.ident[:, :], 0.0).then_inc(zeroed, 1)
            nc.gpsimd.memset(net.ones[:, :], 1.0)
            nc.gpsimd.memset(net.epst[:, 0:1], LN_EPS)
            nc.gpsimd.memset(net.epst[:, 1:2], 1e-6)
            pool.wait_ge(zeroed, 1)
            nc.gpsimd.affine_select(out=net.ident[:, :], in_=net.ident[:, :], compare_op=ALU.not_equal, fill=1.0,
                                    base=0, pattern=[[-1, P]], channel_multiplier=1).then_inc(ready, 1)

        @block.vector
        def _(v):
            for q in range(4):
                v.wait_ge(loaded[q], 16)
                for k in range(8):
                    nc.vector.bn_stats(bst[:, k, :], net.x[:, 8 * q + k, :])
                v.drain()
                for k in range(8):
                    nc.vector.bn_aggr(net.stat[:, 8 * q + k, :], bst[:, k, :])
                v.drain()


def normalise(nc, net, tag, src=None, g=None, b=None):
    with ExitStack() as ctx:
        p = Scope(nc, ctx, tag + "_ln")
        xn = [p.sb(f"xn{i}", [P, TC, D]) for i in range(2)]
        gcol, bcol = p.sb("gcol", [P, 1]), p.sb("bcol", [P, 1])
        w_loaded = p.sem("w_loaded")
        std = p.sb("std", [P, NT])
        tps = [p.ps(f"tps{i}") for i in range(2)]
        std_done, xn_done = p.sem("std_done"), p.sem("xn_done")
        t_done, t_free = p.sem("t_done"), p.sem("t_free")
        block = ctx.enter_context(nc.Block())
        src = net.x if src is None else src

        @block.sync
        def _(sp):
            if g is not None:
                sp.dma_start(gcol[:, :], col(g)).then_inc(w_loaded, 16)
                sp.dma_start(bcol[:, :], col(b)).then_inc(w_loaded, 16)

        @block.vector
        def _(v):
            v.wait_ge(std_done, 1)
            nc.vector.reciprocal(net.rstd[:, :], std[:, :])
            v.drain()
            with v.Fori(0, B // 2) as i:
                for par in range(2):
                    c = 2 * i + par
                    v.wait_ge(t_done, c + 1)
                    for k in range(TC):
                        last = nc.vector.tensor_scalar(xn[par][:, k, :], src[:, 4 * c + k, :], net.stat[:, 4 * c + k, 0:1],
                                                       net.rstd[:, bass.ds(4 * c + k, 1)], ALU.subtract, ALU.mult)
                    last.then_inc(xn_done, 1)

        @block.tensor
        def _(pe):
            pe.sem_inc(t_done, 2)
            with pe.Fori(0, B // 2) as i:
                for par in range(2):
                    c = 2 * i + par
                    pe.wait_ge(xn_done, c + 1)
                    pe.wait_ge(t_free, c + 1)
                    for k in range(TC):
                        last = nc.tensor.transpose(tps[par][:, k * P:(k + 1) * P], xn[par][:, k, :], net.ident[:, :])
                    last.then_inc(t_done, 1)

        @block.scalar
        def _(act):
            nc.scalar.activation(std[:, :], net.stat[:, :, 1], ACT.Sqrt, bias=net.epst[:, 0:1]).then_inc(std_done, 1)
            act.sem_inc(t_free, 2)
            if g is not None:
                act.wait_ge(w_loaded, 32)
            with act.Fori(0, B // 2) as i:
                for par in range(2):
                    c = 2 * i + par
                    act.wait_ge(t_done, c + 3)
                    sc = {} if g is None else dict(scale=gcol[:, :], bias=bcol[:, :])
                    nc.scalar.activation(net.xT[:, bass.ts(c, S)], tps[par][:, :],
                                         ACT.Identity, **sc).then_inc(t_free, 1)


def store(nc, net, out):
    with ExitStack() as ctx:
        p = Scope(nc, ctx, "out")
        stored = p.sem("stored")
        block = ctx.enter_context(nc.Block())
        ov = out.rearrange("b (t p) d -> p (b t) d", p=P)

        @block.sync
        def _(sp):
            for q in range(4):
                sp.dma_start(ov[:, 8 * q:8 * q + 8, :], net.x[:, 8 * q:8 * q + 8, :]).then_inc(stored, 16)
            sp.wait_ge(stored, 64)


def one_chunk_ahead(eng, front, back):
    front(0, 0)
    with eng.Fori(0, B // 2 - 1) as i:
        front(2 * i + 1, 1)
        back(2 * i, 0)
        front(2 * i + 2, 0)
        back(2 * i + 1, 1)
    front(B - 1, 1)
    back(B - 2, 0)
    back(B - 1, 1)


def expert_pairs(eng, n):
    if n == 1:
        yield 0, 0
        return
    with eng.Fori(0, n // 2) as j:
        for ep in range(2):
            yield j, ep


def experts(nc, net, tag, n, nf, func, gate, w1, w2, b1=None, w3=None, nb=1):
    glu = w3 is not None
    with ExitStack() as ctx:
        p = Scope(nc, ctx, tag)
        w1t = [p.sb(f"w1_{i}", [P, nf * P]) for i in range(2)]
        w3t = [p.sb(f"w3_{i}", [P, P]) for i in range(2)] if glu else None
        w2t = [p.sb(f"w2_{i}", [P, nf, nb * P]) for i in range(2)]
        b1t = [p.sb(f"b1_{i}", [P, nf]) for i in range(2)]
        h = [p.sb(f"h{i}", [P, nf, S]) for i in range(2)]
        act_h = [p.sb(f"act{i}", [P, S]) for i in range(2)] if glu else None
        nh = 4 if nf == 4 else 2
        hps = [p.ps(f"hps{i}") for i in range(nh)]
        gps = [p.ps(f"gps{i}") for i in range(2)] if glu else None
        yps = [p.ps(f"yps{i}", [P, TC, nb * P]) for i in range(2)]
        loaded = [p.sem(f"loaded{i}") for i in range(2)]
        zeroed = p.sem("zeroed")
        h_done = p.sem("h_done")
        act_done = p.sem("act_done")
        glu_done = p.sem("glu_done")
        y_done = p.sem("y_done")
        y_used = p.sem("y_used")
        n_load = len(w1(0)) + len(w2(0)) + (len(w3(0)) if glu else 0) + (1 if b1 else 0)
        H0, Y0, U0 = nh, 2, 2
        block = ctx.enter_context(nc.Block())

        @block.sync
        def _(sp):
            def load(e, par):
                for dst, src in w1(e):
                    sp.dma_start(dst(w1t[par]), src).then_inc(loaded[par], 16)
                for dst, src in w3(e) if glu else ():
                    sp.dma_start(dst(w3t[par]), src).then_inc(loaded[par], 16)
                for dst, src in w2(e):
                    sp.dma_start(dst(w2t[par]), src).then_inc(loaded[par], 16)
                if b1:
                    sp.dma_start(b1t[par][:, :], b1(e)).then_inc(loaded[par], 16)
            sp.wait_ge(zeroed, 1)
            load(0, 0)
            if n > 1:
                load(1, 1)
            if n > 2:
                with sp.Fori(1, n // 2) as j:
                    for par in range(2):
                        sp.wait_ge(y_done, Y0 + 8 * (2 * j + par) - 8)
                        load(2 * j + par, par)

        @block.gpsimd
        def _(pool):
            for i in range(2):
                last = nc.gpsimd.memset(w2t[i][:, :, :], 0.0)
            last.then_inc(zeroed, 1)

        @block.tensor
        def _(pe):
            pe.sem_inc(y_done, Y0)
            for j, ep in expert_pairs(pe, n):
                    s0 = 8 * (2 * j + ep)
                    pe.wait_ge(loaded[ep], 16 * n_load * (j + 1))

                    def front(c, par):
                        for f in range(nf):
                            bank = f if nf == 4 else par
                            pe.wait_ge(act_done, (s0 + c) * nf + f + 1)
                            if glu:
                                pe.wait_ge(glu_done, s0 + c + 1)
                            last = nc.tensor.matmul(hps[bank][:, :], w1t[ep][:, f * P:(f + 1) * P],
                                                    net.xT[:, bass.ts(c, S)], start=True, stop=True)
                            if glu:
                                last = nc.tensor.matmul(gps[par][:, :], w3t[ep][:, :],
                                                        net.xT[:, bass.ts(c, S)], start=True, stop=True)
                            last.then_inc(h_done, 1)

                    def back(c, par):
                        if glu:
                            pe.wait_ge(glu_done, 2 + s0 + c + 1)
                        else:
                            pe.wait_ge(act_done, H0 + (s0 + c + 1) * nf)
                        pe.wait_ge(y_used, s0 + c + 1)
                        for k in range(TC):
                            for f in range(nf):
                                last = nc.tensor.matmul(yps[par][:, k, :], h[par][:, f, k * P:(k + 1) * P],
                                                        w2t[ep][:, f, :], start=(f == 0), stop=(f == nf - 1))
                        last.then_inc(y_done, 1)

                    one_chunk_ahead(pe, front, back)

        @block.scalar
        def _(act):
            act.sem_inc(act_done, H0)
            for j, ep in expert_pairs(act, n):
                    act.wait_ge(loaded[ep], 16 * n_load * (j + 1))
                    with act.Fori(0, B // 2) as i:
                        for par in range(2):
                            s = 8 * (2 * j + ep) + 2 * i + par
                            act.wait_ge(y_done, s + 1)
                            for f in range(nf):
                                act.wait_ge(h_done, s * nf + f + 1)
                                bank = f if nf == 4 else par
                                o = act_h[par][:, :] if glu else h[par][:, f, :]
                                bias = dict(bias=b1t[ep][:, f:f + 1]) if b1 else {}
                                nc.scalar.activation(o, hps[bank][:, :], func, **bias).then_inc(act_done, 1)

        @block.vector
        def _(v):
            v.sem_inc(y_used, U0)
            if glu:
                v.sem_inc(glu_done, 2)
            for j, ep in expert_pairs(v, n):
                    e = 2 * j + ep

                    def product(c, par):
                        if glu:
                            v.wait_ge(act_done, H0 + 8 * e + c + 1)
                            nc.vector.tensor_tensor(h[par][:, 0, :], act_h[par][:, :], gps[par][:, :],
                                                    ALU.mult).then_inc(glu_done, 1)

                    def gather(c, par):
                        v.wait_ge(y_done, Y0 + 8 * e + c + 1)
                        for q in range(nb):
                            for k in range(TC):
                                xt = net.x[:, 4 * c + k, :]
                                last = nc.vector.scalar_tensor_tensor(
                                    xt, yps[par][:, k, q * P:(q + 1) * P], gate(4 * c + k, e, q), xt,
                                    ALU.mult, ALU.add)
                            if q == nb - 1:
                                last.then_inc(y_used, 1)
                            v.drain()

                    if glu:
                        one_chunk_ahead(v, product, gather)
                    else:
                        with v.Fori(0, B // 2) as i:
                            for par in range(2):
                                gather(2 * i + par, par)


def gated_bias(nc, net, tag, gate, b2):
    with ExitStack() as ctx:
        p = Scope(nc, ctx, tag + "_gb")
        gT = [p.sb(f"gT{i}", [32, P]) for i in range(2)]
        b2d = p.sb("b2d", [32, TC, D])
        tps = [p.ps(f"tps{i}") for i in range(2)]
        bps = [p.ps(f"bps{i}") for i in range(2)]
        loaded, zeroed, t_done, gT_done = p.sem("loaded"), p.sem("zeroed"), p.sem("t_done"), p.sem("gT_done")
        b_done, b_used = p.sem("b_done"), p.sem("b_used")
        block = ctx.enter_context(nc.Block())

        @block.gpsimd
        def _(pool):
            nc.gpsimd.memset(b2d[:, :, :], 0.0).then_inc(zeroed, 1)

        @block.sync
        def _(sp):
            sp.wait_ge(zeroed, 1)
            for k in range(TC):
                sp.dma_start(b2d[8 * k:8 * k + 8, k, :], b2).then_inc(loaded, 16)

        @block.tensor
        def _(pe):
            pe.wait_ge(loaded, 16 * TC)
            for c in range(B):
                if c >= 2:
                    pe.wait_ge(gT_done, c - 1)
                nc.tensor.transpose(tps[c % 2][0:32, 0:P], gate[:, 4 * c:4 * c + 4, :].rearrange("p a b -> p (a b)"),
                                    net.ident[:, :]).then_inc(t_done, 1)
                pe.wait_ge(gT_done, c + 1)
                if c >= 2:
                    pe.wait_ge(b_used, c - 1)
                nc.tensor.matmul(bps[c % 2][:, :], gT[c % 2][:, :], b2d[:, :, :].rearrange("p a b -> p (a b)"),
                                 start=True, stop=True).then_inc(b_done, 1)

        @block.scalar
        def _(act):
            for c in range(B):
                act.wait_ge(t_done, c + 1)
                if c >= 2:
                    act.wait_ge(b_done, c - 1)
                nc.scalar.activation(gT[c % 2][:, :], tps[c % 2][0:32, 0:P], ACT.Copy).then_inc(gT_done, 1)

        @block.vector
        def _(v):
            for c in range(B):
                v.wait_ge(b_done, c + 1)
                xt = net.x[:, 4 * c:4 * c + 4, :].rearrange("p a b -> p (a b)")
                nc.vector.tensor_tensor(xt, xt, bps[c % 2][:, :], ALU.add).then_inc(b_used, 1)


def measure(nc, net, tag):
    with ExitStack() as ctx:
        p = Scope(nc, ctx, tag + "_st")
        bst, agg = p.sb("bst", [P, 8, 6]), p.sb("agg", [P, 8, 2])
        block = ctx.enter_context(nc.Block())

        @block.vector
        def _(v):
            with v.Fori(0, NT // 8) as i:
                for k in range(8):
                    nc.vector.bn_stats(bst[:, k, :], net.x[:, 8 * i + k, :])
                v.drain()
                for k in range(8):
                    nc.vector.bn_aggr(agg[:, k, :], bst[:, k, :])
                v.drain()
                nc.vector.tensor_copy(net.stat[:, bass.ts(i, 8), :], agg[:, :, :])
                v.drain()


def router_logits(nc, net, tag, w, E, lg, bias=None):
    with ExitStack() as ctx:
        p = Scope(nc, ctx, tag + "_rl")
        lT = [p.sb(f"lT{i}", [E, S]) for i in range(2)]
        wt = p.sb("w", [P, E])
        bt = p.sb("b", [E, 1])
        lps = [p.ps(f"lps{i}") for i in range(2)]
        tps = [p.ps(f"tps{i}", [P, TC, E]) for i in range(2)]
        parts = w if isinstance(w, tuple) else (w,)
        n_loaded = 16 * (len(parts) + (bias is not None))
        loaded, l_done, lT_done, t_done, lg_done = (p.sem(n) for n in ("loaded", "l_done", "lT_done", "t_done", "lg_done"))
        block = ctx.enter_context(nc.Block())

        @block.sync
        def _(sp):
            for i, part in enumerate(parts):
                n = E // len(parts)
                sp.dma_start(wt[:, i * n:(i + 1) * n], part).then_inc(loaded, 16)
            if bias is not None:
                sp.dma_start(bt[:, :], col(bias)).then_inc(loaded, 16)

        @block.tensor
        def _(pe):
            pe.wait_ge(loaded, n_loaded)

            def logits(c, par):
                if isinstance(c, int) and c < 2:
                    pass
                else:
                    pe.wait_ge(lT_done, c - 1)
                nc.tensor.matmul(lps[par][0:E, :], wt[:, :], net.xT[:, bass.ts(c, S)],
                                 start=True, stop=True).then_inc(l_done, 1)

            def turn(c, par):
                pe.wait_ge(lT_done, c + 1)
                if not (isinstance(c, int) and c < 2):
                    pe.wait_ge(lg_done, c - 1)
                for k in range(TC):
                    last = nc.tensor.transpose(tps[par][:, k, :], lT[par][:, k * P:(k + 1) * P], net.ident[0:E, 0:E])
                last.then_inc(t_done, 1)

            for c in range(2):
                logits(c, c)
            for c in range(B):
                turn(c, c % 2)
                if c + 2 < B:
                    logits(c + 2, c % 2)

        @block.scalar
        def _(act):
            act.wait_ge(loaded, n_loaded)
            for c in range(B):
                act.wait_ge(l_done, c + 1)
                if c >= 2:
                    act.wait_ge(t_done, c - 1)
                kw = {} if bias is None else dict(bias=bt[:, :])
                nc.scalar.activation(lT[c % 2][:, :], lps[c % 2][0:E, :], ACT.Identity, **kw).then_inc(lT_done, 1)

        @block.vector
        def _(v):
            for c in range(B):
                v.wait_ge(t_done, c + 1)
                nc.vector.tensor_copy(lg[:, 4 * c:4 * c + 4, :], tps[c % 2][:, :, :]).then_inc(lg_done, 1)


def bcast(ap, n):
    return ap.unsqueeze(len(ap.shape)).to_broadcast(list(ap.shape) + [n])


def first_best(nc, v, lg, m, eq, idx, onehot, iota, E):
    nc.vector.tensor_reduce(m[:, :], lg[:, :, :], AX.X, ALU.max)
    v.drain()
    nc.vector.tensor_tensor(eq[:, :, :], lg[:, :, :], bcast(m[:, :], E), ALU.is_equal)
    v.drain()
    nc.vector.scalar_tensor_tensor(eq[:, :, :], eq[:, :, :], float(-E), iota[:, :, :], ALU.mult, ALU.add)
    v.drain()
    nc.vector.tensor_reduce(idx[:, :], eq[:, :, :], AX.X, ALU.min)
    v.drain()
    nc.vector.tensor_tensor(onehot[:, :, :], eq[:, :, :], bcast(idx[:, :], E), ALU.is_equal)
    v.drain()


class Router:

    def __init__(self, nc, ctx, tag, E):
        p = Scope(nc, ctx, tag)
        self.E = E
        self.lg, self.eq, self.oh = p.sb("lg", [P, NT, E]), p.sb("eq", [P, NT, E]), p.sb("onehot", [P, NT, E])
        self.gate, self.iota = p.sb("gate", [P, NT, E]), p.sb("iota", [P, NT, E])
        self.m, self.idx, self.prob = p.sb("m", [P, NT]), p.sb("idx", [P, NT]), p.sb("prob", [P, NT])


def top1_prob(nc, r, tag):
    with ExitStack() as ctx:
        p = Scope(nc, ctx, tag + "_t1")
        iota_done, shifted, exped = p.sem("iota_done"), p.sem("shifted"), p.sem("exped")
        sh = p.sb("sh", [P, NT, r.E])
        block = ctx.enter_context(nc.Block())

        @block.gpsimd
        def _(pool):
            nc.gpsimd.iota(r.iota[:, :, :], pattern=[[0, NT], [1, r.E]], base=0, channel_multiplier=0,
                           allow_small_or_imprecise_dtypes=True).then_inc(iota_done, 1)

        @block.scalar
        def _(act):
            act.wait_ge(shifted, 1)
            nc.scalar.activation(sh[:, :, :], sh[:, :, :], ACT.Exp).then_inc(exped, 1)

        @block.vector
        def _(v):
            v.wait_ge(iota_done, 1)
            first_best(nc, v, r.lg, r.m, r.eq, r.idx, r.oh, r.iota, r.E)
            nc.vector.tensor_tensor(sh[:, :, :], r.lg[:, :, :], bcast(r.m[:, :], r.E), ALU.subtract).then_inc(shifted, 1)
            v.wait_ge(exped, 1)
            nc.vector.tensor_reduce(r.idx[:, :], sh[:, :, :], AX.X, ALU.add)
            v.drain()
            nc.vector.reciprocal(r.prob[:, :], r.idx[:, :])


def over_tiles(v, n):
    return v.unsqueeze(1).to_broadcast([v.shape[0], n, v.shape[1]])


def prefix_steps(nc, p, E):
    tri = p.sb("tri", [P, P])
    tot, scan, one = p.sb("tot", [P, NT, E]), p.sb("scan", [P, NT, E]), p.sb("one", [P, NT])
    wps, tps = p.ps("wps", [P, NT, E]), p.ps("tps", [P, NT, E])
    tri_zeroed, tri_ready = p.sem("tri_zeroed"), p.sem("tri_ready")
    mask_ready, counted = p.sem("mask_ready"), p.sem("counted")

    def on_pool(pool):
        nc.gpsimd.memset(tri[:, :], 1.0)
        nc.gpsimd.memset(one[:, :], 1.0).then_inc(tri_zeroed, 1)
        pool.wait_ge(tri_zeroed, 1)
        nc.gpsimd.affine_select(out=tri[:, :], in_=tri[:, :], compare_op=ALU.is_ge, fill=0.0,
                                base=-1, pattern=[[1, P]], channel_multiplier=-1).then_inc(tri_ready, 1)

    def on_tensor(pe, net, mask):
        pe.wait_ge(tri_ready, 1)
        pe.wait_ge(mask_ready, 1)
        flat = mask.rearrange("p t e -> p (t e)")
        nc.tensor.matmul(wps[:, :, :].rearrange("p t e -> p (t e)"), tri[:, :], flat, start=True, stop=True)
        nc.tensor.matmul(tps[:, :, :].rearrange("p t e -> p (t e)"), net.ones[:, :], flat,
                         start=True, stop=True).then_inc(counted, 1)

    def on_vector(v, loc):
        v.drain()
        v.sem_inc(mask_ready, 1)
        v.wait_ge(tri_ready, 1)
        v.wait_ge(counted, 1)
        nc.vector.tensor_copy(tot[:, :, :], tps[:, :, :])
        v.drain()
        for e in range(E):
            nc.vector.tensor_tensor_scan(scan[:, :, e], one[:, :], tot[:, :, e], 0.0, ALU.mult, ALU.add)
        v.drain()
        nc.vector.tensor_tensor(scan[:, :, :], scan[:, :, :], tot[:, :, :], ALU.subtract)
        v.drain()
        nc.vector.tensor_tensor(loc, scan[:, :, :], wps[:, :, :], ALU.add)
        v.drain()

    return on_pool, on_tensor, on_vector


def capacity_by_probability(nc, net, r, cap, tag):
    E = r.E
    steps = 28
    with ExitStack() as ctx:
        p = Scope(nc, ctx, tag + "_cap")
        key, cmp = p.sb("key", [P, NT, E]), p.sb("cmp", [P, NT, E])
        gt, loc = p.sb("gt", [P, NT, E]), p.sb("loc", [P, NT, E])
        t, cand, part, take = (p.sb(n, [P, E]) for n in ("t", "cand", "part", "take"))
        step, drop = p.sb("step", [P, 1]), p.sb("drop", [P, NT])
        cps = p.ps("cps", [P, E])
        part_done, total_done = p.sem("part_done"), p.sem("total_done")
        on_pool, on_tensor, on_vector = prefix_steps(nc, p, E)
        block = ctx.enter_context(nc.Block())

        @block.gpsimd
        def _(pool):
            on_pool(pool)

        @block.tensor
        def _(pe):
            with pe.Fori(0, steps + 1) as i:
                pe.wait_ge(part_done, i + 1)
                nc.tensor.matmul(cps[:, :], net.ones[:, :], part[:, :], start=True, stop=True).then_inc(total_done, 1)
            on_tensor(pe, net, r.eq[:, :, :])

        @block.vector
        def _(v):
            def count(op, thr):
                nc.vector.tensor_tensor(cmp[:, :, :], key[:, :, :], over_tiles(thr, NT), op)
                v.drain()
                nc.vector.tensor_reduce(part[:, :], cmp[:, :, :].rearrange("p t e -> p e t"),
                                        AX.X, ALU.add).then_inc(part_done, 1)

            nc.vector.memset(t[:, :], 0.0)
            nc.vector.memset(step[:, :], 1.0)
            nc.vector.tensor_tensor(key[:, :, :], r.oh[:, :, :], bcast(r.prob[:, :], E), ALU.mult)
            v.drain()
            with v.Fori(0, steps) as i:
                nc.vector.tensor_scalar(cand[:, :], t[:, :], step[:, :], None, ALU.add)
                v.drain()
                count(ALU.is_ge, cand[:, :])
                v.wait_ge(total_done, i + 1)
                nc.vector.tensor_scalar(take[:, :], cps[:, :], float(cap), None, ALU.is_ge)
                v.drain()
                nc.vector.tensor_tensor(cand[:, :], cand[:, :], t[:, :], ALU.subtract)
                nc.vector.tensor_scalar(step[:, :], step[:, :], 0.5, None, ALU.mult)
                v.drain()
                nc.vector.tensor_tensor(take[:, :], take[:, :], cand[:, :], ALU.mult)
                v.drain()
                nc.vector.tensor_tensor(t[:, :], t[:, :], take[:, :], ALU.add)
                v.drain()
            count(ALU.is_gt, t[:, :])
            v.wait_ge(total_done, steps + 1)
            nc.vector.tensor_copy(gt[:, :, :], cmp[:, :, :])
            nc.vector.tensor_tensor(r.eq[:, :, :], key[:, :, :], over_tiles(t[:, :], NT), ALU.is_equal)
            nc.vector.tensor_scalar(take[:, :], cps[:, :], -1.0, float(cap), ALU.mult, ALU.add)
            on_vector(v, loc[:, :, :])
            nc.vector.tensor_tensor(cmp[:, :, :], loc[:, :, :], over_tiles(take[:, :], NT), ALU.is_lt)
            v.drain()
            nc.vector.tensor_tensor(cmp[:, :, :], cmp[:, :, :], r.eq[:, :, :], ALU.mult)
            v.drain()
            nc.vector.tensor_tensor(cmp[:, :, :], cmp[:, :, :], gt[:, :, :], ALU.add)
            v.drain()
            nc.vector.tensor_tensor(r.gate[:, :, :], cmp[:, :, :], r.oh[:, :, :], ALU.mult)
            v.drain()
            nc.vector.tensor_reduce(drop[:, :], r.gate[:, :, :], AX.X, ALU.add)
            v.drain()
            nc.vector.tensor_scalar(drop[:, :], drop[:, :], -1.0, 1.0, ALU.mult, ALU.add)
            v.drain()
            nc.vector.tensor_tensor(r.gate[:, :, 0], r.gate[:, :, 0], drop[:, :], ALU.add)


def capacity_by_order(nc, net, r, cap, tag):
    E = r.E
    with ExitStack() as ctx:
        p = Scope(nc, ctx, tag + "_cap")
        loc = p.sb("loc", [P, NT, E])
        on_pool, on_tensor, on_vector = prefix_steps(nc, p, E)
        block = ctx.enter_context(nc.Block())

        @block.gpsimd
        def _(pool):
            on_pool(pool)

        @block.tensor
        def _(pe):
            on_tensor(pe, net, r.oh[:, :, :])

        @block.vector
        def _(v):
            on_vector(v, loc[:, :, :])
            nc.vector.tensor_scalar(loc[:, :, :], loc[:, :, :], float(cap), None, ALU.is_lt)
            v.drain()
            nc.vector.tensor_tensor(loc[:, :, :], loc[:, :, :], r.oh[:, :, :], ALU.mult)
            v.drain()
            nc.vector.tensor_tensor(r.gate[:, :, :], loc[:, :, :], bcast(r.prob[:, :], E), ALU.mult)


def split3(nc, eng, e, src, dst, rest, drain):
    e.tensor_copy(dst[0], src)
    drain()
    e.tensor_tensor(rest, src, dst[0], ALU.subtract)
    drain()
    e.tensor_copy(dst[1], rest)
    drain()
    e.tensor_tensor(rest, rest, dst[1], ALU.subtract)
    drain()
    return e.tensor_copy(dst[2], rest)


Q_PARTS = (0, 0, 0, 1, 1, 2)
K_PARTS = ((0, 3), (3, 2), (5, 1))


def relative_attention(nc, net, d):
    a = lambda n: d[f"L0_attn_{n}"]
    HD, NH = a("w_rel").shape
    qd, kd = (nc.dram_tensor(n, (3, P, B * S), BF, kind="Internal").ap() for n in ("q_parts", "k_parts"))
    ad = nc.dram_tensor("rel_q_parts", (3, P, S), BF, kind="Internal").ap()
    td = nc.dram_tensor("rel_k_parts", (3, HD, S), BF, kind="Internal").ap()
    with ExitStack() as ctx:
        operands = Scope(nc, ctx, "a0o")
        Q, K = operands.sb("Q", [P, 2 * NH, S], BF), operands.sb("K", [P, 2 * NH, S], BF)
        V = operands.sb("V", [P, NT, NH, HD + 1])
        with ExitStack() as part:
            h = Scope(nc, part, "a0h").sb("h", [P, NT, D])
            token_rstd(nc, net, "a0")
            prepare(nc, net, d, a, HD, NH, h, K, 2 * len(Q_PARTS) * HD, ad, td)
            normalise(nc, net, "a0", src=h, g=a("ln_g"), b=a("ln_b"))
        project_parts(nc, net, a, HD, NH, V, qd, kd, Q, K, ad, td)
        heads(nc, net, a, HD, NH, V, qd, kd, Q, K)
    measure(nc, net, "a0")


def prepare(nc, net, d, a, HD, NH, h, K, first_one, ad, td):
    with ExitStack() as ctx:
        p = Scope(nc, ctx, "a0n")
        bst = p.sb("bst", [P, NT, 6])
        t, m1, m2 = p.sb("t", [HD, S]), p.sb("m1", [HD, HD]), p.sb("m2", [HD, HD])
        wr, ws = p.sb("wr", [HD, NH]), p.sb("ws", [HD, NH])
        L, L2 = p.sb("L", [HD, HD, NH]), p.sb("L2", [HD, HD, NH])
        qf, qp, kp = p.sb("qf", [P, S]), p.sb("qp", [P, 3, S], BF), p.sb("kp", [HD, 3, S], BF)
        rest = p.sb("rest", [P, S])
        ps = p.ps("ps")
        loaded, L_done, q_done, split_done, stored = (p.sem(n) for n in ("loaded", "L_done", "q_done", "split_done", "stored"))
        block = ctx.enter_context(nc.Block())

        @block.sync
        def _(sp):
            for dst, src in ((t, d["rel_t"]), (m1, d["rel_m1"]), (m2, d["rel_m2"]), (wr, a("w_rel"))):
                sp.dma_start(dst[:, :], src).then_inc(loaded, 16)
            for r in range(HD):
                sp.dma_start(ws[r:r + 1, :], a("w_rel")[r ^ 1:(r ^ 1) + 1, :]).then_inc(loaded, 16)
            sp.wait_ge(split_done, 1)
            sp.dma_start(td.rearrange("s r n -> r s n"), kp[:, :, :]).then_inc(stored, 16)
            sp.wait_ge(split_done, 2)
            sp.dma_start(ad.rearrange("s p n -> p s n"), qp[:, :, :]).then_inc(stored, 16)
            sp.wait_ge(stored, 32)

        @block.gpsimd
        def _(pool):
            nc.gpsimd.memset(K[first_one:P, :, :], 1.0)

        @block.tensor
        def _(pe):
            pe.wait_ge(L_done, 1)
            nc.tensor.matmul(ps[:, :], L[:, :, :].rearrange("a r h -> a (r h)"), t[:, :], start=True, stop=True).then_inc(q_done, 1)

        @block.vector
        def _(v):
            for k in range(NT):
                nc.vector.tensor_scalar(h[:, k, :], net.x[:, k, :], net.stat[:, k, 0:1], net.rstd[:, k:k + 1],
                                        ALU.subtract, ALU.mult)
            v.wait_ge(loaded, 16 * (4 + HD))
            nc.vector.tensor_tensor(L[:, :, :], over_tiles(wr[:, :], HD), bcast(m1[:, :], NH), ALU.mult)
            nc.vector.tensor_tensor(L2[:, :, :], over_tiles(ws[:, :], HD), bcast(m2[:, :], NH), ALU.mult)
            v.drain()
            nc.vector.tensor_tensor(L[:, :, :], L[:, :, :], L2[:, :, :], ALU.add).then_inc(L_done, 1)
            split3(nc, v, nc.vector, t[:, :], [kp[:, s, :] for s in range(3)], rest[0:HD, :], v.drain).then_inc(split_done, 1)
            v.wait_ge(q_done, 1)
            nc.vector.tensor_copy(qf[:, :], ps[:, :])
            v.drain()
            split3(nc, v, nc.vector, qf[:, :], [qp[:, s, :] for s in range(3)], rest[:, :], v.drain).then_inc(split_done, 1)
            for k in range(NT):
                nc.vector.bn_stats(bst[:, k, :], h[:, k, :])
            v.drain()
            for k in range(NT):
                nc.vector.bn_aggr(net.stat[:, k, :], bst[:, k, :])


def project_parts(nc, net, a, HD, NH, V, qd, kd, Q, K, ad, td):
    with ExitStack() as ctx:
        p = Scope(nc, ctx, "a0p")
        w, bv = p.sb("w", [P, 3, P]), p.sb("bv", [P, P])
        bias, tick = p.sb("bias", [P, 2]), p.sb("tick", [P, 2])
        f = [[p.sb(f"f{t}{i}", [P, S]) for i in range(2)] for t in "qk"]
        parts = [[p.sb(f"parts{t}{i}", [P, 3, S], BF) for i in range(2)] for t in "qk"]
        rest = [p.sb(f"rest{t}", [P, S]) for t in "qk"]
        xc = [p.sb(f"xc{i}", [P, S]) for i in range(2)]
        qkps = [[p.ps(f"ps{t}{i}") for i in range(2)] for t in "qk"]
        vps = [p.ps(f"vps{i}") for i in range(2)]
        loaded, k_split, xc_done, pj_ready, f_done, v_done = (
            p.sem(n) for n in ("loaded", "k_split", "xc_done", "pj_ready", "f_done", "v_done"))
        rel_loaded = p.sem("rel_loaded")
        split_done = [p.sem(f"split_{t}") for t in "qk"]
        stored = [[p.sem(f"stored_{t}{i}") for i in range(2)] for t in "qk"]
        block = ctx.enter_context(nc.Block())
        scale = HD ** -0.5

        @block.sync
        def _(sp):
            sp.dma_start(w[:, :, :], a("w_qkv")).then_inc(loaded, 16)
            for t in range(2):
                sp.dma_start(bias[:, t:t + 1], col(a("b_qkv")[t, :])).then_inc(loaded, 16)
            sp.dma_start(bv[:, :], row(a("b_qkv")[2, :]).to_broadcast([P, P])).then_inc(loaded, 16)
            REL = len(Q_PARTS) * HD
            for par in range(2):
                hh = slice(par * NH, (par + 1) * NH)
                for n, s in enumerate(Q_PARTS):
                    sp.dma_start(Q[REL + n * HD:REL + (n + 1) * HD, hh, :],
                                 ad[s, :, :].rearrange("(r h) n -> r h n", h=NH)).then_inc(rel_loaded, 16)
                for first, s in K_PARTS:
                    src = td[0:s, :, :].rearrange("s r n -> (s r) n")
                    sp.dma_start(K[REL + first * HD:REL + (first + s) * HD, hh, :],
                                 over_tiles(src, NH)).then_inc(rel_loaded, 16)
            for t in range(2):
                for par in range(2):
                    sp.sem_inc(stored[t][par], 16)
            with sp.Fori(0, B // 2) as i:
                for par in range(2):
                    c = 2 * i + par
                    for t, dst in enumerate((qd, kd)):
                        sp.wait_ge(split_done[t], c + 1)
                        sp.dma_start(dst[:, :, bass.ts(c, S)].rearrange("s p n -> p s n"),
                                     parts[t][par][:, :, :]).then_inc(stored[t][par], 16)
            for t in range(2):
                for par in range(2):
                    sp.wait_ge(stored[t][par], 16 + 16 * (B // 2))
            sp.wait_ge(rel_loaded, 32 * (len(Q_PARTS) + len(K_PARTS)))

        @block.tensor
        def _(pe):
            pe.wait_ge(loaded, 64)
            pe.sem_inc(pj_ready, 2)
            with pe.Fori(0, B // 2) as i:
                for par in range(2):
                    c = 2 * i + par
                    pe.wait_ge(f_done, c + 1)
                    for t in range(2):
                        nc.tensor.matmul(qkps[t][par][:, :], w[:, t, :], net.xT[:, bass.ts(c, S)], start=True, stop=True)
                    pe.wait_ge(xc_done, c + 1)
                    pe.wait_ge(v_done, c + 1)
                    for k in range(TC):
                        last = nc.tensor.matmul(vps[par][:, k * P:(k + 1) * P], xc[par][:, k * P:(k + 1) * P], w[:, 2, :],
                                                start=True, stop=True)
                    last.then_inc(pj_ready, 1)

        @block.scalar
        def _(act):
            act.wait_ge(loaded, 64)
            nc.scalar.activation(bias[:, 0:1], bias[:, 0:1], ACT.Copy, scale=scale)
            act.drain()
            act.sem_inc(f_done, 2)
            with act.Fori(0, B // 2) as i:
                for par in range(2):
                    c = 2 * i + par
                    act.wait_ge(pj_ready, c + 1)
                    nc.scalar.activation(xc[par][:, :], net.xT[:, bass.ts(c, S)], ACT.Copy).then_inc(xc_done, 1)
                    act.wait_ge(pj_ready, c + 3)
                    act.wait_ge(v_done, c + 1)
                    act.wait_ge(k_split, c + 1)
                    nc.scalar.activation(f[0][par][:, :], qkps[0][par][:, :], ACT.Identity, bias=bias[:, 0:1], scale=scale)
                    nc.scalar.activation(f[1][par][:, :], qkps[1][par][:, :], ACT.Identity, bias=bias[:, 1:2]).then_inc(f_done, 1)

        @block.vector
        def _(v):
            nc.vector.memset(V[:, :, :, HD:HD + 1], 1.0)
            v.wait_ge(loaded, 64)
            v.sem_inc(v_done, 2)
            with v.Fori(0, B // 2) as i:
                for par in range(2):
                    c = 2 * i + par
                    v.wait_ge(f_done, c + 3)
                    v.wait_ge(stored[0][par], 16 * i + 16)
                    split3(nc, v, nc.vector, f[0][par][:, :], [parts[0][par][:, s, :] for s in range(3)],
                           rest[0][:, :], v.drain).then_inc(split_done[0], 1)
                    for k in range(TC):
                        last = nc.vector.tensor_tensor(V[:, 4 * c + k, :, 0:HD],
                                                       vps[par][:, k * P:(k + 1) * P].rearrange("p (h d) -> p h d", d=HD),
                                                       bv[:, :].rearrange("p (h d) -> p h d", d=HD), ALU.add)
                    last.then_inc(v_done, 1)

        @block.gpsimd
        def _(pool):
            pool.sem_inc(k_split, 2)
            nc.gpsimd.memset(tick[:, :], 1.0)
            pool.drain()
            with pool.Fori(0, B // 2) as i:
                for par in range(2):
                    c = 2 * i + par
                    pool.wait_ge(f_done, c + 3)
                    pool.wait_ge(stored[1][par], 16 * i + 16)
                    nc.gpsimd.tensor_tensor(tick[:, 1:2], tick[:, 0:1], tick[:, 0:1], ALU.mult)
                    split3(nc, pool, nc.gpsimd, f[1][par][:, :], [parts[1][par][:, s, :] for s in range(3)],
                           rest[1][:, :], pool.drain).then_inc(split_done[1], 1)
                    pool.drain()
                    pool.sem_inc(k_split, 1)


def heads(nc, net, a, HD, NH, V, qd, kd, Q, K):
    GH = 4
    NG = NH // GH
    NQ = len(Q_PARTS)
    DYN, MAX = 0, 2 * NQ * HD
    KB = MAX + 3
    NS = TC * GH
    SLOTS = NS + 1
    LQ = 16 * (NQ + 3)
    with ExitStack() as ctx:
        p = Scope(nc, ctx, "a0")
        prob = [p.sb(f"prob{i}", [P, GH, TC, S]) for i in range(2)]
        Vg = [p.sb(f"Vg{i}", [P, TC, GH, 32]) for i in range(2)]
        OT = [p.sb(f"OT{i}", [P, S]) for i in range(2)]
        nm = [p.sb(f"nm{i}", [P, NS]) for i in range(2)]
        mr, ms = [p.sb(f"mr{i}", [NS, P]) for i in range(2)], [p.sb(f"ms{i}", [NS, 3, P], BF) for i in range(2)]
        mrest = p.sb("mrest", [NS, P])
        den, O, OTn = p.sb("den", [P, TC, GH]), p.sb("O", [P, TC, NH * HD]), p.sb("OTn", [P, S])
        wo, bo, one = p.sb("wo", [P, D]), p.sb("bo", [P, D]), p.sb("one", [P, 2])
        aps = [p.ps(f"aps{i}") for i in range(2)]
        sps = [p.ps(f"sps{i}", [P, 2, S]) for i in range(2)]
        ops, mps = p.ps("ops"), p.ps("mps")
        w_loaded, bias_added = p.sem("w_loaded"), p.sem("bias_added")
        qk_loaded = [p.sem(f"qk_loaded{i}") for i in range(2)]
        max_loaded = [p.sem(f"max_loaded{i}") for i in range(2)]
        a_ready = p.sem("a_ready")
        a_used = p.sem("a_used")
        ms_done = p.sem("ms_done")
        s_ready = p.sem("s_ready")
        p_done = p.sem("p_done")
        vg_ready = p.sem("vg_ready")
        av_done = p.sem("av_done")
        ot_copied = p.sem("ot_copied")
        ott_done = p.sem("ott_done")
        o_done = p.sem("o_done")
        on_turned = p.sem("on_turned")
        otn_done = p.sem("otn_done")
        y_done = p.sem("y_done")
        y_added = p.sem("y_added")
        block = ctx.enter_context(nc.Block())

        def wait(eng, sem, n):
            if not isinstance(n, int) or n > 0:
                eng.wait_ge(sem, n)

        def sequences(eng, body):
            body(0)
            with eng.Fori(1, B - 1) as b:
                body(b)
            body(B - 1)

        has = lambda n: not isinstance(n, int) or n >= 0
        more = lambda b: not isinstance(b, int) or b < B - 1
        row0 = lambda b, g: (b % 2) * NH + GH * g

        @block.sync
        def _(sp):
            qv = qd.rearrange("s (r h) n -> s r h n", h=NH)
            kv = kd.rearrange("s (r h) n -> s r h n", h=NH)

            def load(b, g):
                hs = bass.ds(row0(b, g), GH)
                for n, s in enumerate(Q_PARTS):
                    sp.dma_start(Q[DYN + n * HD:DYN + (n + 1) * HD, hs, :],
                                 qv[s, :, GH * g:GH * (g + 1), bass.ts(b, S)]).then_inc(qk_loaded[g % 2], 16)
                for first, s in K_PARTS:
                    sp.dma_start(K[DYN + first * HD:DYN + (first + s) * HD, hs, :],
                                 kv[0:s, :, GH * g:GH * (g + 1), bass.ts(b, S)].rearrange("s r h n -> (s r) h n"))\
                      .then_inc(qk_loaded[g % 2], 16)

            def store_max(b, g):
                sp.wait_ge(ms_done, NG * b + g + 1)
                wait(sp, p_done, 8 * (NG * (b - 2) + g + 1))
                wait(sp, max_loaded[g % 2], 48 * (2 * b + g // 2))
                for s in range(3):
                    sp.dma_start(Q[MAX + s:MAX + s + 1, bass.ds(row0(b, g), GH), :].rearrange("o h (q t) -> o (h q) t", t=P),
                                 ms[g % 2][:, s, :]).then_inc(max_loaded[g % 2], 16)

            def next_loads(b):
                for g in range(NG):
                    if more(b):
                        store_max(b + 1, g)
                    if more(b) and more(b + 1):
                        sp.wait_ge(p_done, 8 * (NG * b + g + 1))
                        sp.wait_ge(qk_loaded[g % 2], LQ * (2 * (b + 2) + g // 2))
                        load(b + 2, g)

            load(0, 0)
            load(0, 1)
            sp.dma_start(wo[:, :], a("w_out")).then_inc(w_loaded, 16)
            sp.dma_start(bo[:, :], row(a("b_out")).to_broadcast([P, D])).then_inc(w_loaded, 16)
            for u in range(2, 2 * NG):
                sp.wait_ge(qk_loaded[u % 2], LQ * (u // 2))
                load(u // NG, u % NG)
            for g in range(NG):
                store_max(0, g)
            next_loads(0)
            with sp.Fori(1, B - 2) as b:
                next_loads(b)
            next_loads(B - 2)

        @block.gpsimd
        def _(pool):
            def split_maxima(b, g):
                m = NG * b + g
                pool.drain()
                pool.wait_ge(a_used, SLOTS * (m + 1))
                wait(pool, max_loaded[g % 2], 48 * (2 * b + g // 2))
                nc.gpsimd.tensor_tensor(one[:, 1:2], one[:, 0:1], one[:, 0:1], ALU.mult)
                split3(nc, pool, nc.gpsimd, mr[g % 2][:, :], [ms[g % 2][:, s, :] for s in range(3)],
                       mrest[:, :], pool.drain).then_inc(ms_done, 1)

            def unit_values(b, g):
                pool.drain()
                wait(pool, av_done, NG * b + g - 1)
                nc.gpsimd.tensor_tensor(one[:, 1:2], one[:, 0:1], one[:, 0:1], ALU.mult)
                for k in range(TC):
                    last = nc.gpsimd.tensor_copy(Vg[g % 2][:, k, :, 0:HD + 1], V[:, 4 * b + k, GH * g:GH * (g + 1), :])
                last.then_inc(vg_ready, 1)

            def body(b):
                for g in range(NG):
                    unit_values(b, g)
                    if more(b):
                        split_maxima(b + 1, g)

            nc.gpsimd.memset(one[:, :], 1.0)
            for i in range(2):
                nc.gpsimd.memset(Vg[i][:, :, :, :], 0.0)
            for g in range(NG):
                split_maxima(0, g)
            pool.wait_ge(w_loaded, 32)
            nc.gpsimd.tensor_tensor(net.x[:, :, :], net.x[:, :, :], over_tiles(bo[:, :], NT), ALU.add).then_inc(bias_added, 1)
            sequences(pool, body)

        @block.tensor
        def _(pe):
            def max_score(b, g, s):
                n = SLOTS * (NG * b + g) + s
                wait(pe, a_used, n - 1)
                j, q = s // TC, s % TC
                head = bass.ds(row0(b, g) + j, 1)
                nc.tensor.matmul(aps[(g + s) % 2][:, :],
                                 Q[0:MAX, head, q * P:(q + 1) * P].rearrange("k a n -> k (a n)"),
                                 K[0:MAX, head, :].rearrange("k a n -> k (a n)"), start=True, stop=True).then_inc(a_ready, 1)

            def turn_maxima(b, g):
                pe.wait_ge(a_used, SLOTS * (NG * b + g) + NS)
                nc.tensor.transpose(aps[(g + NS) % 2][0:NS, 0:P], nm[g % 2][:, :], net.ident[:, :]).then_inc(a_ready, 1)

            def key_scores(b, g, t):
                wait(pe, p_done, 8 * (NG * b + g) + t - 1)
                head = bass.ds(row0(b, g) + t // 2, 1)
                for i in range(2):
                    k = 2 * (t % 2) + i
                    last = nc.tensor.matmul(sps[t % 2][:, i, :],
                                            K[0:KB, head, k * P:(k + 1) * P].rearrange("k a n -> k (a n)"),
                                            Q[0:KB, head, :].rearrange("k a n -> k (a n)"), start=True, stop=True)
                last.then_inc(s_ready, 1)

            def values(u, gp, k):
                if k == 0:
                    pe.wait_ge(p_done, 8 * (u + 1))
                    pe.wait_ge(vg_ready, u + 1)
                    wait(pe, ot_copied, u)
                for j in range(GH):
                    last = nc.tensor.matmul(ops[32 * j:32 * j + 32, :], Vg[gp][:, k, j, :], prob[gp][:, j, k, :],
                                            start=(k == 0), stop=(k == TC - 1))
                if k == TC - 1:
                    last.then_inc(av_done, 1)

            def turn_outputs(u, b, gp):
                pe.wait_ge(ot_copied, u + 1)
                wait(pe, o_done, u)
                wait(pe, y_added, b)
                for q in range(TC):
                    last = nc.tensor.transpose(mps[:, q * P:(q + 1) * P], OT[gp][:, q * P:(q + 1) * P], net.ident[:, :])
                last.then_inc(ott_done, 1)

            def turn_sequence(b):
                pe.wait_ge(o_done, NG * (b + 1))
                for q in range(TC):
                    last = nc.tensor.transpose(mps[:, q * P:(q + 1) * P], O[:, q, :], net.ident[:, :])
                last.then_inc(on_turned, 1)

            def project(b):
                pe.wait_ge(otn_done, b + 1)
                for q in range(TC):
                    last = nc.tensor.matmul(mps[:, q * P:(q + 1) * P], OTn[:, q * P:(q + 1) * P], wo[:, :],
                                            start=True, stop=True)
                last.then_inc(y_done, 1)

            def unit(b, g):
                u = NG * b + g
                if more(b):
                    pe.wait_ge(qk_loaded[g % 2], LQ * (2 * (b + 1) + g // 2 + 1))
                for t in range(8):
                    if more(b):
                        max_score(b + 1, g, 2 * t)
                    if t == 0:
                        pe.wait_ge(max_loaded[g % 2], 48 * (2 * b + g // 2 + 1))
                    key_scores(b, g, t)
                    if more(b):
                        max_score(b + 1, g, 2 * t + 1)
                    if t == 0 and g == 2 and has(b - 1):
                        project(b - 1)
                    if t == 2 and has(u - 2):
                        turn_outputs(u - 2, b if g >= 2 else b - 1, g % 2)
                    if t == 6 and g == 1 and has(b - 1):
                        turn_sequence(b - 1)
                    if t % 2 == 1 and has(u - 1):
                        values(u - 1, (g + 1) % 2, t // 2)
                if more(b):
                    turn_maxima(b + 1, g)

            for g in range(NG):
                pe.wait_ge(qk_loaded[g % 2], LQ * (g // 2 + 1))
                for s in range(NS):
                    max_score(0, g, s)
                turn_maxima(0, g)
            pe.wait_ge(w_loaded, 32)
            sequences(pe, lambda b: [unit(b, g) for g in range(NG)])
            U = NG * B
            turn_outputs(U - 2, B - 1, 0)
            for k in range(TC):
                values(U - 1, 1, k)
            turn_outputs(U - 1, B - 1, 1)
            turn_sequence(B - 1)
            project(B - 1)

        @block.scalar
        def _(act):
            def copy_outputs(u, gp):
                act.wait_ge(av_done, u + 1)
                wait(act, ott_done, u - 1)
                nc.scalar.activation(OT[gp][:, :], ops[:, :], ACT.Copy).then_inc(ot_copied, 1)

            def copy_sequence(b):
                act.wait_ge(on_turned, b + 1)
                wait(act, y_done, b)
                nc.scalar.activation(OTn[:, :], mps[:, :], ACT.Copy).then_inc(otn_done, 1)

            def unit(b, g):
                u = NG * b + g
                wait(act, av_done, u - 1)
                for t in range(8):
                    act.wait_ge(s_ready, 8 * u + t + 1)
                    nc.scalar.activation(prob[g % 2][:, t // 2, 2 * (t % 2):2 * (t % 2) + 2, :].rearrange("p a b -> p (a b)"),
                                         sps[t % 2][:, :, :].rearrange("p a b -> p (a b)"), ACT.Exp).then_inc(p_done, 1)
                if g == 1 and has(b - 1):
                    copy_sequence(b - 1)
                if has(u - 1):
                    copy_outputs(u - 1, (g + 1) % 2)

            sequences(act, lambda b: [unit(b, g) for g in range(NG)])
            copy_outputs(NG * B - 1, 1)
            copy_sequence(B - 1)

        @block.vector
        def _(v):
            def maximum(b, g, s):
                v.wait_ge(a_ready, SLOTS * (NG * b + g) + s + 1)
                nc.vector.tensor_reduce(nm[g % 2][:, s:s + 1], aps[(g + s) % 2][:, :], AX.X, ALU.max, negate=True).then_inc(a_used, 1)

            def take_maxima(b, g):
                m = NG * b + g
                v.wait_ge(a_ready, SLOTS * (m + 1))
                wait(v, ms_done, m - 1)
                nc.vector.tensor_copy(mr[g % 2][:, :], aps[(g + NS) % 2][0:NS, 0:P]).then_inc(a_used, 1)

            def outputs(u, b, g):
                v.drain()
                v.wait_ge(ott_done, u + 1)
                if g == 0:
                    wait(v, on_turned, b)
                m = mps[:, :].rearrange("p (q j e) -> p q j e", q=TC, j=GH)
                nc.vector.reciprocal(den[:, :, :], m[:, :, :, HD])
                v.drain()
                for q in range(TC):
                    last = nc.vector.tensor_tensor(O[:, q, GH * HD * g:GH * HD * (g + 1)].rearrange("p (j e) -> p j e", e=HD),
                                                   m[:, q, :, 0:HD], bcast(den[:, q, :], HD), ALU.mult)
                last.then_inc(o_done, 1)

            def add_output(b):
                v.wait_ge(y_done, b + 1)
                xt = net.x[:, bass.ts(b, 4), :].rearrange("p a b -> p (a b)")
                nc.vector.tensor_tensor(xt, xt, mps[:, :], ALU.add).then_inc(y_added, 1)

            def unit(b, g):
                u = NG * b + g
                for s in range(NS):
                    if more(b):
                        maximum(b + 1, g, s)
                    if s == 1 and g == 2 and has(b - 1):
                        add_output(b - 1)
                    if s == 8 and has(u - 2):
                        outputs(u - 2, b if g >= 2 else b - 1, (g + 2) % NG)
                if more(b):
                    take_maxima(b + 1, g)

            for g in range(NG):
                for s in range(NS):
                    maximum(0, g, s)
                take_maxima(0, g)
            v.wait_ge(bias_added, 1)
            sequences(v, lambda b: [unit(b, g) for g in range(NG)])
            outputs(NG * B - 2, B - 1, NG - 2)
            outputs(NG * B - 1, B - 1, NG - 1)
            add_output(B - 1)


def moe_capacity_relu(nc, net, d):
    E, _, nf = d["L0_ffn_b1"].shape
    cap = -(-(B * S) * 5 // (E * 4))
    with ExitStack() as ctx:
        r = Router(nc, ctx, "m0", E)
        normalise(nc, net, "m0")
        router_logits(nc, net, "m0", d["L0_ffn_router_w"], E, r.lg)
        top1_prob(nc, r, "m0")
        capacity_by_probability(nc, net, r, cap, "m0")
        gated_bias(nc, net, "m0", r.gate, d["L0_ffn_b2"])
        W1 = d["L0_ffn_W1"].rearrange("e d f -> d e f")
        W2 = d["L0_ffn_W2"].rearrange("e (g f) d -> f e g d", f=P)
        b1 = d["L0_ffn_b1"].rearrange("e f g -> f e g")
        experts(nc, net, "m0e", E, nf, ACT.Relu, lambda t, e, k: r.gate[:, t, bass.ds(e, 1)],
                lambda e: [(lambda t: t[:, :], W1[:, bass.ds(e, 1), :].rearrange("d a f -> d (a f)"))],
                lambda e: [(lambda t: t[:, :, :], W2[:, bass.ds(e, 1), :, :].rearrange("f a g d -> f (a g) d"))],
                b1=lambda e: b1[:, bass.ds(e, 1), :].rearrange("f a g -> f (a g)"))
    measure(nc, net, "m0")


def phase_memory(nc, net, d):
    import math
    T1 = d["L1_attn_W_dt1"].shape[1]
    TWO_PI_HI = 6.28125
    TWO_PI_LO = 2 * math.pi - TWO_PI_HI
    ROUND = 1.5 * 2.0 ** 23
    normalise(nc, net, "a1")
    with ExitStack() as ctx:
        p = Scope(nc, ctx, "a1")
        WB, WC, Wo, Dg = (p.sb(n, [P, P]) for n in ("WB", "WC", "Wo", "Dg"))
        W1, W2 = p.sb("W1", [P, T1]), p.sb("W2", [T1, P])
        bB, bC, b2, om0, Dc, b1 = (p.sb(n, [P, 1]) for n in ("bB", "bC", "b2", "om0", "Dc", "b1"))
        half_pi, one, bo = p.sb("half_pi", [P, 1]), p.sb("one", [P, S]), p.sb("bo", [P, D])
        two = lambda n, s=S, q=P: [p.sb(f"{n}{i}", [q, s]) for i in range(2)]
        xc, t1, rz, l, ph, sn, cn, r = (two("xc"), two("t1", S, T1), two("rz"), two("l"), two("ph"), two("sn"),
                                        two("cn"), two("r"))
        az, om, k, content, cc, cs = (p.sb(n, [P, S]) for n in ("az", "om", "k", "content", "cc", "cs"))
        t1ps, t2ps = p.ps("t1ps"), p.ps("t2ps")
        bps, cps, yps = ([p.ps(f"{n}{i}") for i in range(2)] for n in ("bps", "cps", "yps"))
        loaded, consts, diag, bias_added = p.sem("loaded"), p.sem("consts"), p.sem("diag"), p.sem("bias_added")
        xc_done, t1_ready, t1_done, t2_ready, sp_done, phi_done, trig_done, bc_ready, r_done, y_done, y_used = (
            p.sem(n) for n in ("xc_done", "t1_ready", "t1_done", "t2_ready", "sp_done", "phi_done", "trig_done",
                               "bc_ready", "r_done", "y_done", "y_used"))
        block = ctx.enter_context(nc.Block())
        a = lambda n: d[f"L1_attn_{n}"]
        loads = [(WB, a("W_B")), (WC, a("W_C")), (Wo, a("W_out")), (W1, a("W_dt1")), (W2, a("W_dt2")),
                 (bB, col(a("b_B"))), (bC, col(a("b_C"))), (b2, col(a("b_dt2"))), (om0, col(a("omega_base"))),
                 (Dc, col(a("D")))]

        @block.sync
        def _(sp):
            for t, src in loads:
                sp.dma_start(t[:, :], src).then_inc(loaded, 16)
            sp.dma_start(b1[0:T1, :], col(a("b_dt1"))).then_inc(loaded, 16)
            sp.dma_start(bo[:, :], row(a("b_out")).to_broadcast([P, D])).then_inc(loaded, 16)

        N_LOADED = 16 * (len(loads) + 2)

        @block.gpsimd
        def _(pool):
            nc.gpsimd.memset(one[:, :], 1.0)
            nc.gpsimd.memset(half_pi[:, :], math.pi / 2).then_inc(consts, 1)
            pool.wait_ge(loaded, N_LOADED)
            nc.gpsimd.tensor_scalar(Dg[:, :], net.ident[:, :], Dc[:, :], None, ALU.mult).then_inc(diag, 1)
            nc.gpsimd.tensor_tensor(net.x[:, :, :], net.x[:, :, :], over_tiles(bo[:, :], NT), ALU.add).then_inc(bias_added, 1)

        @block.tensor
        def _(pe):
            pe.wait_ge(loaded, N_LOADED)
            pe.wait_ge(diag, 1)
            pe.sem_inc(t2_ready, 2)
            pe.sem_inc(y_done, 2)

            def inner(c, par):
                pe.wait_ge(xc_done, c + 1)
                pe.wait_ge(t1_done, c + 1)
                nc.tensor.matmul(t1ps[0:T1, :], W1[:, :], xc[par][:, :], start=True, stop=True).then_inc(t1_ready, 1)
                pe.wait_ge(r_done, c + 1)
                nc.tensor.matmul(bps[par][:, :], WB[:, :], xc[par][:, :], start=True, stop=True)
                nc.tensor.matmul(cps[par][:, :], WC[:, :], xc[par][:, :], start=True, stop=True).then_inc(bc_ready, 1)
                pe.wait_ge(t1_done, c + 2)
                pe.wait_ge(sp_done, c + 1)
                nc.tensor.matmul(t2ps[:, :], W2[:, :], t1[par][0:T1, :], start=True, stop=True).then_inc(t2_ready, 1)

            def outer(c, par):
                pe.wait_ge(r_done, c + 3)
                pe.wait_ge(y_used, c + 1)
                for q in range(TC):
                    tok = slice(q * P, (q + 1) * P)
                    nc.tensor.matmul(yps[par][:, tok], r[par][:, tok], Wo[:, :], start=True, stop=False)
                    last = nc.tensor.matmul(yps[par][:, tok], xc[par][:, tok], Dg[:, :], start=False, stop=True)
                last.then_inc(y_done, 1)

            one_chunk_ahead(pe, inner, outer)

        @block.scalar
        def _(act):
            act.wait_ge(loaded, N_LOADED)
            act.wait_ge(consts, 1)
            act.sem_inc(t1_done, 1)
            act.sem_inc(sp_done, 1)
            act.sem_inc(trig_done, 2)

            def softplus(c, par):
                act.wait_ge(y_done, c + 1)
                nc.scalar.activation(xc[par][:, :], net.xT[:, bass.ts(c, S)], ACT.Copy).then_inc(xc_done, 1)
                act.wait_ge(t1_ready, c + 1)
                act.wait_ge(t2_ready, c + 1)
                nc.scalar.activation(t1[par][0:T1, :], t1ps[0:T1, :], ACT.Identity, bias=b1[0:T1, :]).then_inc(t1_done, 1)
                act.wait_ge(t2_ready, c + 3)
                act.wait_ge(phi_done, c + 1)
                nc.scalar.activation(rz[par][:, :], t2ps[:, :], ACT.Relu, bias=b2[:, :])
                nc.scalar.activation(az[:, :], t2ps[:, :], ACT.Abs, bias=b2[:, :])
                act.drain()
                nc.scalar.activation(az[:, :], az[:, :], ACT.Exp, scale=-1.0)
                act.drain()
                nc.scalar.activation(l[par][:, :], az[:, :], ACT.Ln, bias=1.0).then_inc(sp_done, 1)

            def trig(c, par):
                act.wait_ge(phi_done, c + 3)
                act.wait_ge(r_done, c + 1)
                nc.scalar.activation(sn[par][:, :], ph[par][:, :], ACT.Sin)
                nc.scalar.activation(cn[par][:, :], ph[par][:, :], ACT.Abs)
                act.drain()
                nc.scalar.activation(cn[par][:, :], cn[par][:, :], ACT.Sin, bias=half_pi[:, :], scale=-1.0).then_inc(trig_done, 1)

            one_chunk_ahead(act, softplus, trig)

        @block.vector
        def _(v):
            tt, ts, stt = nc.vector.tensor_tensor, nc.vector.tensor_scalar, nc.vector.scalar_tensor_tensor
            v.sem_inc(phi_done, 2)
            v.sem_inc(r_done, 2)
            v.sem_inc(y_used, 2)
            v.wait_ge(loaded, N_LOADED)
            v.wait_ge(consts, 1)
            v.wait_ge(bias_added, 1)

            def phase(c, par):
                v.wait_ge(sp_done, c + 2)
                tt(om[:, :], rz[par][:, :], l[par][:, :], ALU.add)
                v.drain()
                ts(om[:, :], om[:, :], om0[:, :], None, ALU.mult)
                v.drain()
                v.wait_ge(trig_done, c + 1)
                nc.vector.tensor_tensor_scan(ph[par][:, :], one[:, :], om[:, :], 0.0, ALU.mult, ALU.add)
                v.drain()
                ts(k[:, :], ph[par][:, :], 1 / (2 * math.pi), ROUND, ALU.mult, ALU.add)
                v.drain()
                ts(k[:, :], k[:, :], -ROUND, None, ALU.add)
                v.drain()
                stt(ph[par][:, :], k[:, :], -TWO_PI_HI, ph[par][:, :], ALU.mult, ALU.add)
                v.drain()
                stt(ph[par][:, :], k[:, :], -TWO_PI_LO, ph[par][:, :], ALU.mult, ALU.add)
                v.drain()
                ts(ph[par][:, :], ph[par][:, :], 3.1415925, -3.1415925, ALU.min, ALU.max).then_inc(phi_done, 1)

            def memory(c, par):
                v.wait_ge(bc_ready, c + 1)
                v.wait_ge(trig_done, c + 3)
                stt(content[:, :], bps[par][:, :], bB[:, :], xc[par][:, :], ALU.add, ALU.mult)
                v.drain()
                tt(cc[:, :], content[:, :], cn[par][:, :], ALU.mult)
                tt(cs[:, :], content[:, :], sn[par][:, :], ALU.mult)
                v.drain()
                nc.vector.tensor_tensor_scan(content[:, :], one[:, :], cc[:, :], 0.0, ALU.mult, ALU.add)
                nc.vector.tensor_tensor_scan(k[:, :], one[:, :], cs[:, :], 0.0, ALU.mult, ALU.add)
                v.drain()
                tt(cc[:, :], content[:, :], cn[par][:, :], ALU.mult)
                tt(cs[:, :], k[:, :], sn[par][:, :], ALU.mult)
                v.drain()
                tt(cc[:, :], cc[:, :], cs[:, :], ALU.add)
                v.drain()
                v.wait_ge(y_done, c + 1)
                stt(r[par][:, :], cps[par][:, :], bC[:, :], cc[:, :], ALU.add, ALU.mult).then_inc(r_done, 1)
                v.wait_ge(y_done, c + 3)
                xt = net.x[:, bass.ts(c, 4), :].rearrange("p a b -> p (a b)")
                tt(xt, xt, yps[par][:, :], ALU.add).then_inc(y_used, 1)

            one_chunk_ahead(v, phase, memory)
    measure(nc, net, "a1")


def best_groups_gate(nc, net, r, scores, groups, keep_groups, top, tag):
    E, size = r.E, r.E // groups
    with ExitStack() as ctx:
        p = Scope(nc, ctx, tag + "_bg")
        iota_done, shifted, exped = p.sem("iota_done"), p.sem("shifted"), p.sem("exped")
        giota, gs, geq, goh, gsel = (p.sb(n, [P, NT, groups]) for n in ("giota", "gs", "geq", "goh", "gsel"))
        gm, total = p.sb("gm", [P, NT]), p.sb("total", [P, NT])
        cur, sel = p.sb("cur", [P, NT, E]), p.sb("sel", [P, NT, E])
        block = ctx.enter_context(nc.Block())

        @block.gpsimd
        def _(pool):
            nc.gpsimd.iota(giota[:, :, :], pattern=[[0, NT], [1, groups]], base=0, channel_multiplier=0,
                           allow_small_or_imprecise_dtypes=True).then_inc(iota_done, 1)
            nc.gpsimd.iota(r.iota[:, :, :], pattern=[[0, NT], [1, E]], base=0, channel_multiplier=0,
                           allow_small_or_imprecise_dtypes=True).then_inc(iota_done, 1)

        @block.scalar
        def _(act):
            act.wait_ge(shifted, 1)
            nc.scalar.activation(scores[:, :, :], scores[:, :, :], ACT.Exp).then_inc(exped, 1)

        @block.vector
        def _(v):
            def pick(cur, m, eq, oh, iota, sel, n, times):
                nc.vector.memset(sel, 0.0)
                for _ in range(times):
                    first_best(nc, v, cur, m, eq, r.idx, oh, iota, n)
                    nc.vector.tensor_tensor(sel, sel, oh[:, :, :], ALU.add)
                    nc.vector.scalar_tensor_tensor(cur[:, :, :], oh[:, :, :], -4.0, cur[:, :, :], ALU.mult, ALU.add)
                    v.drain()

            v.wait_ge(iota_done, 2)
            nc.vector.tensor_reduce(r.m[:, :], r.lg[:, :, :], AX.X, ALU.max)
            v.drain()
            nc.vector.tensor_tensor(scores[:, :, :], r.lg[:, :, :], bcast(r.m[:, :], E), ALU.subtract).then_inc(shifted, 1)
            v.wait_ge(exped, 1)
            nc.vector.tensor_reduce(total[:, :], scores[:, :, :], AX.X, ALU.add)
            v.drain()
            nc.vector.reciprocal(total[:, :], total[:, :])
            v.drain()
            nc.vector.tensor_tensor(scores[:, :, :], scores[:, :, :], bcast(total[:, :], E), ALU.mult)
            v.drain()
            nc.vector.tensor_reduce(gs[:, :, :], scores[:, :, :].rearrange("p t (g s) -> p t g s", s=size), AX.X, ALU.max)
            v.drain()
            pick(gs, gm, geq, goh, giota, gsel[:, :, :], groups, keep_groups)
            v4 = lambda a: a.rearrange("p t (g s) -> p (t g) s", s=size)
            nc.vector.tensor_tensor(v4(cur[:, :, :]), v4(scores[:, :, :]),
                                    bcast(gsel[:, :, :].rearrange("p t g -> p (t g)"), size), ALU.mult)
            v.drain()
            pick(cur, r.m, r.eq, r.oh, r.iota, sel[:, :, :], E, top)
            nc.vector.tensor_tensor(r.gate[:, :, :], sel[:, :, :], scores[:, :, :], ALU.mult)


def moe_grouped_swiglu(nc, net, d):
    E, _, I = d["L1_ffn_w1"].shape
    with ExitStack() as ctx:
        r = Router(nc, ctx, "m1", E)
        scores = Scope(nc, ctx, "m1s").sb("scores", [P, NT, E])
        normalise(nc, net, "m1")
        router_logits(nc, net, "m1", d["L1_ffn_gate_w"], E, r.lg)
        best_groups_gate(nc, net, r, scores, 4, 2, 4, "m1")
        w1, w3 = (d[f"L1_ffn_{n}"].rearrange("e d i -> d e i") for n in ("w1", "w3"))
        w2 = d["L1_ffn_w2"].rearrange("e i d -> i e d")
        one = Scope(nc, ctx, "m1o").sb("one", [P, 1])
        pair = lambda w: lambda e: [(lambda t: t[:, :].rearrange("d (e i) -> d e i", e=2), w[:, bass.ds(2 * e, 2), :])]
        down = lambda e: [(lambda t, q=q: t[q * I:(q + 1) * I, 0, q * P:(q + 1) * P],
                           w2[:, bass.ds(2 * e + q, 1), :].rearrange("i a d -> i (a d)")) for q in range(2)]
        experts(nc, net, "m1e", E // 2, 1, ACT.Silu, lambda t, e, q: r.gate[:, t, bass.ds(2 * e + q, 1)],
                pair(w1), down, w3=pair(w3), nb=2)
        whole = lambda n: lambda e: [(lambda t: t[:, :], d[f"L1_ffn_{n}"])]
        experts(nc, net, "m1sh", 1, 1, ACT.Silu, lambda t, e, q: net.ones[:, 0:1],
                whole("ws1"), lambda e: [(lambda t: t[:, 0, :], d["L1_ffn_ws2"])], w3=whole("ws3"))
    measure(nc, net, "m1")


def causal_attention(nc, net, d):
    H = d["L2_attn_wq"].shape[1]
    scale = H ** -0.5
    a = lambda n: d[f"L2_attn_{n}"]
    PLACE = [(0, 0), (1, 0), (0, P), (2, 0)]
    POFF = [0, P, 3 * P, 6 * P]
    PV0 = 10
    normalise(nc, net, "a2")
    with ExitStack() as ctx:
        p = Scope(nc, ctx, "a2")
        wq, wk, wv = (p.sb(n, [P, H]) for n in ("wq", "wk", "wv"))
        wo, bq, bk = p.sb("wo", [P, D]), p.sb("bq", [H, 1]), p.sb("bk", [H, 1])
        bv, bo, mask = p.sb("bv", [P, H]), p.sb("bo", [P, D]), p.sb("mask", [P, P])
        two = lambda n, s: [p.sb(f"{n}{i}", [P, *s]) for i in range(2)]
        xc, qT, kT, V = two("xc", [S]), two("qT", [S]), two("kT", [S]), two("V", [TC, H])
        prob, nb, sums, ri = two("prob", [10 * P]), two("nb", [TC]), two("sums", [TC]), two("ri", [TC])
        PT, z = two("PT", [S]), p.sb("z", [P, TC, P])
        pj, zps, yps = p.ps("pj"), p.ps("zps", [P, TC, H]), p.ps("yps")
        sps, tps = [p.ps(f"sps{i}") for i in range(3)], [p.ps(f"tps{i}") for i in range(2)]
        wo_zeroed = p.sem("wo_zeroed")
        loaded, zeroed, bias_added = p.sem("loaded"), p.sem("zeroed"), p.sem("bias_added")
        xc_done, pj_ready, pj_used, s_ready, nb_done, p_done = (
            p.sem(n) for n in ("xc_done", "pj_ready", "pj_used", "s_ready", "nb_done", "p_done"))
        t_ready, t_used, pv_done, z_ready, z_done, y_used = (
            p.sem(n) for n in ("t_ready", "t_used", "pv_done", "z_ready", "z_done", "y_used"))
        block = ctx.enter_context(nc.Block())
        N_LOADED = 16 * 8

        @block.sync
        def _(sp):
            sp.wait_ge(wo_zeroed, 1)
            for t, src in ((wq, a("wq")), (wk, a("wk")), (wv, a("wv")), (wo, a("wo")), (bq, col(a("bq"))),
                           (bk, col(a("bk"))), (bv, row(a("bv")).to_broadcast([P, H])),
                           (bo, row(a("bo")).to_broadcast([P, D]))):
                sp.dma_start(t[:, :] if t is not wo else wo[0:H, :], src).then_inc(loaded, 16)

        @block.gpsimd
        def _(pool):
            nc.gpsimd.memset(wo[:, :], 0.0).then_inc(wo_zeroed, 1)
            nc.gpsimd.memset(z[:, :, H:P], 0.0)
            for i in range(2):
                nc.gpsimd.memset(qT[i][:, :], 0.0)
                nc.gpsimd.memset(kT[i][:, :], 0.0)
            nc.gpsimd.memset(mask[:, :], 0.0).then_inc(zeroed, 1)
            pool.wait_ge(zeroed, 1)
            nc.gpsimd.affine_select(out=mask[:, :], in_=mask[:, :], compare_op=ALU.is_ge, fill=-1e11 / scale,
                                    base=0, pattern=[[-1, P]], channel_multiplier=1).then_inc(zeroed, 1)
            pool.wait_ge(loaded, N_LOADED)
            nc.gpsimd.tensor_tensor(net.x[:, :, :], net.x[:, :, :], over_tiles(bo[:, :], NT), ALU.add).then_inc(bias_added, 1)

        @block.tensor
        def _(pe):
            pe.wait_ge(loaded, N_LOADED)
            pe.wait_ge(zeroed, 2)
            pe.sem_inc(pv_done, PV0)

            def scores(c, par):
                pe.wait_ge(xc_done, c + 1)
                pe.wait_ge(pj_used, 3 * c + 1)
                nc.tensor.matmul(pj[0:H, :], wq[:, :], xc[par][:, :], start=True, stop=True).then_inc(pj_ready, 1)
                pe.wait_ge(pj_used, 3 * c + 2)
                nc.tensor.matmul(pj[0:H, :], wk[:, :], xc[par][:, :], start=True, stop=True).then_inc(pj_ready, 1)
                pe.wait_ge(pj_used, 3 * c + 3)
                for k in range(TC):
                    last = nc.tensor.matmul(pj[:, k * H:(k + 1) * H], xc[par][:, k * P:(k + 1) * P], wv[:, :],
                                            start=True, stop=True)
                last.then_inc(pj_ready, 1)
                for q in range(TC):
                    bank, off = PLACE[q]
                    pe.wait_ge(p_done, 4 * c + (3 if bank == 0 else q + 1))
                    n = (q + 1) * P
                    nc.tensor.matmul(sps[bank][:, off:off + n], qT[par][:, q * P:n], kT[par][:, 0:n],
                                     start=True, stop=True).then_inc(s_ready, 1)

            def values(c, par):
                def turn(q):
                    u = 5 * c + q
                    b = (par + q) % 2
                    pe.wait_ge(p_done, 4 * c + q + 5)
                    pe.wait_ge(t_used, u + 1)
                    for k in range(q + 1):
                        last = nc.tensor.transpose(tps[b][:, k * P:(k + 1) * P],
                                                   prob[par][:, POFF[q] + k * P:POFF[q] + (k + 1) * P], net.ident[:, :])
                    last.then_inc(t_ready, 1)

                def pv(q):
                    pe.wait_ge(t_used, 5 * c + q + 3)
                    for k in range(q + 1):
                        last = nc.tensor.matmul(zps[:, q, :], PT[(par + q) % 2][:, k * P:(k + 1) * P], V[par][:, k, :],
                                                start=(k == 0), stop=(k == q))
                    last.then_inc(pv_done, 1)

                turn(0)
                turn(1)
                pe.wait_ge(z_done, c + 1)
                pv(0)
                turn(2)
                pv(1)
                turn(3)
                pv(2)
                pv(3)
                b = par % 2
                pe.wait_ge(z_done, c + 2)
                pe.wait_ge(t_used, 5 * c + 5)
                for k in range(TC):
                    last = nc.tensor.transpose(tps[b][:, k * P:(k + 1) * P], z[:, k, :], net.ident[:, :])
                last.then_inc(t_ready, 1)
                pe.wait_ge(t_used, 5 * c + 7)
                pe.wait_ge(y_used, c + 1)
                for k in range(TC):
                    last = nc.tensor.matmul(yps[:, k * P:(k + 1) * P], PT[b][:, k * P:(k + 1) * P], wo[:, :],
                                            start=True, stop=True)
                last.then_inc(pv_done, 1)

            one_chunk_ahead(pe, scores, values)

        @block.scalar
        def _(act):
            act.wait_ge(loaded, N_LOADED)
            act.wait_ge(zeroed, 2)
            act.sem_inc(pj_used, 1)
            act.sem_inc(p_done, 4)
            with act.Fori(0, B // 2) as i:
                for par in range(2):
                    c = 2 * i + par
                    act.wait_ge(pv_done, PV0 + 5 * c - 5)
                    nc.scalar.activation(xc[par][:, :], net.xT[:, bass.ts(c, S)], ACT.Copy).then_inc(xc_done, 1)
                    for n, (t, bias) in enumerate(((qT, bq), (kT, bk))):
                        act.wait_ge(pj_ready, 3 * c + n + 1)
                        nc.scalar.activation(t[par][0:H, :], pj[0:H, :], ACT.Identity, bias=bias[:, :]).then_inc(pj_used, 1)
                    act.wait_ge(pj_ready, 3 * c + 3)
                    nc.scalar.activation(V[par][:, :, :].rearrange("p a b -> p (a b)"), pj[:, 0:TC * H], ACT.Copy).then_inc(pj_used, 1)
                    for q in range(TC):
                        bank, off = PLACE[q]
                        act.wait_ge(nb_done, 4 * c + (3 if bank == 0 else q + 1))
                        nc.scalar.activation(prob[par][:, POFF[q]:POFF[q] + (q + 1) * P], sps[bank][:, off:off + (q + 1) * P],
                                             ACT.Exp, bias=nb[par][:, q:q + 1], scale=scale,
                                             accum_out=sums[par][:, q:q + 1]).then_inc(p_done, 1)

        @block.vector
        def _(v):
            v.sem_inc(t_used, 2)
            v.sem_inc(z_done, 1)
            v.sem_inc(y_used, 1)
            v.wait_ge(zeroed, 2)
            v.wait_ge(bias_added, 1)

            def maxima(c, par):
                for q in range(TC):
                    bank, off = PLACE[q]
                    n = (q + 1) * P
                    v.wait_ge(s_ready, 4 * c + (3 if bank == 0 else q + 1))
                    dg = sps[bank][:, off + q * P:off + n]
                    nc.vector.tensor_tensor(dg, dg, mask[:, :], ALU.add)
                    v.drain()
                    nc.vector.tensor_reduce(nb[par][:, q:q + 1], sps[bank][:, off:off + n], AX.X, ALU.max)
                    v.drain()
                    nc.vector.tensor_scalar(nb[par][:, q:q + 1], nb[par][:, q:q + 1], -scale, None, ALU.mult).then_inc(nb_done, 1)

            def outputs(c, par):
                def copy(q, rows, n):
                    u = 5 * c + q
                    v.wait_ge(t_ready, u + 1)
                    v.wait_ge(pv_done, PV0 + u - 1)
                    nc.vector.tensor_copy(PT[(par + q) % 2][0:rows, 0:n], tps[(par + q) % 2][0:rows, 0:n]).then_inc(t_used, 1)

                v.wait_ge(p_done, 4 * c + 8)
                nc.vector.reciprocal(ri[par][:, :], sums[par][:, :])
                for q in range(TC):
                    copy(q, P, (q + 1) * P)
                v.drain()
                v.wait_ge(pv_done, PV0 + 5 * c + 4)
                for q in range(TC):
                    last = nc.vector.scalar_tensor_tensor(z[:, q, 0:H], zps[:, q, :], ri[par][:, q:q + 1], bv[:, :],
                                                          ALU.mult, ALU.add)
                last.then_inc(z_done, 1)
                copy(4, P, S)
                v.wait_ge(pv_done, PV0 + 5 * c + 5)
                xt = net.x[:, bass.ts(c, 4), :].rearrange("p a b -> p (a b)")
                nc.vector.tensor_tensor(xt, xt, yps[:, :], ALU.add).then_inc(y_used, 1)

            one_chunk_ahead(v, maxima, outputs)
    measure(nc, net, "a2")


def moe_top1_gelu(nc, net, d):
    E = 8
    with ExitStack() as ctx:
        p = Scope(nc, ctx, "m2")
        lg, eq, oh = p.sb("lg", [P, NT, E]), p.sb("eq", [P, NT, E]), p.sb("onehot", [P, NT, E])
        m, idx, iota = p.sb("m", [P, NT]), p.sb("idx", [P, NT]), p.sb("iota", [P, NT, E])
        normalise(nc, net, "m2")
        router_logits(nc, net, "m2", d["L2_ffn_Wg"], E, lg, bias=d["L2_ffn_bg"])
        with ExitStack() as c2:
            iota_done = Scope(nc, c2, "m2r").sem("iota_done")
            block = c2.enter_context(nc.Block())

            @block.gpsimd
            def _(pool):
                nc.gpsimd.iota(iota[:, :, :], pattern=[[0, NT], [1, E]], base=0, channel_multiplier=0,
                               allow_small_or_imprecise_dtypes=True).then_inc(iota_done, 1)

            @block.vector
            def _(v):
                v.wait_ge(iota_done, 1)
                first_best(nc, v, lg, m, eq, idx, oh, iota, E)
        gated_bias(nc, net, "m2", oh, d["L2_ffn_b2"])
        W1 = d["L2_ffn_W1"].rearrange("e d f -> d e f")
        W2 = d["L2_ffn_W2"].rearrange("e f d -> f e d")
        b1 = d["L2_ffn_b1"].rearrange("e f a -> f e a")
        experts(nc, net, "m2e", E, 1, ACT.Gelu, lambda t, e, k: oh[:, t, bass.ds(e, 1)],
                lambda e: [(lambda t: t[:, :], W1[:, bass.ds(e, 1), :].rearrange("d a f -> d (a f)"))],
                lambda e: [(lambda t: t[:, 0, :], W2[:, bass.ds(e, 1), :].rearrange("d a f -> d (a f)"))],
                b1=lambda e: b1[:, bass.ds(e, 1), :].rearrange("f a b -> f (a b)"))
    measure(nc, net, "m2")


def root_mean_square(nc, net, tag, h, r, weight=None, out=None, first=None):
    with ExitStack() as ctx:
        p = Scope(nc, ctx, tag)
        junk, ss = p.sb("junk", [P, D]), p.sb("ss", [P, NT])
        h_done, ss_done, w_loaded = p.sem("h_done"), p.sem("ss_done"), p.sem("w_loaded")
        wb = p.sb("wb", [P, D])
        block = ctx.enter_context(nc.Block())

        @block.sync
        def _(sp):
            if weight is not None:
                sp.dma_start(wb[:, :], row(weight).to_broadcast([P, D])).then_inc(w_loaded, 16)

        @block.scalar
        def _(act):
            for t in range(NT):
                if first is not None and t % 4 == 0:
                    act.wait_ge(h_done, t // 4 + 1)
                nc.scalar.activation(junk[:, :], h[:, t, :], ACT.Square, accum_out=ss[:, t:t + 1])
                act.drain()
            nc.scalar.activation(ss[:, :], ss[:, :], ACT.Sqrt, scale=1.0 / D, bias=net.epst[:, 1:2]).then_inc(ss_done, 1)

        @block.vector
        def _(v):
            if first is not None:
                for t in range(NT):
                    last = first(t)
                    if t % 4 == 3:
                        last.then_inc(h_done, 1)
            v.wait_ge(ss_done, 1)
            nc.vector.reciprocal(r[:, :], ss[:, :])
            if out is not None:
                v.drain()
                v.wait_ge(w_loaded, 16)
                for t in range(NT):
                    nc.vector.scalar_tensor_tensor(out[:, t, :], h[:, t, :], r[:, t:t + 1], wb[:, :], ALU.mult, ALU.mult)


def turn_tokens(nc, net, tag, src, scale=None, weight=None):
    with ExitStack() as ctx:
        p = Scope(nc, ctx, tag)
        xn = [p.sb(f"xn{i}", [P, TC, D]) for i in range(2)]
        tps = [p.ps(f"tps{i}") for i in range(2)]
        wcol = p.sb("wcol", [P, 1])
        xn_done, t_done, t_free, w_loaded = p.sem("xn_done"), p.sem("t_done"), p.sem("t_free"), p.sem("w_loaded")
        block = ctx.enter_context(nc.Block())

        @block.sync
        def _(sp):
            if weight is not None:
                sp.dma_start(wcol[:, :], col(weight)).then_inc(w_loaded, 16)

        @block.vector
        def _(v):
            with v.Fori(0, B // 2) as i:
                for par in range(2):
                    c = 2 * i + par
                    v.wait_ge(t_done, c + 1)
                    if scale is None:
                        nc.vector.tensor_copy(xn[par][:, :, :], src[:, bass.ts(c, 4), :]).then_inc(xn_done, 1)
                    else:
                        nc.vector.tensor_tensor(xn[par][:, :, :], src[:, bass.ts(c, 4), :],
                                                bcast(scale[:, bass.ts(c, 4)], D), ALU.mult).then_inc(xn_done, 1)

        @block.tensor
        def _(pe):
            pe.sem_inc(t_done, 2)
            with pe.Fori(0, B // 2) as i:
                for par in range(2):
                    c = 2 * i + par
                    pe.wait_ge(xn_done, c + 1)
                    pe.wait_ge(t_free, c + 1)
                    for k in range(TC):
                        last = nc.tensor.transpose(tps[par][:, k * P:(k + 1) * P], xn[par][:, k, :], net.ident[:, :])
                    last.then_inc(t_done, 1)

        @block.scalar
        def _(act):
            act.sem_inc(t_free, 2)
            if weight is not None:
                act.wait_ge(w_loaded, 16)
            with act.Fori(0, B // 2) as i:
                for par in range(2):
                    c = 2 * i + par
                    act.wait_ge(t_done, c + 3)
                    kw = {} if weight is None else dict(scale=wcol[:, :])
                    nc.scalar.activation(net.xT[:, bass.ts(c, S)], tps[par][:, :], ACT.Identity if kw else ACT.Copy,
                                         **kw).then_inc(t_free, 1)


def decay_attention(nc, net, d):
    a = lambda n: d[f"L3_attn_{n}"]
    R = a("u").shape[1]
    K = a("k_base_kernel").shape[0]
    SUB = 32
    with ExitStack() as ctx:
        p = Scope(nc, ctx, "a3")
        h, hn = p.sb("h", [P, NT, D]), p.sb("hn", [P, NT, D])
        qk, rn = p.sb("qk", [P, NT, 2 * R]), p.sb("rn", [P, NT, 2])
        r1, g = p.sb("r1", [P, NT]), p.sb("g", [P, K])
        NB = P // SUB
        tQ, tQ2, tK, gP = p.sb("tQ", [R, P]), p.sb("tQ2", [R, P]), p.sb("tK", [R, NB, P]), p.sb("gP", [R, 1])
        tK2, causal = p.sb("tK2", [P, R]), p.sb("causal", [P, P])

        normalise_only = lambda t: nc.vector.tensor_scalar(h[:, t, :], net.x[:, t, :], net.stat[:, t, 0:1],
                                                           net.rstd[:, t:t + 1], ALU.subtract, ALU.mult)
        token_rstd(nc, net, "a3")
        root_mean_square(nc, net, "a3r1", h, r1, weight=a("norm1_w"), out=hn, first=normalise_only)
        turn_tokens(nc, net, "a3t", hn)
        router_logits(nc, net, "a3", (a("u"), a("v")), 2 * R, qk)
        decay_tables(nc, net, a, R, K, SUB, qk, rn, g, tQ, tQ2, tK, gP, tK2, causal)
        decay_mix(nc, net, a, R, K, SUB, h, hn, qk, rn, g, tQ, tQ2, tK, gP, tK2, causal)
        root_mean_square(nc, net, "a3r2", h, r1)
        turn_tokens(nc, net, "a3t2", h, scale=r1, weight=a("norm2_w"))
    F = a("mlp_w1").shape[1]
    experts(nc, net, "a3m", 1, F // P, ACT.Gelu_apprx_tanh, lambda t, e, q: net.ones[:, 0:1],
            lambda e: [(lambda t: t[:, :], a("mlp_w1"))],
            lambda e: [(lambda t: t[:, :, :], a("mlp_w2").rearrange("(g f) d -> f g d", f=P))],
            b1=lambda e: a("mlp_b1"))
    measure(nc, net, "a3")


def token_rstd(nc, net, tag):
    with ExitStack() as ctx:
        p = Scope(nc, ctx, tag + "_rs")
        std, std_done = p.sb("std", [P, NT]), p.sem("std_done")
        block = ctx.enter_context(nc.Block())

        @block.scalar
        def _(act):
            nc.scalar.activation(std[:, :], net.stat[:, :, 1], ACT.Sqrt, bias=net.epst[:, 0:1]).then_inc(std_done, 1)

        @block.vector
        def _(v):
            v.wait_ge(std_done, 1)
            nc.vector.reciprocal(net.rstd[:, :], std[:, :])


def decay_tables(nc, net, a, R, K, SUB, qk, rn, g, tQ, tQ2, tK, gP, tK2, causal):
    NB = P // SUB
    with ExitStack() as ctx:
        p = Scope(nc, ctx, "a3tab")
        dl, al = p.sb("dl", [R, 1]), p.sb("al", [R, 1])
        dlb, jcol = p.sb("dlb", [P, R]), p.sb("jcol", [P, 1])
        gate, sq = p.sb("gate", [P, 1]), p.sb("sq", [P, NT, 2 * R])
        loaded, counted, sig, clipped, lned, ready, squared, rooted = (
            p.sem(n) for n in ("loaded", "counted", "sig", "clipped", "lned", "ready", "squared", "rooted"))
        block = ctx.enter_context(nc.Block())

        @block.sync
        def _(sp):
            sp.dma_start(dl[:, :], col(a("decay_logit"))).then_inc(loaded, 16)
            sp.dma_start(al[:, :], col(a("alpha_logit"))).then_inc(loaded, 16)
            sp.dma_start(dlb[:, :], row(a("decay_logit")).to_broadcast([P, R])).then_inc(loaded, 16)
            sp.dma_start(gate[:, :], row(a("k_base_gate_logit")).to_broadcast([P, 1])).then_inc(loaded, 16)
            sp.dma_start(g[:, :], row(a("k_base_kernel")).to_broadcast([P, K])).then_inc(loaded, 16)

        @block.gpsimd
        def _(pool):
            io = dict(base=0, channel_multiplier=0, allow_small_or_imprecise_dtypes=True)
            nc.gpsimd.iota(tQ[:, :], pattern=[[0, NB], [1, SUB]], **io)
            nc.gpsimd.iota(tQ2[:, :], pattern=[[1, P]], **io)
            nc.gpsimd.iota(tK[:, :, :], pattern=[[SUB, NB], [-1, P]], **io)
            nc.gpsimd.memset(gP[:, :], float(P))
            nc.gpsimd.iota(jcol[:, :], pattern=[[0, 1]], base=P, channel_multiplier=-1,
                           allow_small_or_imprecise_dtypes=True)
            nc.gpsimd.memset(causal[:, :], 1.0).then_inc(counted, 1)
            pool.wait_ge(counted, 1)
            nc.gpsimd.affine_select(out=causal[:, :], in_=causal[:, :], compare_op=ALU.is_ge, fill=0.0,
                                    base=0, pattern=[[1, P]], channel_multiplier=-1).then_inc(counted, 1)

        @block.scalar
        def _(act):
            act.wait_ge(loaded, 80)
            act.wait_ge(squared, 1)
            nc.scalar.activation(rn[:, :, :], rn[:, :, :], ACT.Sqrt).then_inc(rooted, 1)
            for t in (dl, al, dlb, gate):
                last = nc.scalar.activation(t[:, :], t[:, :], ACT.Sigmoid)
            last.then_inc(sig, 1)
            act.wait_ge(clipped, 1)
            nc.scalar.activation(dl[:, :], dl[:, :], ACT.Ln)
            nc.scalar.activation(dlb[:, :], dlb[:, :], ACT.Ln).then_inc(lned, 1)
            act.wait_ge(ready, 1)
            act.drain()
            for t in (tQ[:, :], tQ2[:, :], tK[:, :, :], gP[:, :]):
                nc.scalar.activation(t, t, ACT.Exp, scale=dl[:, :])
            nc.scalar.activation(tK2[:, :], tK2[:, :], ACT.Exp)
            act.drain()
            for t in (tQ, tQ2):
                nc.scalar.activation(t[:, :], t[:, :], ACT.Copy, scale=al[:, :])

        @block.vector
        def _(v):
            nc.vector.tensor_tensor(sq[:, :, :], qk[:, :, :], qk[:, :, :], ALU.mult)
            v.drain()
            nc.vector.tensor_reduce(rn[:, :, :], sq[:, :, :].rearrange("p t (s r) -> p t s r", s=2), AX.X,
                                    ALU.add).then_inc(squared, 1)
            v.wait_ge(sig, 1)
            for t in (dl, dlb):
                last = nc.vector.tensor_scalar(t[:, :], t[:, :], 0.15, 1.0, ALU.max, ALU.min)
            last.then_inc(clipped, 1)
            v.wait_ge(counted, 2)
            nc.vector.tensor_scalar(tK[:, :, :], tK[:, :, :], float(1 - SUB), None, ALU.max)
            v.wait_ge(lned, 1)
            nc.vector.tensor_scalar(tK2[:, :], dlb[:, :], jcol[:, :], None, ALU.mult).then_inc(ready, 1)
            nc.vector.tensor_scalar(g[:, :], g[:, :], gate[:, :], None, ALU.mult)
            v.wait_ge(rooted, 1)
            nc.vector.tensor_scalar(rn[:, :, :], rn[:, :, :], 1e-8, None, ALU.max)
            v.drain()
            nc.vector.reciprocal(rn[:, :, :], rn[:, :, :])


def decay_mix(nc, net, a, R, K, SUB, h, hn, qk, rn, g, tQ, tQ2, tK, gP, tK2, causal):
    NB = P // SUB
    with ExitStack() as ctx:
        p = Scope(nc, ctx, "a3x")
        two = lambda n, s, q=P: [p.sb(f"{n}{i}", [q, *s]) for i in range(2)]
        proj, pb, mb = p.sb("proj", [P, D]), p.sb("pb", [P, D]), p.sb("mb", [P, D])
        hc, qc, kk = two("hc", [TC, D]), two("qc", [TC, 2 * R]), two("kk", [TC, R])
        Qp, Qpp, Kp = two("Qp", [S], R), two("Qpp", [S], R), two("Kp", [NB, S], R)
        AT, SS, T = two("AT", [S]), two("SS", [TC, D], R), two("T", [S])
        tq, tk, aps, sps = p.ps("tq"), p.ps("tk"), p.ps("aps"), p.ps("sps", [P, TC, D])
        dps, ops = [p.ps(f"dps{i}") for i in range(2)], [p.ps(f"ops{i}") for i in range(2)]
        loaded, bias_added, hc_done, qc_done, t_ready, tab_done = (
            p.sem(n) for n in ("loaded", "bias_added", "hc_done", "qc_done", "t_ready", "tab_done"))
        a_done, am_done, dec_done, conv_done, proj_done, add_done = (
            p.sem(n) for n in ("a_done", "am_done", "dec_done", "conv_done", "proj_done", "add_done"))
        block = ctx.enter_context(nc.Block())

        @block.sync
        def _(sp):
            sp.dma_start(proj[:, :], a("proj_w")).then_inc(loaded, 16)
            sp.dma_start(pb[:, :], row(a("proj_b")).to_broadcast([P, D])).then_inc(loaded, 16)
            sp.dma_start(mb[:, :], row(a("mlp_b2")).to_broadcast([P, D])).then_inc(loaded, 16)

        @block.gpsimd
        def _(pool):
            pool.wait_ge(loaded, 48)
            nc.gpsimd.tensor_tensor(h[:, :, :], h[:, :, :], over_tiles(pb[:, :], NT), ALU.add).then_inc(bias_added, 1)
            nc.gpsimd.tensor_tensor(net.x[:, :, :], net.x[:, :, :], over_tiles(mb[:, :], NT), ALU.add).then_inc(bias_added, 1)
            pool.wait_ge(bias_added, 2)
            with pool.Fori(0, B) as c:
                pool.wait_ge(add_done, c + 3)
                xt = net.x[:, bass.ts(c, 4), :]
                nc.gpsimd.tensor_tensor(xt, xt, h[:, bass.ts(c, 4), :], ALU.add)

        @block.scalar
        def _(act):
            with act.Fori(0, B // 2) as i:
                for par in range(2):
                    c = 2 * i + par
                    act.wait_ge(dec_done, c + 1)
                    nc.scalar.activation(hc[par][:, :, :], hn[:, bass.ts(c, 4), :], ACT.Copy).then_inc(hc_done, 1)

        @block.tensor
        def _(pe):
            pe.wait_ge(loaded, 48)
            pe.sem_inc(t_ready, 2)
            pe.sem_inc(a_done, 2)
            pe.sem_inc(dec_done, 2)
            pe.sem_inc(proj_done, 2)

            def inside(c, par):
                pe.wait_ge(qc_done, c + 1)
                pe.wait_ge(tab_done, c + 1)
                for k in range(TC):
                    tok = slice(k * P, (k + 1) * P)
                    nc.tensor.transpose(tq[0:R, tok], qc[par][:, k, 0:R], net.ident[:, :])
                    last = nc.tensor.transpose(tk[0:R, tok], qc[par][:, k, R:2 * R], net.ident[:, :])
                last.then_inc(t_ready, 1)
                pe.wait_ge(hc_done, c + 1)
                pe.wait_ge(am_done, c + 1)
                pe.wait_ge(tab_done, c + 2)
                for k in range(TC - 1):
                    nc.tensor.matmul(sps[0:R, k, :], kk[par][:, k, :], hc[par][:, k, :], start=True, stop=True)
                for k in range(TC):
                    for b in range(NB):
                        sub = slice(k * P + b * SUB, k * P + (b + 1) * SUB)
                        last = nc.tensor.matmul(aps[:, sub], Kp[par][0:R, b, k * P:(k + 1) * P], Qp[par][0:R, sub],
                                                start=True, stop=True)
                last.then_inc(a_done, 1)

            def across(c, par):
                pe.wait_ge(am_done, c + 2)
                pe.wait_ge(conv_done, c + 1)
                for k in range(TC):
                    tok = slice(k * P, (k + 1) * P)
                    last = nc.tensor.matmul(dps[par][:, tok], hc[par][:, k, :], AT[par][:, tok], start=True, stop=(k == 0))
                    if k > 0:
                        last = nc.tensor.matmul(dps[par][:, tok], SS[par][0:R, k, :], Qpp[par][0:R, tok],
                                                start=False, stop=True)
                last.then_inc(dec_done, 1)
                pe.wait_ge(conv_done, c + 3)
                pe.wait_ge(add_done, c + 1)
                for k in range(TC):
                    tok = slice(k * P, (k + 1) * P)
                    last = nc.tensor.matmul(ops[par][:, tok], T[par][:, tok], proj[:, :], start=True, stop=True)
                last.then_inc(proj_done, 1)

            one_chunk_ahead(pe, inside, across)

        @block.vector
        def _(v):
            tt, stt = nc.vector.tensor_tensor, nc.vector.scalar_tensor_tensor
            v.sem_inc(tab_done, 1)
            v.sem_inc(am_done, 1)
            v.sem_inc(conv_done, 2)
            v.sem_inc(add_done, 2)

            def inside(c, par):
                v.wait_ge(t_ready, c + 1)
                tt(qc[par][:, :, :].rearrange("p t (s r) -> p (t s) r", s=2),
                   qk[:, bass.ts(c, 4), :].rearrange("p t (s r) -> p (t s) r", s=2),
                   bcast(rn[:, bass.ts(c, 4), :].rearrange("p t s -> p (t s)"), R), ALU.mult).then_inc(qc_done, 1)
                v.drain()
                v.wait_ge(a_done, c + 1)
                tt(kk[par][:, :, :], qc[par][:, :, R:2 * R], over_tiles(tK2[:, :], TC), ALU.mult)
                v.wait_ge(t_ready, c + 3)
                v.wait_ge(dec_done, c + 1)
                tiles = lambda t: t.rearrange("r (t i) -> r t i", i=P)
                tt(tiles(Qp[par][:, :]), tiles(tq[0:R, :]), over_tiles(tQ[:, :], TC), ALU.mult)
                tt(tiles(Qpp[par][:, :]), tiles(tq[0:R, :]), over_tiles(tQ2[:, :], TC), ALU.mult)
                for b in range(NB):
                    last = tt(tiles(Kp[par][:, b, :]), tiles(tk[0:R, :]), over_tiles(tK[:, b, :], TC), ALU.mult)
                last.then_inc(tab_done, 1)
                v.wait_ge(a_done, c + 3)
                tt(AT[par][:, :].rearrange("j (t i) -> j t i", i=P), aps[:, :].rearrange("j (t i) -> j t i", i=P),
                   over_tiles(causal[:, :], TC), ALU.mult)
                nc.vector.tensor_copy(SS[par][:, 1, :], sps[0:R, 0, :])
                v.drain()
                stt(SS[par][:, 2, :], SS[par][:, 1, :], gP[:, :], sps[0:R, 1, :], ALU.mult, ALU.add)
                v.drain()
                stt(SS[par][:, 3, :], SS[par][:, 2, :], gP[:, :], sps[0:R, 2, :], ALU.mult, ALU.add).then_inc(am_done, 1)

            def across(c, par):
                v.wait_ge(dec_done, c + 3)
                v.wait_ge(proj_done, c + 1)
                t = T[par]
                stt(t[:, :], net.xT[:, bass.ts(c, S)], g[:, 0:1], dps[par][:, :], ALU.mult, ALU.add)
                v.drain()
                for j in range(1, K):
                    last = stt(t[:, j:], net.xT[:, bass.ds(c * S, S - j)], g[:, j:j + 1], t[:, j:], ALU.mult, ALU.add)
                    if j == K - 1:
                        last.then_inc(conv_done, 1)
                    v.drain()
                v.wait_ge(proj_done, c + 3)
                v.wait_ge(bias_added, 2)
                ht = h[:, bass.ts(c, 4), :].rearrange("p a b -> p (a b)")
                tt(ht, ht, ops[par][:, :], ALU.add).then_inc(add_done, 1)

            one_chunk_ahead(v, inside, across)


def moe_linear(nc, net, d):
    E = d["L3_ffn_b"].shape[0]
    with ExitStack() as ctx:
        r = Router(nc, ctx, "m3", E)
        normalise(nc, net, "m3")
        router_logits(nc, net, "m3", d["L3_ffn_wg"], E, r.lg)
        top1_prob(nc, r, "m3")
        capacity_by_order(nc, net, r, B * S // E, "m3")
        moe_linear_products(nc, net, d, r, E)
        gated_bias(nc, net, "m3", r.gate, d["L3_ffn_b"])


def moe_linear_products(nc, net, d, r, E):
    with ExitStack() as ctx:
        p = Scope(nc, ctx, "m3e")
        WT = p.sb("WT", [P, E, D])
        xn = [p.sb(f"xn{i}", [P, TC, D]) for i in range(2)]
        xc = [p.sb(f"xc{i}", [P, S]) for i in range(2)]
        tps = [p.ps(f"tps{i}") for i in range(2)]
        yps = [p.ps(f"yps{i}", [P, E, D]) for i in range(2)]
        loaded = p.sem("loaded")
        xn_done = p.sem("xn_done")
        t_done = p.sem("t_done")
        xc_done = p.sem("xc_done")
        y_done = p.sem("y_done")
        y_used = p.sem("y_used")
        block = ctx.enter_context(nc.Block())

        @block.sync
        def _(sp):
            sp.dma_start(WT[:, :, :], d["L3_ffn_W"]).then_inc(loaded, 16)

        @block.tensor
        def _(pe):
            pe.wait_ge(loaded, 16)
            pe.sem_inc(t_done, 2)
            pe.sem_inc(y_done, 5)

            def turn(c, par):
                pe.wait_ge(xn_done, c + 1)
                pe.wait_ge(xc_done, c + 1)
                for k in range(TC):
                    last = nc.tensor.transpose(tps[par][:, k * P:(k + 1) * P], xn[par][:, k, :], net.ident[:, :])
                last.then_inc(t_done, 1)

            def products(c, par):
                pe.wait_ge(xc_done, c + 3)
                for k in range(TC):
                    pe.wait_ge(y_used, 4 * c + k + 1)
                    for q in range(2):
                        last = nc.tensor.matmul(yps[k % 2][:, 4 * q:4 * q + 4, :].rearrange("p e d -> p (e d)"),
                                                xc[par][:, k * P:(k + 1) * P],
                                                WT[:, 4 * q:4 * q + 4, :].rearrange("p e d -> p (e d)"),
                                                start=True, stop=True)
                    last.then_inc(y_done, 1)

            one_chunk_ahead(pe, turn, products)

        @block.scalar
        def _(act):
            act.sem_inc(xc_done, 2)
            with act.Fori(0, B // 2) as i:
                for par in range(2):
                    c = 2 * i + par
                    act.wait_ge(t_done, c + 3)
                    act.wait_ge(y_done, 4 * c + 1)
                    nc.scalar.activation(xc[par][:, :], tps[par][:, :], ACT.Copy).then_inc(xc_done, 1)

        @block.vector
        def _(v):
            v.sem_inc(y_used, 2)

            def norm(c, par):
                v.wait_ge(t_done, c + 1)
                for k in range(TC):
                    last = nc.vector.tensor_scalar(xn[par][:, k, :], net.x[:, 4 * c + k, :],
                                                   net.stat[:, 4 * c + k, 0:1],
                                                   net.rstd[:, bass.ds(4 * c + k, 1)], ALU.subtract, ALU.mult)
                last.then_inc(xn_done, 1)

            def gather(c, par):
                for k in range(TC):
                    v.wait_ge(y_done, 4 * c + k + 6)
                    for e in range(E):
                        xt = net.x[:, 4 * c + k, :]
                        last = nc.vector.scalar_tensor_tensor(xt, yps[k % 2][:, e, :], r.gate[:, 4 * c + k, e:e + 1],
                                                              xt, ALU.mult, ALU.add)
                        if e == E - 1:
                            last.then_inc(y_used, 1)
                        v.drain()

            one_chunk_ahead(v, norm, gather)


def program(nc, d, out):
    Scope.used = []
    with ExitStack() as ctx:
        net = Net(nc, ctx)
        load_and_measure(nc, net, d["L0_attn_x"])
        relative_attention(nc, net, d)
        renew_semaphores(nc)
        moe_capacity_relu(nc, net, d)
        renew_semaphores(nc)
        phase_memory(nc, net, d)
        renew_semaphores(nc)
        moe_grouped_swiglu(nc, net, d)
        renew_semaphores(nc)
        causal_attention(nc, net, d)
        renew_semaphores(nc)
        moe_top1_gelu(nc, net, d)
        renew_semaphores(nc)
        decay_attention(nc, net, d)
        renew_semaphores(nc)
        moe_linear(nc, net, d)
        store(nc, net, out)


def tables():
    import numpy as np
    HD = 8
    div = np.exp(np.arange(0, HD, 2, dtype=np.float64) * (-np.log(10000.0) / HD))
    angle = np.arange(512)[None, :] * div[:, None]
    t = np.stack([np.sin(angle), np.cos(angle)], axis=1).reshape(HD, 512)
    m1, m2 = np.zeros((HD, HD)), np.zeros((HD, HD))
    for m in range(HD // 2):
        s, c = 2 * m, 2 * m + 1
        m1[s, c] = m1[c, c] = 1
        m2[s, s], m2[c, s] = 1, -1
    return {"rel_t": t.astype(np.float32), "rel_m1": m1.astype(np.float32), "rel_m2": m2.astype(np.float32)}


def laid_out(name, a):
    import numpy as np
    if name in ("L0_ffn_router_w", "L1_ffn_gate_w", "L3_attn_proj_w"):
        a = a.T
    elif name in ("L0_attn_w_qkv", "L0_attn_b_qkv"):
        a = a.reshape(a.shape[:-1] + (3, 16, 8))
        a = np.stack([np.swapaxes(a[..., 0, :, :], -1, -2).reshape(a.shape[:-3] + (128,)),
                      np.swapaxes(a[..., 1, :, :], -1, -2).reshape(a.shape[:-3] + (128,)),
                      a[..., 2, :, :].reshape(a.shape[:-3] + (128,))], axis=-2)
    elif name == "L3_ffn_W":
        a = a.transpose(2, 0, 1)
    elif name in ("L0_ffn_b1", "L2_ffn_b1"):
        a = a.reshape(a.shape[0], -1, 128).transpose(0, 2, 1)
    elif name == "L3_attn_mlp_b1":
        a = a.reshape(-1, 128).T
    elif a.ndim == 0:
        a = a.reshape(1)
    return np.ascontiguousarray(a)


def kernel(**inputs):
    import numpy as _np
    import concourse.bacc as _bacc
    from concourse import mybir as _mybir
    from concourse.bass_utils import run_bass_kernel_spmd as _run

    nc = _bacc.Bacc("TRN2", target_bir_lowering=False, num_devices=1)
    arrays, dram = {}, {}
    for name in inputs:
        a = laid_out(name, _np.asarray(inputs[name]))
        arrays[f"in_{name}"] = a
        dram[name] = nc.dram_tensor(f"in_{name}", a.shape, _mybir.dt.from_np(a.dtype), kind="ExternalInput").ap()
    for name, a in tables().items():
        arrays[f"tab_{name}"] = a
        dram[name] = nc.dram_tensor(f"tab_{name}", a.shape, _mybir.dt.from_np(a.dtype), kind="ExternalInput").ap()
    out = nc.dram_tensor("out_x", (B, S, D), _mybir.dt.float32, kind="ExternalOutput").ap()
    program(nc, dram, out)
    return _run(nc, [arrays], core_ids=[0]).results[0]["out_x"]
```

```python
import numpy as np
import concourse.bass as bass
from concourse import mybir
from contextlib import ExitStack

FP = mybir.dt.float32
BF = mybir.dt.bfloat16
I32 = mybir.dt.int32
ACT = mybir.ActivationFunctionType
ALU = mybir.AluOpType
AX = mybir.AxisListType

B, S, D = 8, 512, 128
P = 128
NT = B * S // P
TC = S // P
LN_EPS = 1e-5


class Net:

    def __init__(self, nc, ctx):
        self.nc = nc
        sb = lambda n, s, d=FP: ctx.enter_context(nc.sbuf_tensor(n, s, d))
        self.x = sb("x_resid", [P, NT, D])
        self.stat = sb("x_stat", [P, NT, 2])
        self.rstd = sb("x_rstd", [P, NT])
        self.ident = sb("ident", [P, P])
        self.ones = sb("ones_sq", [P, P])
        self.xT = sb("x_normT", [P, B * S])
        self.epst = sb("eps_col", [P, 2])


class Scope:

    used = []

    def __init__(self, nc, ctx, tag):
        self.nc, self.ctx, self.tag = nc, ctx, tag

    def sb(self, name, shape, dt=FP):
        return self.ctx.enter_context(self.nc.sbuf_tensor(f"{self.tag}_{name}", shape, dt))

    def ps(self, name, shape=(P, 512), dt=FP):
        return self.ctx.enter_context(self.nc.psum_tensor(f"{self.tag}_{name}", list(shape), dt))

    def sem(self, name):
        handle = self.nc.alloc_semaphore(name=f"{self.tag}_{name}")
        Scope.used.append(handle)
        return handle


def renew_semaphores(nc):
    nc.clear_and_free_semaphores(Scope.used)
    nc.all_engine_barrier()
    Scope.used = []


def row(v):
    return v.rearrange("(a n) -> a n", a=1)


def col(v):
    return v.rearrange("(n a) -> n a", a=1)


def load_and_measure(nc, net, x_dram):
    with ExitStack() as ctx:
        p = Scope(nc, ctx, "in")
        loaded = [p.sem(f"loaded{i}") for i in range(4)]
        zeroed, ready = p.sem("ident_zeroed"), p.sem("ident_ready")
        bst = p.sb("bst", [P, 8, 6])
        block = ctx.enter_context(nc.Block())
        xv = x_dram.rearrange("b (t p) d -> p (b t) d", p=P)

        @block.sync
        def _(sp):
            for q in range(4):
                sp.dma_start(net.x[:, 8 * q:8 * q + 8, :], xv[:, 8 * q:8 * q + 8, :]).then_inc(loaded[q], 16)

        @block.gpsimd
        def _(pool):
            nc.gpsimd.memset(net.ident[:, :], 0.0).then_inc(zeroed, 1)
            nc.gpsimd.memset(net.ones[:, :], 1.0)
            nc.gpsimd.memset(net.epst[:, 0:1], LN_EPS)
            nc.gpsimd.memset(net.epst[:, 1:2], 1e-6)
            pool.wait_ge(zeroed, 1)
            nc.gpsimd.affine_select(out=net.ident[:, :], in_=net.ident[:, :], compare_op=ALU.not_equal, fill=1.0,
                                    base=0, pattern=[[-1, P]], channel_multiplier=1).then_inc(ready, 1)

        @block.vector
        def _(v):
            for q in range(4):
                v.wait_ge(loaded[q], 16)
                for k in range(8):
                    nc.vector.bn_stats(bst[:, k, :], net.x[:, 8 * q + k, :])
                v.drain()
                for k in range(8):
                    nc.vector.bn_aggr(net.stat[:, 8 * q + k, :], bst[:, k, :])
                v.drain()


def normalise(nc, net, tag, src=None, g=None, b=None):
    with ExitStack() as ctx:
        p = Scope(nc, ctx, tag + "_ln")
        xn = [p.sb(f"xn{i}", [P, TC, D]) for i in range(2)]
        gcol, bcol = p.sb("gcol", [P, 1]), p.sb("bcol", [P, 1])
        w_loaded = p.sem("w_loaded")
        std = p.sb("std", [P, NT])
        tps = [p.ps(f"tps{i}") for i in range(2)]
        std_done, xn_done = p.sem("std_done"), p.sem("xn_done")
        t_done, t_free = p.sem("t_done"), p.sem("t_free")
        block = ctx.enter_context(nc.Block())
        src = net.x if src is None else src

        @block.sync
        def _(sp):
            if g is not None:
                sp.dma_start(gcol[:, :], col(g)).then_inc(w_loaded, 16)
                sp.dma_start(bcol[:, :], col(b)).then_inc(w_loaded, 16)

        @block.vector
        def _(v):
            v.wait_ge(std_done, 1)
            nc.vector.reciprocal(net.rstd[:, :], std[:, :])
            v.drain()
            with v.Fori(0, B // 2) as i:
                for par in range(2):
                    c = 2 * i + par
                    v.wait_ge(t_done, c + 1)
                    for k in range(TC):
                        last = nc.vector.tensor_scalar(xn[par][:, k, :], src[:, 4 * c + k, :], net.stat[:, 4 * c + k, 0:1],
                                                       net.rstd[:, bass.ds(4 * c + k, 1)], ALU.subtract, ALU.mult)
                    last.then_inc(xn_done, 1)

        @block.tensor
        def _(pe):
            pe.sem_inc(t_done, 2)
            with pe.Fori(0, B // 2) as i:
                for par in range(2):
                    c = 2 * i + par
                    pe.wait_ge(xn_done, c + 1)
                    pe.wait_ge(t_free, c + 1)
                    for k in range(TC):
                        last = nc.tensor.transpose(tps[par][:, k * P:(k + 1) * P], xn[par][:, k, :], net.ident[:, :])
                    last.then_inc(t_done, 1)

        @block.scalar
        def _(act):
            nc.scalar.activation(std[:, :], net.stat[:, :, 1], ACT.Sqrt, bias=net.epst[:, 0:1]).then_inc(std_done, 1)
            act.sem_inc(t_free, 2)
            if g is not None:
                act.wait_ge(w_loaded, 32)
            with act.Fori(0, B // 2) as i:
                for par in range(2):
                    c = 2 * i + par
                    act.wait_ge(t_done, c + 3)
                    sc = {} if g is None else dict(scale=gcol[:, :], bias=bcol[:, :])
                    nc.scalar.activation(net.xT[:, bass.ts(c, S)], tps[par][:, :],
                                         ACT.Identity, **sc).then_inc(t_free, 1)


def store(nc, net, out):
    with ExitStack() as ctx:
        p = Scope(nc, ctx, "out")
        stored = p.sem("stored")
        block = ctx.enter_context(nc.Block())
        ov = out.rearrange("b (t p) d -> p (b t) d", p=P)

        @block.sync
        def _(sp):
            for q in range(4):
                sp.dma_start(ov[:, 8 * q:8 * q + 8, :], net.x[:, 8 * q:8 * q + 8, :]).then_inc(stored, 16)
            sp.wait_ge(stored, 64)


def one_chunk_ahead(eng, front, back):
    front(0, 0)
    with eng.Fori(0, B // 2 - 1) as i:
        front(2 * i + 1, 1)
        back(2 * i, 0)
        front(2 * i + 2, 0)
        back(2 * i + 1, 1)
    front(B - 1, 1)
    back(B - 2, 0)
    back(B - 1, 1)


def skewed(eng, *stages):
    first, last = -max(k for _, k in stages), B - 1 - min(k for _, k in stages)
    lo = -min(k for _, k in stages)
    lo += lo % 2
    n = (B - max(k for _, k in stages) - lo) // 2

    def step(c):
        for f, k in stages:
            if 0 <= c + k < B:
                f(c + k, (c + k) % 2)

    for c in range(first, lo):
        step(c)
    with eng.Fori(lo // 2, lo // 2 + n) as i:
        for par in range(2):
            for f, k in stages:
                f(2 * i + par + k, (par + k) % 2)
    for c in range(lo + 2 * n, last + 1):
        step(c)


def expert_pairs(eng, n):
    if n == 1:
        yield 0, 0
        return
    with eng.Fori(0, n // 2) as j:
        for ep in range(2):
            yield j, ep


def experts(nc, net, tag, n, nf, func, gate, w1, w2, b1=None, w3=None, nb=1):
    glu = w3 is not None
    with ExitStack() as ctx:
        p = Scope(nc, ctx, tag)
        w1t = [p.sb(f"w1_{i}", [P, nf * P]) for i in range(2)]
        w3t = [p.sb(f"w3_{i}", [P, P]) for i in range(2)] if glu else None
        w2t = [p.sb(f"w2_{i}", [P, nf, nb * P]) for i in range(2)]
        b1t = [p.sb(f"b1_{i}", [P, nf]) for i in range(2)]
        h = [p.sb(f"h{i}", [P, nf, S]) for i in range(2)]
        act_h = [p.sb(f"act{i}", [P, S]) for i in range(2)] if glu else None
        nh = 4 if nf == 4 else 2
        hps = [p.ps(f"hps{i}") for i in range(nh)]
        gps = [p.ps(f"gps{i}") for i in range(2)] if glu else None
        yps = [p.ps(f"yps{i}", [P, TC, nb * P]) for i in range(2)]
        loaded = [p.sem(f"loaded{i}") for i in range(2)]
        zeroed = p.sem("zeroed")
        h_done = p.sem("h_done")
        act_done = p.sem("act_done")
        glu_done = p.sem("glu_done")
        y_done = p.sem("y_done")
        y_used = p.sem("y_used")
        n_load = len(w1(0)) + len(w2(0)) + (len(w3(0)) if glu else 0) + (1 if b1 else 0)
        H0, Y0, U0 = nh, 2, 2
        block = ctx.enter_context(nc.Block())

        @block.sync
        def _(sp):
            def load(e, par):
                for dst, src in w1(e):
                    sp.dma_start(dst(w1t[par]), src).then_inc(loaded[par], 16)
                for dst, src in w3(e) if glu else ():
                    sp.dma_start(dst(w3t[par]), src).then_inc(loaded[par], 16)
                for dst, src in w2(e):
                    sp.dma_start(dst(w2t[par]), src).then_inc(loaded[par], 16)
                if b1:
                    sp.dma_start(b1t[par][:, :], b1(e)).then_inc(loaded[par], 16)
            sp.wait_ge(zeroed, 1)
            load(0, 0)
            if n > 1:
                load(1, 1)
            if n > 2:
                with sp.Fori(1, n // 2) as j:
                    for par in range(2):
                        sp.wait_ge(y_done, Y0 + 8 * (2 * j + par) - 8)
                        load(2 * j + par, par)

        @block.gpsimd
        def _(pool):
            for i in range(2):
                last = nc.gpsimd.memset(w2t[i][:, :, :], 0.0)
            last.then_inc(zeroed, 1)

        @block.tensor
        def _(pe):
            pe.sem_inc(y_done, Y0)
            for j, ep in expert_pairs(pe, n):
                    s0 = 8 * (2 * j + ep)
                    pe.wait_ge(loaded[ep], 16 * n_load * (j + 1))

                    def front(c, par):
                        for f in range(nf):
                            bank = f if nf == 4 else par
                            pe.wait_ge(act_done, (s0 + c) * nf + f + 1)
                            if glu:
                                pe.wait_ge(glu_done, s0 + c + 1)
                            last = nc.tensor.matmul(hps[bank][:, :], w1t[ep][:, f * P:(f + 1) * P],
                                                    net.xT[:, bass.ts(c, S)], start=True, stop=True)
                            if glu:
                                last = nc.tensor.matmul(gps[par][:, :], w3t[ep][:, :],
                                                        net.xT[:, bass.ts(c, S)], start=True, stop=True)
                            last.then_inc(h_done, 1)

                    def back(c, par):
                        if glu:
                            pe.wait_ge(glu_done, 2 + s0 + c + 1)
                        else:
                            pe.wait_ge(act_done, H0 + (s0 + c + 1) * nf)
                        pe.wait_ge(y_used, s0 + c + 1)
                        for k in range(TC):
                            for f in range(nf):
                                last = nc.tensor.matmul(yps[par][:, k, :], h[par][:, f, k * P:(k + 1) * P],
                                                        w2t[ep][:, f, :], start=(f == 0), stop=(f == nf - 1))
                        last.then_inc(y_done, 1)

                    one_chunk_ahead(pe, front, back)

        @block.scalar
        def _(act):
            act.sem_inc(act_done, H0)
            nc.scalar.preload_act_table(func)
            for j, ep in expert_pairs(act, n):
                    act.wait_ge(loaded[ep], 16 * n_load * (j + 1))
                    with act.Fori(0, B // 2) as i:
                        for par in range(2):
                            s = 8 * (2 * j + ep) + 2 * i + par
                            act.wait_ge(y_done, s + 1)
                            for f in range(nf):
                                act.wait_ge(h_done, s * nf + f + 1)
                                bank = f if nf == 4 else par
                                o = act_h[par][:, :] if glu else h[par][:, f, :]
                                bias = dict(bias=b1t[ep][:, f:f + 1]) if b1 else {}
                                nc.scalar.activation(o, hps[bank][:, :], func, **bias).then_inc(act_done, 1)

        @block.vector
        def _(v):
            v.sem_inc(y_used, U0)
            if glu:
                v.sem_inc(glu_done, 2)
            for j, ep in expert_pairs(v, n):
                    e = 2 * j + ep

                    def product(c, par):
                        if glu:
                            v.wait_ge(act_done, H0 + 8 * e + c + 1)
                            nc.vector.tensor_tensor(h[par][:, 0, :], act_h[par][:, :], gps[par][:, :],
                                                    ALU.mult).then_inc(glu_done, 1)

                    def gather(c, par):
                        v.wait_ge(y_done, Y0 + 8 * e + c + 1)
                        for q in range(nb):
                            for k in range(TC):
                                xt = net.x[:, 4 * c + k, :]
                                last = nc.vector.scalar_tensor_tensor(
                                    xt, yps[par][:, k, q * P:(q + 1) * P], gate(4 * c + k, e, q), xt,
                                    ALU.mult, ALU.add)
                            if q == nb - 1:
                                last.then_inc(y_used, 1)
                            v.drain()

                    if glu:
                        one_chunk_ahead(v, product, gather)
                    else:
                        with v.Fori(0, B // 2) as i:
                            for par in range(2):
                                gather(2 * i + par, par)


def gated_bias(nc, net, tag, gate, b2):
    with ExitStack() as ctx:
        p = Scope(nc, ctx, tag + "_gb")
        gT = [p.sb(f"gT{i}", [32, P]) for i in range(2)]
        b2d = p.sb("b2d", [32, TC, D])
        tps = [p.ps(f"tps{i}") for i in range(2)]
        bps = [p.ps(f"bps{i}") for i in range(2)]
        loaded, zeroed, t_done, gT_done = p.sem("loaded"), p.sem("zeroed"), p.sem("t_done"), p.sem("gT_done")
        b_done, b_used = p.sem("b_done"), p.sem("b_used")
        block = ctx.enter_context(nc.Block())

        @block.gpsimd
        def _(pool):
            nc.gpsimd.memset(b2d[:, :, :], 0.0).then_inc(zeroed, 1)

        @block.sync
        def _(sp):
            sp.wait_ge(zeroed, 1)
            for k in range(TC):
                sp.dma_start(b2d[8 * k:8 * k + 8, k, :], b2).then_inc(loaded, 16)

        @block.tensor
        def _(pe):
            pe.wait_ge(loaded, 16 * TC)

            def turn(c):
                if c >= 2:
                    pe.wait_ge(gT_done, c - 1)
                nc.tensor.transpose(tps[c % 2][0:32, 0:P], gate[:, 4 * c:4 * c + 4, :].rearrange("p a b -> p (a b)"),
                                    net.ident[:, :]).then_inc(t_done, 1)

            turn(0)
            for c in range(B):
                if c + 1 < B:
                    turn(c + 1)
                pe.wait_ge(gT_done, c + 1)
                if c >= 2:
                    pe.wait_ge(b_used, c - 1)
                nc.tensor.matmul(bps[c % 2][:, :], gT[c % 2][:, :], b2d[:, :, :].rearrange("p a b -> p (a b)"),
                                 start=True, stop=True).then_inc(b_done, 1)

        @block.scalar
        def _(act):
            for c in range(B):
                act.wait_ge(t_done, c + 1)
                if c >= 2:
                    act.wait_ge(b_done, c - 1)
                nc.scalar.activation(gT[c % 2][:, :], tps[c % 2][0:32, 0:P], ACT.Copy).then_inc(gT_done, 1)

        @block.vector
        def _(v):
            for c in range(B):
                v.wait_ge(b_done, c + 1)
                xt = net.x[:, 4 * c:4 * c + 4, :].rearrange("p a b -> p (a b)")
                nc.vector.tensor_tensor(xt, xt, bps[c % 2][:, :], ALU.add).then_inc(b_used, 1)


def measure(nc, net, tag):
    with ExitStack() as ctx:
        p = Scope(nc, ctx, tag + "_st")
        bst = p.sb("bst", [P, NT, 6])
        block = ctx.enter_context(nc.Block())

        @block.vector
        def _(v):
            for t in range(NT):
                nc.vector.bn_stats(bst[:, t, :], net.x[:, t, :])
            v.drain()
            for t in range(NT):
                nc.vector.bn_aggr(net.stat[:, t, :], bst[:, t, :])


def normalise_and_route(nc, net, tag, w, E, lg, bias=None):
    with ExitStack() as ctx:
        p = Scope(nc, ctx, tag + "_nr")
        xn = [p.sb(f"xn{i}", [P, TC, D]) for i in range(2)]
        lT = [p.sb(f"lT{i}", [E, S]) for i in range(2)]
        std, wt, bt = p.sb("std", [P, NT]), p.sb("w", [P, E]), p.sb("b", [E, 1])
        tps, lps = ([p.ps(f"{n}{i}") for i in range(2)] for n in ("tps", "lps"))
        gps = [p.ps(f"gps{i}", [P, TC, E]) for i in range(2)]
        loaded, std_done = p.sem("loaded"), p.sem("std_done")
        xn_done, t_done, xT_done = p.sem("xn_done"), p.sem("t_done"), p.sem("xT_done")
        l_done, lT_done = p.sem("l_done"), p.sem("lT_done")
        g_done, lg_done = p.sem("g_done"), p.sem("lg_done")
        block = ctx.enter_context(nc.Block())
        n_loaded = 16 * (1 + (bias is not None))

        def wait(eng, sem, n):
            if n > 0:
                eng.wait_ge(sem, n)

        def side_by_side(*stages):
            for c in range(-3, B):
                for f, k in stages:
                    if 0 <= c + k < B:
                        f(c + k)

        @block.sync
        def _(sp):
            sp.dma_start(wt[:, :], w).then_inc(loaded, 16)
            if bias is not None:
                sp.dma_start(bt[:, :], col(bias)).then_inc(loaded, 16)

        @block.vector
        def _(v):
            v.wait_ge(std_done, 1)
            nc.vector.reciprocal(net.rstd[:, :], std[:, :])
            v.drain()

            def norm(c):
                wait(v, t_done, c - 1)
                for k in range(TC):
                    t = TC * c + k
                    last = nc.vector.tensor_scalar(xn[c % 2][:, k, :], net.x[:, t, :], net.stat[:, t, 0:1],
                                                   net.rstd[:, t:t + 1], ALU.subtract, ALU.mult)
                last.then_inc(xn_done, 1)

            def take_logits(c):
                v.wait_ge(g_done, c + 1)
                nc.vector.tensor_copy(lg[:, TC * c:TC * c + TC, :], gps[c % 2][:, :, :]).then_inc(lg_done, 1)

            side_by_side((norm, 3), (take_logits, 0))

        @block.tensor
        def _(pe):
            pe.wait_ge(loaded, n_loaded)

            def turn(c):
                pe.wait_ge(xn_done, c + 1)
                wait(pe, xT_done, c - 1)
                for k in range(TC):
                    last = nc.tensor.transpose(tps[c % 2][:, k * P:(k + 1) * P], xn[c % 2][:, k, :], net.ident[:, :])
                last.then_inc(t_done, 1)

            def logits(c):
                pe.wait_ge(xT_done, c + 1)
                wait(pe, lT_done, c - 1)
                nc.tensor.matmul(lps[c % 2][0:E, :], wt[:, :], net.xT[:, c * S:(c + 1) * S],
                                 start=True, stop=True).then_inc(l_done, 1)

            def turn_logits(c):
                pe.wait_ge(lT_done, c + 1)
                wait(pe, lg_done, c - 1)
                for k in range(TC):
                    last = nc.tensor.transpose(gps[c % 2][:, k, :], lT[c % 2][:, k * P:(k + 1) * P], net.ident[0:E, 0:E])
                last.then_inc(g_done, 1)

            side_by_side((turn, 2), (logits, 1), (turn_logits, 0))

        @block.scalar
        def _(act):
            nc.scalar.activation(std[:, :], net.stat[:, :, 1], ACT.Sqrt, bias=net.epst[:, 0:1]).then_inc(std_done, 1)
            act.wait_ge(loaded, n_loaded)

            def copy_tokens(c):
                act.wait_ge(t_done, c + 1)
                nc.scalar.activation(net.xT[:, c * S:(c + 1) * S], tps[c % 2][:, :], ACT.Copy).then_inc(xT_done, 1)

            def copy_logits(c):
                act.wait_ge(l_done, c + 1)
                wait(act, g_done, c - 1)
                kw = {} if bias is None else dict(bias=bt[:, :])
                nc.scalar.activation(lT[c % 2][:, :], lps[c % 2][0:E, :], ACT.Identity, **kw).then_inc(lT_done, 1)

            side_by_side((copy_tokens, 2), (copy_logits, 1))


def router_logits(nc, net, tag, w, E, lg, bias=None):
    with ExitStack() as ctx:
        p = Scope(nc, ctx, tag + "_rl")
        lT = [p.sb(f"lT{i}", [E, S]) for i in range(2)]
        wt = p.sb("w", [P, E])
        bt = p.sb("b", [E, 1])
        lps = [p.ps(f"lps{i}") for i in range(2)]
        tps = [p.ps(f"tps{i}", [P, TC, E]) for i in range(2)]
        parts = w if isinstance(w, tuple) else (w,)
        n_loaded = 16 * (len(parts) + (bias is not None))
        loaded, l_done, lT_done, t_done, lg_done = (p.sem(n) for n in ("loaded", "l_done", "lT_done", "t_done", "lg_done"))
        block = ctx.enter_context(nc.Block())

        @block.sync
        def _(sp):
            for i, part in enumerate(parts):
                n = E // len(parts)
                sp.dma_start(wt[:, i * n:(i + 1) * n], part).then_inc(loaded, 16)
            if bias is not None:
                sp.dma_start(bt[:, :], col(bias)).then_inc(loaded, 16)

        @block.tensor
        def _(pe):
            pe.wait_ge(loaded, n_loaded)

            def logits(c, par):
                if isinstance(c, int) and c < 2:
                    pass
                else:
                    pe.wait_ge(lT_done, c - 1)
                nc.tensor.matmul(lps[par][0:E, :], wt[:, :], net.xT[:, bass.ts(c, S)],
                                 start=True, stop=True).then_inc(l_done, 1)

            def turn(c, par):
                pe.wait_ge(lT_done, c + 1)
                if not (isinstance(c, int) and c < 2):
                    pe.wait_ge(lg_done, c - 1)
                for k in range(TC):
                    last = nc.tensor.transpose(tps[par][:, k, :], lT[par][:, k * P:(k + 1) * P], net.ident[0:E, 0:E])
                last.then_inc(t_done, 1)

            for c in range(2):
                logits(c, c)
            for c in range(B):
                turn(c, c % 2)
                if c + 2 < B:
                    logits(c + 2, c % 2)

        @block.scalar
        def _(act):
            act.wait_ge(loaded, n_loaded)
            for c in range(B):
                act.wait_ge(l_done, c + 1)
                if c >= 2:
                    act.wait_ge(t_done, c - 1)
                kw = {} if bias is None else dict(bias=bt[:, :])
                nc.scalar.activation(lT[c % 2][:, :], lps[c % 2][0:E, :], ACT.Identity, **kw).then_inc(lT_done, 1)

        @block.vector
        def _(v):
            for c in range(B):
                v.wait_ge(t_done, c + 1)
                nc.vector.tensor_copy(lg[:, 4 * c:4 * c + 4, :], tps[c % 2][:, :, :]).then_inc(lg_done, 1)


def bcast(ap, n):
    return ap.unsqueeze(len(ap.shape)).to_broadcast(list(ap.shape) + [n])


def first_best(nc, v, lg, m, eq, idx, onehot, iota, E):
    nc.vector.tensor_reduce(m[:, :], lg[:, :, :], AX.X, ALU.max)
    v.drain()
    nc.vector.tensor_tensor(eq[:, :, :], lg[:, :, :], bcast(m[:, :], E), ALU.is_equal)
    v.drain()
    nc.vector.scalar_tensor_tensor(eq[:, :, :], eq[:, :, :], float(-E), iota[:, :, :], ALU.mult, ALU.add)
    v.drain()
    nc.vector.tensor_reduce(idx[:, :], eq[:, :, :], AX.X, ALU.min)
    v.drain()
    nc.vector.tensor_tensor(onehot[:, :, :], eq[:, :, :], bcast(idx[:, :], E), ALU.is_equal)
    v.drain()


class Router:

    def __init__(self, nc, ctx, tag, E):
        p = Scope(nc, ctx, tag)
        self.E = E
        self.lg, self.eq, self.oh = p.sb("lg", [P, NT, E]), p.sb("eq", [P, NT, E]), p.sb("onehot", [P, NT, E])
        self.gate, self.iota = p.sb("gate", [P, NT, E]), p.sb("iota", [P, NT, E])
        self.m, self.idx, self.prob = p.sb("m", [P, NT]), p.sb("idx", [P, NT]), p.sb("prob", [P, NT])


def top1_prob(nc, r, tag):
    with ExitStack() as ctx:
        p = Scope(nc, ctx, tag + "_t1")
        iota_done, shifted, exped = p.sem("iota_done"), p.sem("shifted"), p.sem("exped")
        sh = p.sb("sh", [P, NT, r.E])
        block = ctx.enter_context(nc.Block())

        @block.gpsimd
        def _(pool):
            nc.gpsimd.iota(r.iota[:, :, :], pattern=[[0, NT], [1, r.E]], base=0, channel_multiplier=0,
                           allow_small_or_imprecise_dtypes=True).then_inc(iota_done, 1)

        @block.scalar
        def _(act):
            act.wait_ge(shifted, 1)
            nc.scalar.activation(sh[:, :, :], sh[:, :, :], ACT.Exp).then_inc(exped, 1)

        @block.vector
        def _(v):
            v.wait_ge(iota_done, 1)
            first_best(nc, v, r.lg, r.m, r.eq, r.idx, r.oh, r.iota, r.E)
            nc.vector.tensor_tensor(sh[:, :, :], r.lg[:, :, :], bcast(r.m[:, :], r.E), ALU.subtract).then_inc(shifted, 1)
            v.wait_ge(exped, 1)
            nc.vector.tensor_reduce(r.idx[:, :], sh[:, :, :], AX.X, ALU.add)
            v.drain()
            nc.vector.reciprocal(r.prob[:, :], r.idx[:, :])


def over_tiles(v, n):
    return v.unsqueeze(1).to_broadcast([v.shape[0], n, v.shape[1]])


def prefix_steps(nc, p, E):
    tri = p.sb("tri", [P, P])
    tot, scan, one = p.sb("tot", [P, NT, E]), p.sb("scan", [P, NT, E]), p.sb("one", [P, NT])
    wps, tps = p.ps("wps", [P, NT, E]), p.ps("tps", [P, NT, E])
    tri_zeroed, tri_ready = p.sem("tri_zeroed"), p.sem("tri_ready")
    mask_ready, counted = p.sem("mask_ready"), p.sem("counted")

    def on_pool(pool):
        nc.gpsimd.memset(tri[:, :], 1.0)
        nc.gpsimd.memset(one[:, :], 1.0).then_inc(tri_zeroed, 1)
        pool.wait_ge(tri_zeroed, 1)
        nc.gpsimd.affine_select(out=tri[:, :], in_=tri[:, :], compare_op=ALU.is_ge, fill=0.0,
                                base=-1, pattern=[[1, P]], channel_multiplier=-1).then_inc(tri_ready, 1)

    def on_tensor(pe, net, mask):
        pe.wait_ge(tri_ready, 1)
        pe.wait_ge(mask_ready, 1)
        flat = mask.rearrange("p t e -> p (t e)")
        nc.tensor.matmul(wps[:, :, :].rearrange("p t e -> p (t e)"), tri[:, :], flat, start=True, stop=True)
        nc.tensor.matmul(tps[:, :, :].rearrange("p t e -> p (t e)"), net.ones[:, :], flat,
                         start=True, stop=True).then_inc(counted, 1)

    def on_vector(v, loc, total=None):
        v.drain()
        v.sem_inc(mask_ready, 1)
        v.wait_ge(tri_ready, 1)
        v.wait_ge(counted, 1)
        nc.vector.tensor_copy(tot[:, :, :], tps[:, :, :])
        v.drain()
        for e in range(E):
            nc.vector.tensor_tensor_scan(scan[:, :, e], one[:, :], tot[:, :, e], 0.0, ALU.mult, ALU.add)
        v.drain()
        if total is not None:
            nc.vector.tensor_copy(total, scan[:, NT - 1, :])
            v.drain()
        nc.vector.tensor_tensor(scan[:, :, :], scan[:, :, :], tot[:, :, :], ALU.subtract)
        v.drain()
        nc.vector.tensor_tensor(loc, scan[:, :, :], wps[:, :, :], ALU.add)
        v.drain()

    return on_pool, on_tensor, on_vector


def capacity_by_probability(nc, net, r, cap, tag):
    E = r.E
    steps = 28
    with ExitStack() as ctx:
        p = Scope(nc, ctx, tag + "_cap")
        key, cmp = p.sb("key", [P, NT, E]), p.sb("cmp", [P, NT, E])
        gt, loc = p.sb("gt", [P, NT, E]), p.sb("loc", [P, NT, E])
        t, cand, part, take = (p.sb(n, [P, E]) for n in ("t", "cand", "part", "take"))
        step, drop = p.sb("step", [P, 1]), p.sb("drop", [P, NT])
        cps = p.ps("cps", [P, E])
        part_done, total_done = p.sem("part_done"), p.sem("total_done")
        on_pool, on_tensor, on_vector = prefix_steps(nc, p, E)
        block = ctx.enter_context(nc.Block())

        @block.gpsimd
        def _(pool):
            on_pool(pool)

        @block.tensor
        def _(pe):
            with pe.Fori(0, steps + 1) as i:
                pe.wait_ge(part_done, i + 1)
                nc.tensor.matmul(cps[:, :], net.ones[:, :], part[:, :], start=True, stop=True).then_inc(total_done, 1)
            on_tensor(pe, net, r.eq[:, :, :])

        @block.vector
        def _(v):
            def count(op, thr):
                nc.vector.tensor_tensor(cmp[:, :, :], key[:, :, :], over_tiles(thr, NT), op)
                v.drain()
                nc.vector.tensor_reduce(part[:, :], cmp[:, :, :].rearrange("p t e -> p e t"),
                                        AX.X, ALU.add).then_inc(part_done, 1)

            nc.vector.memset(t[:, :], 0.0)
            nc.vector.memset(step[:, :], 1.0)
            nc.vector.tensor_tensor(key[:, :, :], r.oh[:, :, :], bcast(r.prob[:, :], E), ALU.mult)
            v.drain()
            with v.Fori(0, steps) as i:
                nc.vector.tensor_scalar(cand[:, :], t[:, :], step[:, :], None, ALU.add)
                v.drain()
                count(ALU.is_ge, cand[:, :])
                v.wait_ge(total_done, i + 1)
                nc.vector.tensor_scalar(take[:, :], cps[:, :], float(cap), None, ALU.is_ge)
                v.drain()
                nc.vector.tensor_tensor(cand[:, :], cand[:, :], t[:, :], ALU.subtract)
                nc.vector.tensor_scalar(step[:, :], step[:, :], 0.5, None, ALU.mult)
                v.drain()
                nc.vector.tensor_tensor(take[:, :], take[:, :], cand[:, :], ALU.mult)
                v.drain()
                nc.vector.tensor_tensor(t[:, :], t[:, :], take[:, :], ALU.add)
                v.drain()
            count(ALU.is_gt, t[:, :])
            v.wait_ge(total_done, steps + 1)
            nc.vector.tensor_copy(gt[:, :, :], cmp[:, :, :])
            nc.vector.tensor_tensor(r.eq[:, :, :], key[:, :, :], over_tiles(t[:, :], NT), ALU.is_equal)
            nc.vector.tensor_scalar(take[:, :], cps[:, :], -1.0, float(cap), ALU.mult, ALU.add)
            on_vector(v, loc[:, :, :])
            nc.vector.tensor_tensor(cmp[:, :, :], loc[:, :, :], over_tiles(take[:, :], NT), ALU.is_lt)
            v.drain()
            nc.vector.tensor_tensor(cmp[:, :, :], cmp[:, :, :], r.eq[:, :, :], ALU.mult)
            v.drain()
            nc.vector.tensor_tensor(cmp[:, :, :], cmp[:, :, :], gt[:, :, :], ALU.add)
            v.drain()
            nc.vector.tensor_tensor(r.gate[:, :, :], cmp[:, :, :], r.oh[:, :, :], ALU.mult)
            v.drain()
            nc.vector.tensor_reduce(drop[:, :], r.gate[:, :, :], AX.X, ALU.add)
            v.drain()
            nc.vector.tensor_scalar(drop[:, :], drop[:, :], -1.0, 1.0, ALU.mult, ALU.add)
            v.drain()
            nc.vector.tensor_tensor(r.gate[:, :, 0], r.gate[:, :, 0], drop[:, :], ALU.add)


def capacity_by_order(nc, net, r, cap, tag):
    E = r.E
    with ExitStack() as ctx:
        p = Scope(nc, ctx, tag + "_cap")
        loc = p.sb("loc", [P, NT, E])
        on_pool, on_tensor, on_vector = prefix_steps(nc, p, E)
        block = ctx.enter_context(nc.Block())

        @block.gpsimd
        def _(pool):
            on_pool(pool)

        @block.tensor
        def _(pe):
            on_tensor(pe, net, r.oh[:, :, :])

        @block.vector
        def _(v):
            on_vector(v, loc[:, :, :])
            nc.vector.tensor_scalar(loc[:, :, :], loc[:, :, :], float(cap), None, ALU.is_lt)
            v.drain()
            nc.vector.tensor_tensor(loc[:, :, :], loc[:, :, :], r.oh[:, :, :], ALU.mult)
            v.drain()
            nc.vector.tensor_tensor(r.gate[:, :, :], loc[:, :, :], bcast(r.prob[:, :], E), ALU.mult)


def split3(nc, eng, e, src, dst, rest, drain):
    e.tensor_copy(dst[0], src)
    drain()
    e.tensor_tensor(rest, src, dst[0], ALU.subtract)
    drain()
    e.tensor_copy(dst[1], rest)
    drain()
    e.tensor_tensor(rest, rest, dst[1], ALU.subtract)
    drain()
    return e.tensor_copy(dst[2], rest)


Q_PARTS = (0, 0, 0, 1, 1, 2)
K_PARTS = ((0, 3), (3, 2), (5, 1))


def relative_attention(nc, net, d):
    a = lambda n: d[f"L0_attn_{n}"]
    HD, NH = a("w_rel").shape
    qd, kd = (nc.dram_tensor(n, (3, P, B * S), BF, kind="Internal").ap() for n in ("q_parts", "k_parts"))
    ad = nc.dram_tensor("rel_q_parts", (3, P, S), BF, kind="Internal").ap()
    td = nc.dram_tensor("rel_k_parts", (3, HD, S), BF, kind="Internal").ap()
    with ExitStack() as ctx:
        operands = Scope(nc, ctx, "a0o")
        Q, K = operands.sb("Q", [P, 2 * NH, S], BF), operands.sb("K", [P, 2 * NH, S], BF)
        V = operands.sb("V", [P, NT, NH, HD + 1])
        with ExitStack() as part:
            h = Scope(nc, part, "a0h").sb("h", [P, NT, D])
            token_rstd(nc, net, "a0")
            prepare(nc, net, d, a, HD, NH, h, K, 2 * len(Q_PARTS) * HD, ad, td)
            normalise(nc, net, "a0", src=h, g=a("ln_g"), b=a("ln_b"))
        project_parts(nc, net, a, HD, NH, V, qd, kd, Q, K, ad, td)
        heads(nc, net, a, HD, NH, V, qd, kd, Q, K)
    measure(nc, net, "a0")


def prepare(nc, net, d, a, HD, NH, h, K, first_one, ad, td):
    with ExitStack() as ctx:
        p = Scope(nc, ctx, "a0n")
        bst = p.sb("bst", [P, NT, 6])
        t, m1, m2 = p.sb("t", [HD, S]), p.sb("m1", [HD, HD]), p.sb("m2", [HD, HD])
        wr, ws = p.sb("wr", [HD, NH]), p.sb("ws", [HD, NH])
        L, L2 = p.sb("L", [HD, HD, NH]), p.sb("L2", [HD, HD, NH])
        qf, qp, kp = p.sb("qf", [P, S]), p.sb("qp", [P, 3, S], BF), p.sb("kp", [HD, 3, S], BF)
        rest = p.sb("rest", [P, S])
        ps = p.ps("ps")
        loaded, L_done, q_done, split_done, stored = (p.sem(n) for n in ("loaded", "L_done", "q_done", "split_done", "stored"))
        block = ctx.enter_context(nc.Block())

        @block.sync
        def _(sp):
            for dst, src in ((t, d["rel_t"]), (m1, d["rel_m1"]), (m2, d["rel_m2"]), (wr, a("w_rel"))):
                sp.dma_start(dst[:, :], src).then_inc(loaded, 16)
            for r in range(HD):
                sp.dma_start(ws[r:r + 1, :], a("w_rel")[r ^ 1:(r ^ 1) + 1, :]).then_inc(loaded, 16)
            sp.wait_ge(split_done, 1)
            sp.dma_start(td.rearrange("s r n -> r s n"), kp[:, :, :]).then_inc(stored, 16)
            sp.wait_ge(split_done, 2)
            sp.dma_start(ad.rearrange("s p n -> p s n"), qp[:, :, :]).then_inc(stored, 16)
            sp.wait_ge(stored, 32)

        @block.gpsimd
        def _(pool):
            nc.gpsimd.memset(K[first_one:P, :, :], 1.0)

        @block.tensor
        def _(pe):
            pe.wait_ge(L_done, 1)
            nc.tensor.matmul(ps[:, :], L[:, :, :].rearrange("a r h -> a (r h)"), t[:, :], start=True, stop=True).then_inc(q_done, 1)

        @block.vector
        def _(v):
            for k in range(NT):
                nc.vector.tensor_scalar(h[:, k, :], net.x[:, k, :], net.stat[:, k, 0:1], net.rstd[:, k:k + 1],
                                        ALU.subtract, ALU.mult)
            v.wait_ge(loaded, 16 * (4 + HD))
            nc.vector.tensor_tensor(L[:, :, :], over_tiles(wr[:, :], HD), bcast(m1[:, :], NH), ALU.mult)
            nc.vector.tensor_tensor(L2[:, :, :], over_tiles(ws[:, :], HD), bcast(m2[:, :], NH), ALU.mult)
            v.drain()
            nc.vector.tensor_tensor(L[:, :, :], L[:, :, :], L2[:, :, :], ALU.add).then_inc(L_done, 1)
            split3(nc, v, nc.vector, t[:, :], [kp[:, s, :] for s in range(3)], rest[0:HD, :], v.drain).then_inc(split_done, 1)
            v.wait_ge(q_done, 1)
            nc.vector.tensor_copy(qf[:, :], ps[:, :])
            v.drain()
            split3(nc, v, nc.vector, qf[:, :], [qp[:, s, :] for s in range(3)], rest[:, :], v.drain).then_inc(split_done, 1)
            for k in range(NT):
                nc.vector.bn_stats(bst[:, k, :], h[:, k, :])
            v.drain()
            for k in range(NT):
                nc.vector.bn_aggr(net.stat[:, k, :], bst[:, k, :])


def project_parts(nc, net, a, HD, NH, V, qd, kd, Q, K, ad, td):
    with ExitStack() as ctx:
        p = Scope(nc, ctx, "a0p")
        w, bv = p.sb("w", [P, 3, P]), p.sb("bv", [P, P])
        bias, tick = p.sb("bias", [P, 2]), p.sb("tick", [P, 2])
        f = [[p.sb(f"f{t}{i}", [P, S]) for i in range(2)] for t in "qk"]
        parts = [[p.sb(f"parts{t}{i}", [P, 3, S], BF) for i in range(2)] for t in "qk"]
        rest = [p.sb(f"rest{t}", [P, S]) for t in "qk"]
        xc = [p.sb(f"xc{i}", [P, S]) for i in range(2)]
        qkps = [[p.ps(f"ps{t}{i}") for i in range(2)] for t in "qk"]
        vps = [p.ps(f"vps{i}") for i in range(2)]
        loaded, k_split, xc_done, pj_ready, f_done, v_done = (
            p.sem(n) for n in ("loaded", "k_split", "xc_done", "pj_ready", "f_done", "v_done"))
        rel_loaded = p.sem("rel_loaded")
        split_done = [p.sem(f"split_{t}") for t in "qk"]
        stored = [[p.sem(f"stored_{t}{i}") for i in range(2)] for t in "qk"]
        block = ctx.enter_context(nc.Block())
        scale = HD ** -0.5

        @block.sync
        def _(sp):
            sp.dma_start(w[:, :, :], a("w_qkv")).then_inc(loaded, 16)
            for t in range(2):
                sp.dma_start(bias[:, t:t + 1], col(a("b_qkv")[t, :])).then_inc(loaded, 16)
            sp.dma_start(bv[:, :], row(a("b_qkv")[2, :]).to_broadcast([P, P])).then_inc(loaded, 16)
            REL = len(Q_PARTS) * HD
            for par in range(2):
                hh = slice(par * NH, (par + 1) * NH)
                for n, s in enumerate(Q_PARTS):
                    sp.dma_start(Q[REL + n * HD:REL + (n + 1) * HD, hh, :],
                                 ad[s, :, :].rearrange("(r h) n -> r h n", h=NH)).then_inc(rel_loaded, 16)
                for first, s in K_PARTS:
                    src = td[0:s, :, :].rearrange("s r n -> (s r) n")
                    sp.dma_start(K[REL + first * HD:REL + (first + s) * HD, hh, :],
                                 over_tiles(src, NH)).then_inc(rel_loaded, 16)
            for t in range(2):
                for par in range(2):
                    sp.sem_inc(stored[t][par], 16)
            with sp.Fori(0, B // 2) as i:
                for par in range(2):
                    c = 2 * i + par
                    for t, dst in enumerate((qd, kd)):
                        sp.wait_ge(split_done[t], c + 1)
                        sp.dma_start(dst[:, :, bass.ts(c, S)].rearrange("s p n -> p s n"),
                                     parts[t][par][:, :, :]).then_inc(stored[t][par], 16)
            for t in range(2):
                for par in range(2):
                    sp.wait_ge(stored[t][par], 16 + 16 * (B // 2))
            sp.wait_ge(rel_loaded, 32 * (len(Q_PARTS) + len(K_PARTS)))

        @block.tensor
        def _(pe):
            pe.wait_ge(loaded, 64)
            pe.sem_inc(pj_ready, 2)
            with pe.Fori(0, B // 2) as i:
                for par in range(2):
                    c = 2 * i + par
                    pe.wait_ge(f_done, c + 1)
                    for t in range(2):
                        nc.tensor.matmul(qkps[t][par][:, :], w[:, t, :], net.xT[:, bass.ts(c, S)], start=True, stop=True)
                    pe.wait_ge(xc_done, c + 1)
                    pe.wait_ge(v_done, c + 1)
                    for k in range(TC):
                        last = nc.tensor.matmul(vps[par][:, k * P:(k + 1) * P], xc[par][:, k * P:(k + 1) * P], w[:, 2, :],
                                                start=True, stop=True)
                    last.then_inc(pj_ready, 1)

        @block.scalar
        def _(act):
            act.wait_ge(loaded, 64)
            nc.scalar.activation(bias[:, 0:1], bias[:, 0:1], ACT.Copy, scale=scale)
            act.drain()
            act.sem_inc(f_done, 2)
            with act.Fori(0, B // 2) as i:
                for par in range(2):
                    c = 2 * i + par
                    act.wait_ge(pj_ready, c + 1)
                    nc.scalar.activation(xc[par][:, :], net.xT[:, bass.ts(c, S)], ACT.Copy).then_inc(xc_done, 1)
                    act.wait_ge(pj_ready, c + 3)
                    act.wait_ge(v_done, c + 1)
                    act.wait_ge(k_split, c + 1)
                    nc.scalar.activation(f[0][par][:, :], qkps[0][par][:, :], ACT.Identity, bias=bias[:, 0:1], scale=scale)
                    nc.scalar.activation(f[1][par][:, :], qkps[1][par][:, :], ACT.Identity, bias=bias[:, 1:2]).then_inc(f_done, 1)

        @block.vector
        def _(v):
            nc.vector.memset(V[:, :, :, HD:HD + 1], 1.0)
            v.wait_ge(loaded, 64)
            v.sem_inc(v_done, 2)
            with v.Fori(0, B // 2) as i:
                for par in range(2):
                    c = 2 * i + par
                    v.wait_ge(f_done, c + 3)
                    v.wait_ge(stored[0][par], 16 * i + 16)
                    split3(nc, v, nc.vector, f[0][par][:, :], [parts[0][par][:, s, :] for s in range(3)],
                           rest[0][:, :], v.drain).then_inc(split_done[0], 1)
                    for k in range(TC):
                        last = nc.vector.tensor_tensor(V[:, 4 * c + k, :, 0:HD],
                                                       vps[par][:, k * P:(k + 1) * P].rearrange("p (h d) -> p h d", d=HD),
                                                       bv[:, :].rearrange("p (h d) -> p h d", d=HD), ALU.add)
                    last.then_inc(v_done, 1)

        @block.gpsimd
        def _(pool):
            pool.sem_inc(k_split, 2)
            nc.gpsimd.memset(tick[:, :], 1.0)
            pool.drain()
            with pool.Fori(0, B // 2) as i:
                for par in range(2):
                    c = 2 * i + par
                    pool.wait_ge(f_done, c + 3)
                    pool.wait_ge(stored[1][par], 16 * i + 16)
                    nc.gpsimd.tensor_tensor(tick[:, 1:2], tick[:, 0:1], tick[:, 0:1], ALU.mult)
                    split3(nc, pool, nc.gpsimd, f[1][par][:, :], [parts[1][par][:, s, :] for s in range(3)],
                           rest[1][:, :], pool.drain).then_inc(split_done[1], 1)
                    pool.drain()
                    pool.sem_inc(k_split, 1)


def heads(nc, net, a, HD, NH, V, qd, kd, Q, K):
    GH = 4
    NG = NH // GH
    NQ = len(Q_PARTS)
    DYN, MAX = 0, 2 * NQ * HD
    KB = MAX + 3
    NS = TC * GH
    SLOTS = NS + 1
    LQ = 16 * (NQ + 3)
    with ExitStack() as ctx:
        p = Scope(nc, ctx, "a0")
        prob = [p.sb(f"prob{i}", [P, GH, TC, S]) for i in range(2)]
        Vg = [p.sb(f"Vg{i}", [P, TC, GH, 32]) for i in range(2)]
        OT = [p.sb(f"OT{i}", [P, S]) for i in range(2)]
        nm = [p.sb(f"nm{i}", [P, NS]) for i in range(2)]
        mr, ms = [p.sb(f"mr{i}", [NS, P]) for i in range(2)], [p.sb(f"ms{i}", [NS, 3, P], BF) for i in range(2)]
        mrest = p.sb("mrest", [NS, P])
        den, O, OTn = p.sb("den", [P, TC, GH]), p.sb("O", [P, TC, NH * HD]), p.sb("OTn", [P, S])
        wo, bo, one = p.sb("wo", [P, D]), p.sb("bo", [P, D]), p.sb("one", [P, 2])
        aps = [p.ps(f"aps{i}") for i in range(2)]
        sps = [p.ps(f"sps{i}", [P, 2, S]) for i in range(2)]
        ops, mps = p.ps("ops"), p.ps("mps")
        w_loaded, bias_added = p.sem("w_loaded"), p.sem("bias_added")
        qk_loaded = [p.sem(f"qk_loaded{i}") for i in range(2)]
        max_loaded = [p.sem(f"max_loaded{i}") for i in range(2)]
        a_ready = p.sem("a_ready")
        a_used = p.sem("a_used")
        ms_done = p.sem("ms_done")
        s_ready = p.sem("s_ready")
        p_done = p.sem("p_done")
        vg_ready = p.sem("vg_ready")
        av_done = p.sem("av_done")
        ot_copied = p.sem("ot_copied")
        ott_done = p.sem("ott_done")
        o_done = p.sem("o_done")
        on_turned = p.sem("on_turned")
        otn_done = p.sem("otn_done")
        y_done = p.sem("y_done")
        y_added = p.sem("y_added")
        block = ctx.enter_context(nc.Block())

        def wait(eng, sem, n):
            if not isinstance(n, int) or n > 0:
                eng.wait_ge(sem, n)

        def sequences(eng, body):
            body(0)
            with eng.Fori(1, B - 1) as b:
                body(b)
            body(B - 1)

        has = lambda n: not isinstance(n, int) or n >= 0
        more = lambda b: not isinstance(b, int) or b < B - 1
        row0 = lambda b, g: (b % 2) * NH + GH * g

        @block.sync
        def _(sp):
            qv = qd.rearrange("s (r h) n -> s r h n", h=NH)
            kv = kd.rearrange("s (r h) n -> s r h n", h=NH)

            def load(b, g):
                hs = bass.ds(row0(b, g), GH)
                for n, s in enumerate(Q_PARTS):
                    sp.dma_start(Q[DYN + n * HD:DYN + (n + 1) * HD, hs, :],
                                 qv[s, :, GH * g:GH * (g + 1), bass.ts(b, S)]).then_inc(qk_loaded[g % 2], 16)
                for first, s in K_PARTS:
                    sp.dma_start(K[DYN + first * HD:DYN + (first + s) * HD, hs, :],
                                 kv[0:s, :, GH * g:GH * (g + 1), bass.ts(b, S)].rearrange("s r h n -> (s r) h n"))\
                      .then_inc(qk_loaded[g % 2], 16)

            def store_max(b, g):
                sp.wait_ge(ms_done, NG * b + g + 1)
                wait(sp, p_done, 8 * (NG * (b - 2) + g + 1))
                wait(sp, max_loaded[g % 2], 48 * (2 * b + g // 2))
                for s in range(3):
                    sp.dma_start(Q[MAX + s:MAX + s + 1, bass.ds(row0(b, g), GH), :].rearrange("o h (q t) -> o (h q) t", t=P),
                                 ms[g % 2][:, s, :]).then_inc(max_loaded[g % 2], 16)

            def next_loads(b):
                for g in range(NG):
                    if more(b):
                        store_max(b + 1, g)
                    if more(b) and more(b + 1):
                        sp.wait_ge(p_done, 8 * (NG * b + g + 1))
                        sp.wait_ge(qk_loaded[g % 2], LQ * (2 * (b + 2) + g // 2))
                        load(b + 2, g)

            load(0, 0)
            load(0, 1)
            sp.dma_start(wo[:, :], a("w_out")).then_inc(w_loaded, 16)
            sp.dma_start(bo[:, :], row(a("b_out")).to_broadcast([P, D])).then_inc(w_loaded, 16)
            for u in range(2, 2 * NG):
                sp.wait_ge(qk_loaded[u % 2], LQ * (u // 2))
                load(u // NG, u % NG)
            for g in range(NG):
                store_max(0, g)
            next_loads(0)
            with sp.Fori(1, B - 2) as b:
                next_loads(b)
            next_loads(B - 2)

        @block.gpsimd
        def _(pool):
            def split_maxima(b, g):
                m = NG * b + g
                pool.drain()
                pool.wait_ge(a_used, SLOTS * (m + 1))
                wait(pool, max_loaded[g % 2], 48 * (2 * b + g // 2))
                nc.gpsimd.tensor_tensor(one[:, 1:2], one[:, 0:1], one[:, 0:1], ALU.mult)
                split3(nc, pool, nc.gpsimd, mr[g % 2][:, :], [ms[g % 2][:, s, :] for s in range(3)],
                       mrest[:, :], pool.drain).then_inc(ms_done, 1)

            def unit_values(b, g):
                pool.drain()
                wait(pool, av_done, NG * b + g - 1)
                nc.gpsimd.tensor_tensor(one[:, 1:2], one[:, 0:1], one[:, 0:1], ALU.mult)
                for k in range(TC):
                    last = nc.gpsimd.tensor_copy(Vg[g % 2][:, k, :, 0:HD + 1], V[:, 4 * b + k, GH * g:GH * (g + 1), :])
                last.then_inc(vg_ready, 1)

            def body(b):
                for g in range(NG):
                    unit_values(b, g)
                    if more(b):
                        split_maxima(b + 1, g)

            nc.gpsimd.memset(one[:, :], 1.0)
            for i in range(2):
                nc.gpsimd.memset(Vg[i][:, :, :, :], 0.0)
            for g in range(NG):
                split_maxima(0, g)
            pool.wait_ge(w_loaded, 32)
            nc.gpsimd.tensor_tensor(net.x[:, :, :], net.x[:, :, :], over_tiles(bo[:, :], NT), ALU.add).then_inc(bias_added, 1)
            sequences(pool, body)

        @block.tensor
        def _(pe):
            def max_score(b, g, s):
                n = SLOTS * (NG * b + g) + s
                wait(pe, a_used, n - 1)
                j, q = s // TC, s % TC
                head = bass.ds(row0(b, g) + j, 1)
                nc.tensor.matmul(aps[(g + s) % 2][:, :],
                                 Q[0:MAX, head, q * P:(q + 1) * P].rearrange("k a n -> k (a n)"),
                                 K[0:MAX, head, :].rearrange("k a n -> k (a n)"), start=True, stop=True).then_inc(a_ready, 1)

            def turn_maxima(b, g):
                pe.wait_ge(a_used, SLOTS * (NG * b + g) + NS)
                nc.tensor.transpose(aps[(g + NS) % 2][0:NS, 0:P], nm[g % 2][:, :], net.ident[:, :]).then_inc(a_ready, 1)

            def key_scores(b, g, t):
                wait(pe, p_done, 8 * (NG * b + g) + t - 1)
                head = bass.ds(row0(b, g) + t // 2, 1)
                for i in range(2):
                    k = 2 * (t % 2) + i
                    last = nc.tensor.matmul(sps[t % 2][:, i, :],
                                            K[0:KB, head, k * P:(k + 1) * P].rearrange("k a n -> k (a n)"),
                                            Q[0:KB, head, :].rearrange("k a n -> k (a n)"), start=True, stop=True)
                last.then_inc(s_ready, 1)

            def values(u, gp, k):
                if k == 0:
                    pe.wait_ge(p_done, 8 * (u + 1))
                    pe.wait_ge(vg_ready, u + 1)
                    wait(pe, ot_copied, u)
                for j in range(GH):
                    last = nc.tensor.matmul(ops[32 * j:32 * j + 32, :], Vg[gp][:, k, j, :], prob[gp][:, j, k, :],
                                            start=(k == 0), stop=(k == TC - 1))
                if k == TC - 1:
                    last.then_inc(av_done, 1)

            def turn_outputs(u, b, gp):
                pe.wait_ge(ot_copied, u + 1)
                wait(pe, o_done, u)
                wait(pe, y_added, b)
                for q in range(TC):
                    last = nc.tensor.transpose(mps[:, q * P:(q + 1) * P], OT[gp][:, q * P:(q + 1) * P], net.ident[:, :])
                last.then_inc(ott_done, 1)

            def turn_sequence(b):
                pe.wait_ge(o_done, NG * (b + 1))
                for q in range(TC):
                    last = nc.tensor.transpose(mps[:, q * P:(q + 1) * P], O[:, q, :], net.ident[:, :])
                last.then_inc(on_turned, 1)

            def project(b):
                pe.wait_ge(otn_done, b + 1)
                for q in range(TC):
                    last = nc.tensor.matmul(mps[:, q * P:(q + 1) * P], OTn[:, q * P:(q + 1) * P], wo[:, :],
                                            start=True, stop=True)
                last.then_inc(y_done, 1)

            def unit(b, g):
                u = NG * b + g
                if more(b):
                    pe.wait_ge(qk_loaded[g % 2], LQ * (2 * (b + 1) + g // 2 + 1))
                for t in range(8):
                    if more(b):
                        max_score(b + 1, g, 2 * t)
                    if t == 0:
                        pe.wait_ge(max_loaded[g % 2], 48 * (2 * b + g // 2 + 1))
                    key_scores(b, g, t)
                    if more(b):
                        max_score(b + 1, g, 2 * t + 1)
                    if t == 0 and g == 2 and has(b - 1):
                        project(b - 1)
                    if t == 2 and has(u - 2):
                        turn_outputs(u - 2, b if g >= 2 else b - 1, g % 2)
                    if t == 6 and g == 1 and has(b - 1):
                        turn_sequence(b - 1)
                    if t % 2 == 1 and has(u - 1):
                        values(u - 1, (g + 1) % 2, t // 2)
                if more(b):
                    turn_maxima(b + 1, g)

            for g in range(NG):
                pe.wait_ge(qk_loaded[g % 2], LQ * (g // 2 + 1))
                for s in range(NS):
                    max_score(0, g, s)
                turn_maxima(0, g)
            pe.wait_ge(w_loaded, 32)
            sequences(pe, lambda b: [unit(b, g) for g in range(NG)])
            U = NG * B
            turn_outputs(U - 2, B - 1, 0)
            for k in range(TC):
                values(U - 1, 1, k)
            turn_outputs(U - 1, B - 1, 1)
            turn_sequence(B - 1)
            project(B - 1)

        @block.scalar
        def _(act):
            def copy_outputs(u, gp):
                act.wait_ge(av_done, u + 1)
                wait(act, ott_done, u - 1)
                nc.scalar.activation(OT[gp][:, :], ops[:, :], ACT.Copy).then_inc(ot_copied, 1)

            def copy_sequence(b):
                act.wait_ge(on_turned, b + 1)
                wait(act, y_done, b)
                nc.scalar.activation(OTn[:, :], mps[:, :], ACT.Copy).then_inc(otn_done, 1)

            def unit(b, g):
                u = NG * b + g
                wait(act, av_done, u - 1)
                for t in range(8):
                    act.wait_ge(s_ready, 8 * u + t + 1)
                    nc.scalar.activation(prob[g % 2][:, t // 2, 2 * (t % 2):2 * (t % 2) + 2, :].rearrange("p a b -> p (a b)"),
                                         sps[t % 2][:, :, :].rearrange("p a b -> p (a b)"), ACT.Exp).then_inc(p_done, 1)
                if g == 1 and has(b - 1):
                    copy_sequence(b - 1)
                if has(u - 1):
                    copy_outputs(u - 1, (g + 1) % 2)

            sequences(act, lambda b: [unit(b, g) for g in range(NG)])
            copy_outputs(NG * B - 1, 1)
            copy_sequence(B - 1)

        @block.vector
        def _(v):
            def maximum(b, g, s):
                v.wait_ge(a_ready, SLOTS * (NG * b + g) + s + 1)
                nc.vector.tensor_reduce(nm[g % 2][:, s:s + 1], aps[(g + s) % 2][:, :], AX.X, ALU.max, negate=True).then_inc(a_used, 1)

            def take_maxima(b, g):
                m = NG * b + g
                v.wait_ge(a_ready, SLOTS * (m + 1))
                wait(v, ms_done, m - 1)
                nc.vector.tensor_copy(mr[g % 2][:, :], aps[(g + NS) % 2][0:NS, 0:P]).then_inc(a_used, 1)

            def outputs(u, b, g):
                v.drain()
                v.wait_ge(ott_done, u + 1)
                if g == 0:
                    wait(v, on_turned, b)
                m = mps[:, :].rearrange("p (q j e) -> p q j e", q=TC, j=GH)
                nc.vector.reciprocal(den[:, :, :], m[:, :, :, HD])
                v.drain()
                for q in range(TC):
                    last = nc.vector.tensor_tensor(O[:, q, GH * HD * g:GH * HD * (g + 1)].rearrange("p (j e) -> p j e", e=HD),
                                                   m[:, q, :, 0:HD], bcast(den[:, q, :], HD), ALU.mult)
                last.then_inc(o_done, 1)

            def add_output(b):
                v.wait_ge(y_done, b + 1)
                xt = net.x[:, bass.ts(b, 4), :].rearrange("p a b -> p (a b)")
                nc.vector.tensor_tensor(xt, xt, mps[:, :], ALU.add).then_inc(y_added, 1)

            def unit(b, g):
                u = NG * b + g
                for s in range(NS):
                    if more(b):
                        maximum(b + 1, g, s)
                    if s == 1 and g == 2 and has(b - 1):
                        add_output(b - 1)
                    if s == 8 and has(u - 2):
                        outputs(u - 2, b if g >= 2 else b - 1, (g + 2) % NG)
                if more(b):
                    take_maxima(b + 1, g)

            for g in range(NG):
                for s in range(NS):
                    maximum(0, g, s)
                take_maxima(0, g)
            v.wait_ge(bias_added, 1)
            sequences(v, lambda b: [unit(b, g) for g in range(NG)])
            outputs(NG * B - 2, B - 1, NG - 2)
            outputs(NG * B - 1, B - 1, NG - 1)
            add_output(B - 1)


def dispatch(nc, net, gate, E, n_tiles, pos, expert_of, zeros, xs, ws):
    with ExitStack() as ctx:
        p = Scope(nc, ctx, "m0d")
        loc, f = p.sb("loc", [P, NT, E]), p.sb("f", [P, NT])
        total, start, width, unit = (p.sb(n, [P, E]) for n in ("total", "start", "width", "unit"))
        step, above = p.sb("step", [P, NT]), p.sb("above", [P, E, NT])
        tile, past, ef = p.sb("tile", [1, n_tiles]), p.sb("past", [1, n_tiles, E]), p.sb("ef", [1, n_tiles])
        made, moved = p.sem("made"), p.sem("moved")
        sums = p.sb("sums", [P, NT, E])
        on_pool, on_tensor, on_vector = prefix_steps(nc, p, E)
        block = ctx.enter_context(nc.Block())

        @block.sync
        def _(sp):
            sp.wait_ge(made, 1)
            sp.dma_start(xs.rearrange("(t p) d -> p t d", p=P), over_tiles(zeros[:, :], n_tiles)).then_inc(moved, 16)
            for dst, src in ws:
                sp.dma_start(dst, src).then_inc(moved, 16)
            sp.wait_ge(moved, 16 * (1 + len(ws)))

        @block.gpsimd
        def _(pool):
            nc.gpsimd.memset(zeros[:, :], 0.0).then_inc(made, 1)
            nc.gpsimd.iota(step[:, :], pattern=[[P, NT]], base=0, channel_multiplier=0,
                           allow_small_or_imprecise_dtypes=True)
            nc.gpsimd.iota(tile[:, :], pattern=[[1, n_tiles]], base=0, channel_multiplier=0,
                           allow_small_or_imprecise_dtypes=True).then_inc(made, 1)
            on_pool(pool)

        @block.tensor
        def _(pe):
            on_tensor(pe, net, gate)

        @block.vector
        def _(v):
            nc.vector.memset(unit[:, :], 1.0)
            v.wait_ge(made, 2)
            on_vector(v, loc[:, :, :], total[:, :])
            nc.vector.tensor_tensor(sums[:, :, :], loc[:, :, :], gate, ALU.mult)
            v.drain()
            nc.vector.tensor_reduce(f[:, :], sums[:, :, :], AX.X, ALU.add)
            v.drain()
            nc.vector.tensor_tensor(above[:, :, :], bcast(total[:, :], NT), over_tiles(step[:, :], E), ALU.is_gt)
            v.drain()
            nc.vector.tensor_reduce(width[:, :], above[:, :, :], AX.X, ALU.add)
            v.drain()
            nc.vector.tensor_tensor_scan(start[:, :], unit[:, :], width[:, :], 0.0, ALU.mult, ALU.add)
            v.drain()
            nc.vector.tensor_tensor(start[:, :], start[:, :], width[:, :], ALU.subtract)
            v.drain()
            nc.vector.tensor_tensor(sums[:, :, :], over_tiles(start[:, :], NT), gate, ALU.mult)
            nc.vector.tensor_tensor(past[:, :, :], bcast(tile[:, :], E), over_tiles(start[0:1, :], n_tiles), ALU.is_ge)
            v.drain()
            nc.vector.tensor_reduce(loc[:, :, 0], sums[:, :, :], AX.X, ALU.add)
            nc.vector.tensor_reduce(ef[:, :], past[:, :, 1:E], AX.X, ALU.add)
            v.drain()
            nc.vector.scalar_tensor_tensor(f[:, :], loc[:, :, 0], float(P), f[:, :], ALU.mult, ALU.add)
            nc.vector.tensor_copy(expert_of[:, :], ef[:, :])
            v.drain()
            nc.vector.tensor_copy(pos[:, :], f[:, :])


def scatter_tokens(nc, net, pos, xs):
    with ExitStack() as ctx:
        p = Scope(nc, ctx, "m0s")
        h = p.sb("h", [P, NT, D])
        h_done, moved = p.sem("h_done"), p.sem("moved")
        block = ctx.enter_context(nc.Block())

        @block.vector
        def _(v):
            for t in range(NT):
                nc.vector.tensor_scalar(h[:, t, :], net.x[:, t, :], net.stat[:, t, 0:1], net.rstd[:, t:t + 1],
                                        ALU.subtract, ALU.mult).then_inc(h_done, 1)

        @block.gpsimd
        def _(pool):
            for t in range(NT):
                pool.wait_ge(h_done, t + 1)
                nc.gpsimd.indirect_dma_start(xs[:, :], bass.IndirectOffsetOnAxis(pos[:, t:t + 1], 0),
                                             h[:, t, :], None).then_inc(moved, 16)
            pool.wait_ge(moved, 16 * NT)


def gather_outputs(nc, net, pos, ys):
    with ExitStack() as ctx:
        p = Scope(nc, ctx, "m0g")
        y = p.sb("y", [P, NT, D])
        gathered = [p.sem(f"gathered{q}") for q in range(4)]
        block = ctx.enter_context(nc.Block())

        @block.gpsimd
        def _(pool):
            for t in range(NT):
                nc.gpsimd.indirect_dma_start(y[:, t, :], None, ys[:, :],
                                             bass.IndirectOffsetOnAxis(pos[:, t:t + 1], 0)).then_inc(gathered[t // 8], 16)

        @block.vector
        def _(v):
            for q in range(4):
                v.wait_ge(gathered[q], 16 * 8)
                s = slice(8 * q, 8 * q + 8)
                nc.vector.tensor_tensor(net.x[:, s, :], net.x[:, s, :], y[:, s, :], ALU.add)


def tiles_by_expert(nc, net, N, expert_of, w1, b1, w2, b2, xs, ys):
    E, F = b1.shape[1:]
    nf = F // P
    with ExitStack() as ctx:
        p = Scope(nc, ctx, "m0e")
        two = lambda name, shape: [p.sb(f"{name}{i}", shape) for i in range(2)]
        x, xT, h, hT, y = two("x", [P, D]), two("xT", [P, P]), two("h", [P, F]), two("hT", [P, nf, P]), two("y", [P, D])
        xps, hps, tps, yps = ([p.ps(f"{n}{i}") for i in range(2)] for n in ("xps", "hps", "tps", "yps"))
        x_loaded, y_stored = ([p.sem(f"{n}{i}") for i in range(2)] for n in ("x_loaded", "y_stored"))
        x_turned, xT_done = p.sem("x_turned"), p.sem("xT_done")
        h_made, h_done = p.sem("h_made"), p.sem("h_done")
        h_turned, hT_done = p.sem("h_turned"), p.sem("hT_done")
        y_made, y_done = p.sem("y_made"), p.sem("y_done")
        block = ctx.enter_context(nc.Block())

        def steps(eng, step):
            inside = lambda i: (lambda k: 0 <= i + k < N)
            for i in range(-2, 2):
                step(i, i % 2, inside(i))
            with eng.Fori(1, (N - 4) // 2) as j:
                for par in range(2):
                    step(2 * j + par, par, lambda k: True)
            for i in range(N - 4, N + 2):
                step(i, i % 2, inside(i))

        def wait(eng, sem, n):
            if not isinstance(n, int) or n > 0:
                eng.wait_ge(sem, n)

        def expert(eng, t):
            return eng.value_load(expert_of[0:1, bass.ds(t, 1)], min_val=0, max_val=E - 1)

        @block.sync
        def _(sp):
            def load(t, par):
                wait(sp, x_turned, t - 1)
                sp.dma_start(x[par][:, :], xs[bass.ts(t, P), :]).then_inc(x_loaded[par], 16)

            def step(i, par, is_tile):
                if is_tile(-1):
                    sp.wait_ge(y_done, i)
                    sp.dma_start(ys[bass.ts(i - 1, P), :], y[1 - par][:, :]).then_inc(y_stored[1 - par], 16)
                if is_tile(4):
                    load(i + 4, par)

            load(0, 0)
            load(1, 1)
            steps(sp, step)
            for par in range(2):
                sp.wait_ge(y_stored[par], 16 * (N // 2))

        @block.tensor
        def _(pe):
            def step(i, par, is_tile):
                if is_tile(2):
                    pe.wait_ge(x_loaded[par], 8 * (i + 4 - par))
                    wait(pe, xT_done, i + 1)
                    nc.tensor.transpose(xps[par][:, 0:P], x[par][:, :], net.ident[:, :]).then_inc(x_turned, 1)
                if is_tile(1):
                    t, q = i + 1, 1 - par
                    e = expert(pe, t)
                    pe.wait_ge(xT_done, t + 1)
                    wait(pe, h_done, t - 1)
                    nc.tensor.matmul(hps[q][:, :], xT[q][:, :], w1[:, bass.ds(e, 1), :].rearrange("p a f -> p (a f)"),
                                     start=True, stop=True).then_inc(h_made, 1)
                if is_tile(-1):
                    t, q = i - 1, 1 - par
                    e = expert(pe, t)
                    pe.wait_ge(hT_done, t + 1)
                    wait(pe, y_done, t - 1)
                    for f in range(nf):
                        last = nc.tensor.matmul(yps[q][:, 0:D], hT[q][:, f, :],
                                                w2[:, bass.ds(e, 1), f, :].rearrange("p a d -> p (a d)"),
                                                start=(f == 0), stop=(f == nf - 1))
                    last.then_inc(y_made, 1)
                if is_tile(0):
                    pe.wait_ge(h_done, i + 1)
                    wait(pe, hT_done, i - 1)
                    for f in range(nf):
                        last = nc.tensor.transpose(tps[par][:, f * P:(f + 1) * P], h[par][:, f * P:(f + 1) * P], net.ident[:, :])
                    last.then_inc(h_turned, 1)

            steps(pe, step)

        @block.scalar
        def _(act):
            nc.scalar.preload_act_table(ACT.Relu)

            def step(i, par, is_tile):
                if is_tile(2):
                    act.wait_ge(x_turned, i + 3)
                    wait(act, h_made, i + 1)
                    nc.scalar.activation(xT[par][:, :], xps[par][:, 0:P], ACT.Copy).then_inc(xT_done, 1)
                if is_tile(0):
                    act.wait_ge(h_turned, i + 1)
                    wait(act, y_made, i - 1)
                    nc.scalar.activation(hT[par][:, :, :].rearrange("p a b -> p (a b)"), tps[par][:, :],
                                         ACT.Relu).then_inc(hT_done, 1)

            steps(act, step)

        @block.vector
        def _(v):
            def step(i, par, is_tile):
                if is_tile(1):
                    t, q = i + 1, 1 - par
                    e = expert(v, t)
                    v.wait_ge(h_made, t + 1)
                    wait(v, h_turned, t - 1)
                    nc.vector.tensor_tensor(h[q][:, :], hps[q][:, :], b1[:, bass.ds(e, 1), :].rearrange("p a f -> p (a f)"),
                                            ALU.add).then_inc(h_done, 1)
                if is_tile(-1):
                    t, q = i - 1, 1 - par
                    e = expert(v, t)
                    v.wait_ge(y_made, t + 1)
                    wait(v, y_stored[q], 8 * (t - q))
                    nc.vector.tensor_tensor(y[q][:, :], yps[q][:, 0:D], b2[:, bass.ds(e, 1), :].rearrange("p a d -> p (a d)"),
                                            ALU.add).then_inc(y_done, 1)

            steps(v, step)


def moe_capacity_relu(nc, net, d):
    E, F = d["L0_ffn_b1"].shape
    nf = F // P
    cap = -(-(B * S) * 5 // (E * 4))
    N = NT + E
    xs, ys = (nc.dram_tensor(n, (N * P, D), FP, kind="Internal").ap() for n in ("rows_in", "rows_out"))
    with ExitStack() as ctx:
        p = Scope(nc, ctx, "m0w")
        w1, w2 = p.sb("w1", [P, E, F]), p.sb("w2", [P, E, nf, D])
        b1, b2 = p.sb("b1", [P, E, F]), p.sb("b2", [P, E, D])
        pos, expert_of, zeros = p.sb("pos", [P, NT], I32), p.sb("expert_of", [1, N], I32), p.sb("zeros", [P, D])
        with ExitStack() as part:
            r = Router(nc, part, "m0", E)
            normalise_and_route(nc, net, "m0", d["L0_ffn_router_w"], E, r.lg)
            top1_prob(nc, r, "m0")
            capacity_by_probability(nc, net, r, cap, "m0")
            to_all = lambda v: v.rearrange("(a e) f -> a e f", a=1).to_broadcast([P] + list(v.shape))
            dispatch(nc, net, r.gate[:, :, :], E, N, pos, expert_of, zeros, xs,
                     [(w1[:, :, :], d["L0_ffn_W1"].rearrange("e d f -> d e f")),
                      (w2[:, :, :, :], d["L0_ffn_W2"].rearrange("e (g f) d -> f e g d", f=P)),
                      (b1[:, :, :], to_all(d["L0_ffn_b1"])), (b2[:, :, :], to_all(d["L0_ffn_b2"]))])
        scatter_tokens(nc, net, pos, xs)
        tiles_by_expert(nc, net, N, expert_of, w1, b1, w2, b2, xs, ys)
        gather_outputs(nc, net, pos, ys)
    measure(nc, net, "m0")


def phase_memory(nc, net, d):
    import math
    T1 = d["L1_attn_W_dt1"].shape[1]
    TWO_PI_HI = 6.28125
    TWO_PI_LO = 2 * math.pi - TWO_PI_HI
    ROUND = 1.5 * 2.0 ** 23
    normalise(nc, net, "a1")
    with ExitStack() as ctx:
        p = Scope(nc, ctx, "a1")
        WB, WC, Wo, Dg = (p.sb(n, [P, P]) for n in ("WB", "WC", "Wo", "Dg"))
        W1, W2 = p.sb("W1", [P, T1]), p.sb("W2", [T1, P])
        bB, bC, b2, om0, Dc, b1 = (p.sb(n, [P, 1]) for n in ("bB", "bC", "b2", "om0", "Dc", "b1"))
        half_pi, one, bo = p.sb("half_pi", [P, 1]), p.sb("one", [P, S]), p.sb("bo", [P, D])
        two = lambda n, s=S, q=P: [p.sb(f"{n}{i}", [q, s]) for i in range(2)]
        xc, t1, rz, l, ph, sn, cn, r = (two("xc"), two("t1", S, T1), two("rz"), two("l"), two("ph"), two("sn"),
                                        two("cn"), two("r"))
        az, om, k, content, cc, cs = (p.sb(n, [P, S]) for n in ("az", "om", "k", "content", "cc", "cs"))
        t1ps, t2ps = p.ps("t1ps"), p.ps("t2ps")
        bps, cps, yps = ([p.ps(f"{n}{i}") for i in range(2)] for n in ("bps", "cps", "yps"))
        loaded, consts, diag, bias_added = p.sem("loaded"), p.sem("consts"), p.sem("diag"), p.sem("bias_added")
        xc_done, t1_ready, t1_done, t2_ready, sp_done, phi_done, trig_done, bc_ready, r_done, y_done, y_used = (
            p.sem(n) for n in ("xc_done", "t1_ready", "t1_done", "t2_ready", "sp_done", "phi_done", "trig_done",
                               "bc_ready", "r_done", "y_done", "y_used"))
        block = ctx.enter_context(nc.Block())
        a = lambda n: d[f"L1_attn_{n}"]
        loads = [(WB, a("W_B")), (WC, a("W_C")), (Wo, a("W_out")), (W1, a("W_dt1")), (W2, a("W_dt2")),
                 (bB, col(a("b_B"))), (bC, col(a("b_C"))), (b2, col(a("b_dt2"))), (om0, col(a("omega_base"))),
                 (Dc, col(a("D")))]

        @block.sync
        def _(sp):
            for t, src in loads:
                sp.dma_start(t[:, :], src).then_inc(loaded, 16)
            sp.dma_start(b1[0:T1, :], col(a("b_dt1"))).then_inc(loaded, 16)
            sp.dma_start(bo[:, :], row(a("b_out")).to_broadcast([P, D])).then_inc(loaded, 16)

        N_LOADED = 16 * (len(loads) + 2)

        @block.gpsimd
        def _(pool):
            nc.gpsimd.memset(one[:, :], 1.0)
            nc.gpsimd.memset(half_pi[:, :], math.pi / 2).then_inc(consts, 1)
            pool.wait_ge(loaded, N_LOADED)
            nc.gpsimd.tensor_scalar(Dg[:, :], net.ident[:, :], Dc[:, :], None, ALU.mult).then_inc(diag, 1)
            nc.gpsimd.tensor_tensor(net.x[:, :, :], net.x[:, :, :], over_tiles(bo[:, :], NT), ALU.add).then_inc(bias_added, 1)

        @block.tensor
        def _(pe):
            pe.wait_ge(loaded, N_LOADED)
            pe.wait_ge(diag, 1)
            pe.sem_inc(t2_ready, 2)
            pe.sem_inc(y_done, 2)

            def inner(c, par):
                pe.wait_ge(t1_done, c + 1)
                nc.tensor.matmul(t1ps[0:T1, :], W1[:, :], net.xT[:, bass.ts(c, S)], start=True, stop=True).then_inc(t1_ready, 1)
                pe.wait_ge(t1_done, c + 2)
                pe.wait_ge(sp_done, c + 1)
                nc.tensor.matmul(t2ps[:, :], W2[:, :], t1[par][0:T1, :], start=True, stop=True).then_inc(t2_ready, 1)

            def gates(c, par):
                pe.wait_ge(r_done, c + 1)
                nc.tensor.matmul(bps[par][:, :], WB[:, :], net.xT[:, bass.ts(c, S)], start=True, stop=True)
                nc.tensor.matmul(cps[par][:, :], WC[:, :], net.xT[:, bass.ts(c, S)], start=True, stop=True).then_inc(bc_ready, 1)

            def outer(c, par):
                pe.wait_ge(xc_done, c + 1)
                pe.wait_ge(r_done, c + 3)
                pe.wait_ge(y_used, c + 1)
                for q in range(TC):
                    tok = slice(q * P, (q + 1) * P)
                    nc.tensor.matmul(yps[par][:, tok], r[par][:, tok], Wo[:, :], start=True, stop=False)
                    last = nc.tensor.matmul(yps[par][:, tok], xc[par][:, tok], Dg[:, :], start=False, stop=True)
                last.then_inc(y_done, 1)

            skewed(pe, (inner, 2), (gates, 1), (outer, 0))

        @block.scalar
        def _(act):
            act.wait_ge(loaded, N_LOADED)
            act.wait_ge(consts, 1)
            act.sem_inc(t1_done, 1)
            act.sem_inc(sp_done, 1)
            act.sem_inc(trig_done, 2)

            def softplus(c, par):
                act.wait_ge(t1_ready, c + 1)
                act.wait_ge(t2_ready, c + 1)
                nc.scalar.activation(t1[par][0:T1, :], t1ps[0:T1, :], ACT.Identity, bias=b1[0:T1, :]).then_inc(t1_done, 1)
                act.wait_ge(t2_ready, c + 3)
                act.wait_ge(phi_done, c + 1)
                nc.scalar.activation(rz[par][:, :], t2ps[:, :], ACT.Relu, bias=b2[:, :])
                nc.scalar.activation(az[:, :], t2ps[:, :], ACT.Abs, bias=b2[:, :])
                act.drain()
                nc.scalar.activation(az[:, :], az[:, :], ACT.Exp, scale=-1.0)
                act.drain()
                nc.scalar.activation(l[par][:, :], az[:, :], ACT.Ln, bias=1.0).then_inc(sp_done, 1)

            def trig(c, par):
                act.wait_ge(phi_done, c + 3)
                act.wait_ge(r_done, c + 1)
                nc.scalar.activation(sn[par][:, :], ph[par][:, :], ACT.Sin)
                nc.scalar.activation(cn[par][:, :], ph[par][:, :], ACT.Abs)
                act.drain()
                nc.scalar.activation(cn[par][:, :], cn[par][:, :], ACT.Sin, bias=half_pi[:, :], scale=-1.0).then_inc(trig_done, 1)
                act.wait_ge(y_done, c + 1)
                nc.scalar.activation(xc[par][:, :], net.xT[:, bass.ts(c, S)], ACT.Copy).then_inc(xc_done, 1)

            skewed(act, (softplus, 2), (trig, 1))

        @block.vector
        def _(v):
            tt, ts, stt = nc.vector.tensor_tensor, nc.vector.tensor_scalar, nc.vector.scalar_tensor_tensor
            v.sem_inc(phi_done, 2)
            v.sem_inc(r_done, 2)
            v.sem_inc(y_used, 2)
            v.wait_ge(loaded, N_LOADED)
            v.wait_ge(consts, 1)
            v.wait_ge(bias_added, 1)

            def phase(c, par):
                v.wait_ge(sp_done, c + 2)
                tt(om[:, :], rz[par][:, :], l[par][:, :], ALU.add)
                v.drain()
                ts(om[:, :], om[:, :], om0[:, :], None, ALU.mult)
                v.drain()
                v.wait_ge(trig_done, c + 1)
                nc.vector.tensor_tensor_scan(ph[par][:, :], one[:, :], om[:, :], 0.0, ALU.mult, ALU.add)
                v.drain()
                ts(k[:, :], ph[par][:, :], 1 / (2 * math.pi), ROUND, ALU.mult, ALU.add)
                v.drain()
                ts(k[:, :], k[:, :], -ROUND, None, ALU.add)
                v.drain()
                stt(ph[par][:, :], k[:, :], -TWO_PI_HI, ph[par][:, :], ALU.mult, ALU.add)
                v.drain()
                stt(ph[par][:, :], k[:, :], -TWO_PI_LO, ph[par][:, :], ALU.mult, ALU.add)
                v.drain()
                ts(ph[par][:, :], ph[par][:, :], 3.1415925, -3.1415925, ALU.min, ALU.max).then_inc(phi_done, 1)

            def memory(c, par):
                v.wait_ge(bc_ready, c + 1)
                v.wait_ge(trig_done, c + 3)
                stt(content[:, :], bps[par][:, :], bB[:, :], net.xT[:, bass.ts(c, S)], ALU.add, ALU.mult)
                v.drain()
                tt(cc[:, :], content[:, :], cn[par][:, :], ALU.mult)
                tt(cs[:, :], content[:, :], sn[par][:, :], ALU.mult)
                v.drain()
                nc.vector.tensor_tensor_scan(content[:, :], one[:, :], cc[:, :], 0.0, ALU.mult, ALU.add)
                nc.vector.tensor_tensor_scan(k[:, :], one[:, :], cs[:, :], 0.0, ALU.mult, ALU.add)
                v.drain()
                tt(cc[:, :], content[:, :], cn[par][:, :], ALU.mult)
                tt(cs[:, :], k[:, :], sn[par][:, :], ALU.mult)
                v.drain()
                tt(cc[:, :], cc[:, :], cs[:, :], ALU.add)
                v.drain()
                v.wait_ge(y_done, c + 1)
                stt(r[par][:, :], cps[par][:, :], bC[:, :], cc[:, :], ALU.add, ALU.mult).then_inc(r_done, 1)

            def add_output(c, par):
                v.wait_ge(y_done, c + 3)
                xt = net.x[:, bass.ts(c, 4), :].rearrange("p a b -> p (a b)")
                tt(xt, xt, yps[par][:, :], ALU.add).then_inc(y_used, 1)

            skewed(v, (phase, 1), (add_output, -1), (memory, 0))
    measure(nc, net, "a1")


def best_groups_gate(nc, net, r, scores, groups, keep_groups, top, tag):
    E, size = r.E, r.E // groups
    with ExitStack() as ctx:
        p = Scope(nc, ctx, tag + "_bg")
        iota_done, shifted, exped = p.sem("iota_done"), p.sem("shifted"), p.sem("exped")
        giota, gs, geq, goh, gsel = (p.sb(n, [P, NT, groups]) for n in ("giota", "gs", "geq", "goh", "gsel"))
        gm, total = p.sb("gm", [P, NT]), p.sb("total", [P, NT])
        cur, sel = p.sb("cur", [P, NT, E]), p.sb("sel", [P, NT, E])
        block = ctx.enter_context(nc.Block())

        @block.gpsimd
        def _(pool):
            nc.gpsimd.iota(giota[:, :, :], pattern=[[0, NT], [1, groups]], base=0, channel_multiplier=0,
                           allow_small_or_imprecise_dtypes=True).then_inc(iota_done, 1)
            nc.gpsimd.iota(r.iota[:, :, :], pattern=[[0, NT], [1, E]], base=0, channel_multiplier=0,
                           allow_small_or_imprecise_dtypes=True).then_inc(iota_done, 1)

        @block.scalar
        def _(act):
            act.wait_ge(shifted, 1)
            nc.scalar.activation(scores[:, :, :], scores[:, :, :], ACT.Exp).then_inc(exped, 1)

        @block.vector
        def _(v):
            def pick(cur, m, eq, oh, iota, sel, n, times):
                nc.vector.memset(sel, 0.0)
                for _ in range(times):
                    first_best(nc, v, cur, m, eq, r.idx, oh, iota, n)
                    nc.vector.tensor_tensor(sel, sel, oh[:, :, :], ALU.add)
                    nc.vector.scalar_tensor_tensor(cur[:, :, :], oh[:, :, :], -4.0, cur[:, :, :], ALU.mult, ALU.add)
                    v.drain()

            v.wait_ge(iota_done, 2)
            nc.vector.tensor_reduce(r.m[:, :], r.lg[:, :, :], AX.X, ALU.max)
            v.drain()
            nc.vector.tensor_tensor(scores[:, :, :], r.lg[:, :, :], bcast(r.m[:, :], E), ALU.subtract).then_inc(shifted, 1)
            v.wait_ge(exped, 1)
            nc.vector.tensor_reduce(total[:, :], scores[:, :, :], AX.X, ALU.add)
            v.drain()
            nc.vector.reciprocal(total[:, :], total[:, :])
            v.drain()
            nc.vector.tensor_tensor(scores[:, :, :], scores[:, :, :], bcast(total[:, :], E), ALU.mult)
            v.drain()
            nc.vector.tensor_reduce(gs[:, :, :], scores[:, :, :].rearrange("p t (g s) -> p t g s", s=size), AX.X, ALU.max)
            v.drain()
            pick(gs, gm, geq, goh, giota, gsel[:, :, :], groups, keep_groups)
            v4 = lambda a: a.rearrange("p t (g s) -> p (t g) s", s=size)
            nc.vector.tensor_tensor(v4(cur[:, :, :]), v4(scores[:, :, :]),
                                    bcast(gsel[:, :, :].rearrange("p t g -> p (t g)"), size), ALU.mult)
            v.drain()
            pick(cur, r.m, r.eq, r.oh, r.iota, sel[:, :, :], E, top)
            nc.vector.tensor_tensor(r.gate[:, :, :], sel[:, :, :], scores[:, :, :], ALU.mult)


def moe_grouped_swiglu(nc, net, d):
    E, _, I = d["L1_ffn_w1"].shape
    with ExitStack() as ctx:
        r = Router(nc, ctx, "m1", E)
        scores = Scope(nc, ctx, "m1s").sb("scores", [P, NT, E])
        normalise_and_route(nc, net, "m1", d["L1_ffn_gate_w"], E, r.lg)
        best_groups_gate(nc, net, r, scores, 4, 2, 4, "m1")
        w1, w3 = (d[f"L1_ffn_{n}"].rearrange("e d i -> d e i") for n in ("w1", "w3"))
        w2 = d["L1_ffn_w2"].rearrange("e i d -> i e d")
        one = Scope(nc, ctx, "m1o").sb("one", [P, 1])
        pair = lambda w: lambda e: [(lambda t: t[:, :].rearrange("d (e i) -> d e i", e=2), w[:, bass.ds(2 * e, 2), :])]
        down = lambda e: [(lambda t, q=q: t[q * I:(q + 1) * I, 0, q * P:(q + 1) * P],
                           w2[:, bass.ds(2 * e + q, 1), :].rearrange("i a d -> i (a d)")) for q in range(2)]
        experts(nc, net, "m1e", E // 2, 1, ACT.Silu, lambda t, e, q: r.gate[:, t, bass.ds(2 * e + q, 1)],
                pair(w1), down, w3=pair(w3), nb=2)
        whole = lambda n: lambda e: [(lambda t: t[:, :], d[f"L1_ffn_{n}"])]
        experts(nc, net, "m1sh", 1, 1, ACT.Silu, lambda t, e, q: net.ones[:, 0:1],
                whole("ws1"), lambda e: [(lambda t: t[:, 0, :], d["L1_ffn_ws2"])], w3=whole("ws3"))
    measure(nc, net, "m1")


def causal_attention(nc, net, d):
    H = d["L2_attn_wq"].shape[1]
    scale = H ** -0.5
    a = lambda n: d[f"L2_attn_{n}"]
    PLACE = [(0, 0), (1, 0), (0, P), (2, 0)]
    POFF = [0, P, 3 * P, 6 * P]
    PV0 = 10
    normalise(nc, net, "a2")
    with ExitStack() as ctx:
        p = Scope(nc, ctx, "a2")
        wq, wk, wv = (p.sb(n, [P, H]) for n in ("wq", "wk", "wv"))
        wo, bq, bk = p.sb("wo", [P, D]), p.sb("bq", [H, 1]), p.sb("bk", [H, 1])
        bv, bo, mask = p.sb("bv", [P, H]), p.sb("bo", [P, D]), p.sb("mask", [P, P])
        two = lambda n, s: [p.sb(f"{n}{i}", [P, *s]) for i in range(2)]
        xc, qT, kT, V = two("xc", [S]), two("qT", [S]), two("kT", [S]), two("V", [TC, H])
        prob, nb, sums, ri = two("prob", [10 * P]), two("nb", [TC]), two("sums", [TC]), two("ri", [TC])
        PT, z = two("PT", [S]), p.sb("z", [P, TC, P])
        pj, zps, yps = p.ps("pj"), p.ps("zps", [P, TC, H]), p.ps("yps")
        sps, tps = [p.ps(f"sps{i}") for i in range(3)], [p.ps(f"tps{i}") for i in range(2)]
        wo_zeroed = p.sem("wo_zeroed")
        loaded, zeroed, bias_added = p.sem("loaded"), p.sem("zeroed"), p.sem("bias_added")
        xc_done, pj_ready, pj_used, s_ready, nb_done, p_done = (
            p.sem(n) for n in ("xc_done", "pj_ready", "pj_used", "s_ready", "nb_done", "p_done"))
        v_ready, v_used = p.sem("v_ready"), p.sem("v_used")
        t_ready, t_used, pv_done, z_ready, z_done, y_used = (
            p.sem(n) for n in ("t_ready", "t_used", "pv_done", "z_ready", "z_done", "y_used"))
        block = ctx.enter_context(nc.Block())
        N_LOADED = 16 * 8

        @block.sync
        def _(sp):
            sp.wait_ge(wo_zeroed, 1)
            for t, src in ((wq, a("wq")), (wk, a("wk")), (wv, a("wv")), (wo, a("wo")), (bq, col(a("bq"))),
                           (bk, col(a("bk"))), (bv, row(a("bv")).to_broadcast([P, H])),
                           (bo, row(a("bo")).to_broadcast([P, D]))):
                sp.dma_start(t[:, :] if t is not wo else wo[0:H, :], src).then_inc(loaded, 16)

        @block.gpsimd
        def _(pool):
            nc.gpsimd.memset(wo[:, :], 0.0).then_inc(wo_zeroed, 1)
            nc.gpsimd.memset(z[:, :, H:P], 0.0)
            for i in range(2):
                nc.gpsimd.memset(qT[i][:, :], 0.0)
                nc.gpsimd.memset(kT[i][:, :], 0.0)
            nc.gpsimd.memset(mask[:, :], 0.0).then_inc(zeroed, 1)
            pool.wait_ge(zeroed, 1)
            nc.gpsimd.affine_select(out=mask[:, :], in_=mask[:, :], compare_op=ALU.is_ge, fill=-1e11 / scale,
                                    base=0, pattern=[[-1, P]], channel_multiplier=1).then_inc(zeroed, 1)
            pool.wait_ge(loaded, N_LOADED)
            nc.gpsimd.tensor_tensor(net.x[:, :, :], net.x[:, :, :], over_tiles(bo[:, :], NT), ALU.add).then_inc(bias_added, 1)

        @block.tensor
        def _(pe):
            pe.wait_ge(loaded, N_LOADED)
            pe.wait_ge(zeroed, 2)
            pe.sem_inc(pv_done, PV0)
            pe.sem_inc(v_ready, 2)

            def queries(c, par):
                pe.wait_ge(xc_done, c + 1)
                pe.wait_ge(v_used, c + 1)
                nc.tensor.matmul(pj[0:H, :], wq[:, :], xc[par][:, :], start=True, stop=True).then_inc(pj_ready, 1)

            def keys(c, par):
                pe.wait_ge(pj_used, 2 * c + 1)
                nc.tensor.matmul(pj[0:H, :], wk[:, :], xc[par][:, :], start=True, stop=True).then_inc(pj_ready, 1)

            def tokens_values(c, par):
                pe.wait_ge(pj_used, min(2 * (c + 2), 2 * B) if isinstance(c, int) else 2 * (c + 2))
                for k in range(TC):
                    last = nc.tensor.matmul(pj[:, k * H:(k + 1) * H], xc[par][:, k * P:(k + 1) * P], wv[:, :],
                                            start=True, stop=True)
                last.then_inc(v_ready, 1)

            def scores(c, par):
                pe.wait_ge(pj_used, 2 * c + 2)
                for q in range(TC):
                    bank, off = PLACE[q]
                    pe.wait_ge(p_done, 4 * c + (3 if bank == 0 else q + 1))
                    n = (q + 1) * P
                    nc.tensor.matmul(sps[bank][:, off:off + n], qT[par][:, q * P:n], kT[par][:, 0:n],
                                     start=True, stop=True).then_inc(s_ready, 1)

            def values(c, par):
                def turn(q):
                    u = 5 * c + q
                    b = (par + q) % 2
                    pe.wait_ge(p_done, 4 * c + q + 5)
                    pe.wait_ge(t_used, u + 1)
                    for k in range(q + 1):
                        last = nc.tensor.transpose(tps[b][:, k * P:(k + 1) * P],
                                                   prob[par][:, POFF[q] + k * P:POFF[q] + (k + 1) * P], net.ident[:, :])
                    last.then_inc(t_ready, 1)

                def pv(q):
                    if q == 0:
                        pe.wait_ge(v_used, c + 3)
                    pe.wait_ge(t_used, 5 * c + q + 3)
                    for k in range(q + 1):
                        last = nc.tensor.matmul(zps[:, q, :], PT[(par + q) % 2][:, k * P:(k + 1) * P], V[par][:, k, :],
                                                start=(k == 0), stop=(k == q))
                    last.then_inc(pv_done, 1)

                turn(0)
                turn(1)
                pe.wait_ge(z_done, c + 1)
                pv(0)
                turn(2)
                pv(1)
                turn(3)
                pv(2)
                pv(3)

            def project(c, par):
                b = par % 2
                pe.wait_ge(z_done, c + 2)
                pe.wait_ge(t_used, 5 * c + 5)
                for k in range(TC):
                    last = nc.tensor.transpose(tps[b][:, k * P:(k + 1) * P], z[:, k, :], net.ident[:, :])
                last.then_inc(t_ready, 1)
                pe.wait_ge(t_used, 5 * c + 7)
                pe.wait_ge(y_used, c + 1)
                for k in range(TC):
                    last = nc.tensor.matmul(yps[:, k * P:(k + 1) * P], PT[b][:, k * P:(k + 1) * P], wo[:, :],
                                            start=True, stop=True)
                last.then_inc(pv_done, 1)

            skewed(pe, (queries, 2), (scores, 1), (keys, 2), (project, -1), (values, 0), (tokens_values, 1))

        @block.scalar
        def _(act):
            act.wait_ge(loaded, N_LOADED)
            act.wait_ge(zeroed, 2)
            act.sem_inc(v_used, 2)
            act.sem_inc(p_done, 4)

            def queries_and_keys(c, par):
                act.wait_ge(v_ready, c + 1)
                nc.scalar.activation(xc[par][:, :], net.xT[:, bass.ts(c, S)], ACT.Copy).then_inc(xc_done, 1)
                for n, (t, bias) in enumerate(((qT, bq), (kT, bk))):
                    act.wait_ge(pj_ready, 2 * c + n + 1)
                    nc.scalar.activation(t[par][0:H, :], pj[0:H, :], ACT.Identity, bias=bias[:, :]).then_inc(pj_used, 1)

            def exponentials(c, par):
                act.wait_ge(pv_done, PV0 + 5 * c - 6)
                for q in range(TC):
                    bank, off = PLACE[q]
                    act.wait_ge(nb_done, 4 * c + (3 if bank == 0 else q + 1))
                    nc.scalar.activation(prob[par][:, POFF[q]:POFF[q] + (q + 1) * P], sps[bank][:, off:off + (q + 1) * P],
                                         ACT.Exp, bias=nb[par][:, q:q + 1], scale=scale,
                                         accum_out=sums[par][:, q:q + 1]).then_inc(p_done, 1)

            def tokens_values(c, par):
                act.wait_ge(v_ready, c + 3)
                nc.scalar.activation(V[par][:, :, :].rearrange("p a b -> p (a b)"), pj[:, 0:TC * H], ACT.Copy).then_inc(v_used, 1)

            skewed(act, (queries_and_keys, 2), (exponentials, 1), (tokens_values, 1))

        @block.vector
        def _(v):
            v.sem_inc(t_used, 2)
            v.sem_inc(z_done, 1)
            v.sem_inc(y_used, 1)
            v.wait_ge(zeroed, 2)
            v.wait_ge(bias_added, 1)

            def maxima(c, par):
                for q in range(TC):
                    bank, off = PLACE[q]
                    n = (q + 1) * P
                    v.wait_ge(s_ready, 4 * c + (3 if bank == 0 else q + 1))
                    dg = sps[bank][:, off + q * P:off + n]
                    nc.vector.tensor_tensor(dg, dg, mask[:, :], ALU.add)
                    v.drain()
                    nc.vector.tensor_reduce(nb[par][:, q:q + 1], sps[bank][:, off:off + n], AX.X, ALU.max)
                    v.drain()
                    nc.vector.tensor_scalar(nb[par][:, q:q + 1], nb[par][:, q:q + 1], -scale, None, ALU.mult).then_inc(nb_done, 1)

            def copy(c, par, q, rows, n):
                u = 5 * c + q
                v.wait_ge(t_ready, u + 1)
                v.wait_ge(pv_done, PV0 + u - 1)
                nc.vector.tensor_copy(PT[(par + q) % 2][0:rows, 0:n], tps[(par + q) % 2][0:rows, 0:n]).then_inc(t_used, 1)

            def outputs(c, par):
                v.wait_ge(p_done, 4 * c + 8)
                nc.vector.reciprocal(ri[par][:, :], sums[par][:, :])
                for q in range(TC):
                    copy(c, par, q, P, (q + 1) * P)
                v.drain()
                v.wait_ge(pv_done, PV0 + 5 * c + 4)
                for q in range(TC):
                    last = nc.vector.scalar_tensor_tensor(z[:, q, 0:H], zps[:, q, :], ri[par][:, q:q + 1], bv[:, :],
                                                          ALU.mult, ALU.add)
                last.then_inc(z_done, 1)

            def add_output(c, par):
                copy(c, par, 4, P, S)
                v.wait_ge(pv_done, PV0 + 5 * c + 5)
                xt = net.x[:, bass.ts(c, 4), :].rearrange("p a b -> p (a b)")
                nc.vector.tensor_tensor(xt, xt, yps[:, :], ALU.add).then_inc(y_used, 1)

            skewed(v, (maxima, 1), (add_output, -1), (outputs, 0))
    measure(nc, net, "a2")


def moe_top1_gelu(nc, net, d):
    E = 8
    with ExitStack() as ctx:
        p = Scope(nc, ctx, "m2")
        lg, eq, oh = p.sb("lg", [P, NT, E]), p.sb("eq", [P, NT, E]), p.sb("onehot", [P, NT, E])
        m, idx, iota = p.sb("m", [P, NT]), p.sb("idx", [P, NT]), p.sb("iota", [P, NT, E])
        normalise_and_route(nc, net, "m2", d["L2_ffn_Wg"], E, lg, bias=d["L2_ffn_bg"])
        with ExitStack() as c2:
            iota_done = Scope(nc, c2, "m2r").sem("iota_done")
            block = c2.enter_context(nc.Block())

            @block.gpsimd
            def _(pool):
                nc.gpsimd.iota(iota[:, :, :], pattern=[[0, NT], [1, E]], base=0, channel_multiplier=0,
                               allow_small_or_imprecise_dtypes=True).then_inc(iota_done, 1)

            @block.vector
            def _(v):
                v.wait_ge(iota_done, 1)
                first_best(nc, v, lg, m, eq, idx, oh, iota, E)
        gated_bias(nc, net, "m2", oh, d["L2_ffn_b2"])
        W1 = d["L2_ffn_W1"].rearrange("e d f -> d e f")
        W2 = d["L2_ffn_W2"].rearrange("e f d -> f e d")
        b1 = d["L2_ffn_b1"].rearrange("e f a -> f e a")
        experts(nc, net, "m2e", E, 1, ACT.Gelu, lambda t, e, k: oh[:, t, bass.ds(e, 1)],
                lambda e: [(lambda t: t[:, :], W1[:, bass.ds(e, 1), :].rearrange("d a f -> d (a f)"))],
                lambda e: [(lambda t: t[:, 0, :], W2[:, bass.ds(e, 1), :].rearrange("d a f -> d (a f)"))],
                b1=lambda e: b1[:, bass.ds(e, 1), :].rearrange("f a b -> f (a b)"))
    measure(nc, net, "m2")


def root_mean_square(nc, net, tag, h, r, weight=None, out=None, first=None):
    with ExitStack() as ctx:
        p = Scope(nc, ctx, tag)
        junk, ss = p.sb("junk", [P, D]), p.sb("ss", [P, NT])
        h_done, ss_done, w_loaded = p.sem("h_done"), p.sem("ss_done"), p.sem("w_loaded")
        wb = p.sb("wb", [P, D])
        block = ctx.enter_context(nc.Block())

        @block.sync
        def _(sp):
            if weight is not None:
                sp.dma_start(wb[:, :], row(weight).to_broadcast([P, D])).then_inc(w_loaded, 16)

        @block.scalar
        def _(act):
            for t in range(NT):
                if first is not None and t % 4 == 0:
                    act.wait_ge(h_done, t // 4 + 1)
                nc.scalar.activation(junk[:, :], h[:, t, :], ACT.Square, accum_out=ss[:, t:t + 1])
                act.drain()
            nc.scalar.activation(ss[:, :], ss[:, :], ACT.Sqrt, scale=1.0 / D, bias=net.epst[:, 1:2]).then_inc(ss_done, 1)

        @block.vector
        def _(v):
            if first is not None:
                for t in range(NT):
                    last = first(t)
                    if t % 4 == 3:
                        last.then_inc(h_done, 1)
            v.wait_ge(ss_done, 1)
            nc.vector.reciprocal(r[:, :], ss[:, :])
            if out is not None:
                v.drain()
                v.wait_ge(w_loaded, 16)
                for t in range(NT):
                    nc.vector.scalar_tensor_tensor(out[:, t, :], h[:, t, :], r[:, t:t + 1], wb[:, :], ALU.mult, ALU.mult)


def turn_tokens(nc, net, tag, src, scale=None, weight=None):
    with ExitStack() as ctx:
        p = Scope(nc, ctx, tag)
        xn = [p.sb(f"xn{i}", [P, TC, D]) for i in range(2)]
        tps = [p.ps(f"tps{i}") for i in range(2)]
        wcol = p.sb("wcol", [P, 1])
        xn_done, t_done, t_free, w_loaded = p.sem("xn_done"), p.sem("t_done"), p.sem("t_free"), p.sem("w_loaded")
        block = ctx.enter_context(nc.Block())

        @block.sync
        def _(sp):
            if weight is not None:
                sp.dma_start(wcol[:, :], col(weight)).then_inc(w_loaded, 16)

        @block.vector
        def _(v):
            with v.Fori(0, B // 2) as i:
                for par in range(2):
                    c = 2 * i + par
                    v.wait_ge(t_done, c + 1)
                    if scale is None:
                        nc.vector.tensor_copy(xn[par][:, :, :], src[:, bass.ts(c, 4), :]).then_inc(xn_done, 1)
                    else:
                        nc.vector.tensor_tensor(xn[par][:, :, :], src[:, bass.ts(c, 4), :],
                                                bcast(scale[:, bass.ts(c, 4)], D), ALU.mult).then_inc(xn_done, 1)

        @block.tensor
        def _(pe):
            pe.sem_inc(t_done, 2)
            with pe.Fori(0, B // 2) as i:
                for par in range(2):
                    c = 2 * i + par
                    pe.wait_ge(xn_done, c + 1)
                    pe.wait_ge(t_free, c + 1)
                    for k in range(TC):
                        last = nc.tensor.transpose(tps[par][:, k * P:(k + 1) * P], xn[par][:, k, :], net.ident[:, :])
                    last.then_inc(t_done, 1)

        @block.scalar
        def _(act):
            act.sem_inc(t_free, 2)
            if weight is not None:
                act.wait_ge(w_loaded, 16)
            with act.Fori(0, B // 2) as i:
                for par in range(2):
                    c = 2 * i + par
                    act.wait_ge(t_done, c + 3)
                    kw = {} if weight is None else dict(scale=wcol[:, :])
                    nc.scalar.activation(net.xT[:, bass.ts(c, S)], tps[par][:, :], ACT.Identity if kw else ACT.Copy,
                                         **kw).then_inc(t_free, 1)


def decay_attention(nc, net, d):
    a = lambda n: d[f"L3_attn_{n}"]
    R = a("u").shape[1]
    K = a("k_base_kernel").shape[0]
    SUB = 32
    with ExitStack() as ctx:
        p = Scope(nc, ctx, "a3")
        h, hn = p.sb("h", [P, NT, D]), p.sb("hn", [P, NT, D])
        qk, rn = p.sb("qk", [P, NT, 2 * R]), p.sb("rn", [P, NT, 2])
        r1, g = p.sb("r1", [P, NT]), p.sb("g", [P, K])
        NB = P // SUB
        tQ, tQ2, tK, gP = p.sb("tQ", [R, P]), p.sb("tQ2", [R, P]), p.sb("tK", [R, NB, P]), p.sb("gP", [R, 1])
        tK2, causal = p.sb("tK2", [P, R]), p.sb("causal", [P, P])

        normalise_only = lambda t: nc.vector.tensor_scalar(h[:, t, :], net.x[:, t, :], net.stat[:, t, 0:1],
                                                           net.rstd[:, t:t + 1], ALU.subtract, ALU.mult)
        token_rstd(nc, net, "a3")
        root_mean_square(nc, net, "a3r1", h, r1, weight=a("norm1_w"), out=hn, first=normalise_only)
        turn_tokens(nc, net, "a3t", hn)
        router_logits(nc, net, "a3", (a("u"), a("v")), 2 * R, qk)
        decay_tables(nc, net, a, R, K, SUB, qk, rn, g, tQ, tQ2, tK, gP, tK2, causal)
        decay_mix(nc, net, a, R, K, SUB, h, hn, qk, rn, g, tQ, tQ2, tK, gP, tK2, causal)
        root_mean_square(nc, net, "a3r2", h, r1)
        turn_tokens(nc, net, "a3t2", h, scale=r1, weight=a("norm2_w"))
    F = a("mlp_w1").shape[1]
    experts(nc, net, "a3m", 1, F // P, ACT.Gelu_apprx_tanh, lambda t, e, q: net.ones[:, 0:1],
            lambda e: [(lambda t: t[:, :], a("mlp_w1"))],
            lambda e: [(lambda t: t[:, :, :], a("mlp_w2").rearrange("(g f) d -> f g d", f=P))],
            b1=lambda e: a("mlp_b1"))
    measure(nc, net, "a3")


def token_rstd(nc, net, tag):
    with ExitStack() as ctx:
        p = Scope(nc, ctx, tag + "_rs")
        std, std_done = p.sb("std", [P, NT]), p.sem("std_done")
        block = ctx.enter_context(nc.Block())

        @block.scalar
        def _(act):
            nc.scalar.activation(std[:, :], net.stat[:, :, 1], ACT.Sqrt, bias=net.epst[:, 0:1]).then_inc(std_done, 1)

        @block.vector
        def _(v):
            v.wait_ge(std_done, 1)
            nc.vector.reciprocal(net.rstd[:, :], std[:, :])


def decay_tables(nc, net, a, R, K, SUB, qk, rn, g, tQ, tQ2, tK, gP, tK2, causal):
    NB = P // SUB
    with ExitStack() as ctx:
        p = Scope(nc, ctx, "a3tab")
        dl, al = p.sb("dl", [R, 1]), p.sb("al", [R, 1])
        dlb, jcol = p.sb("dlb", [P, R]), p.sb("jcol", [P, 1])
        gate, sq = p.sb("gate", [P, 1]), p.sb("sq", [P, NT, 2 * R])
        loaded, counted, sig, clipped, lned, ready, squared, rooted = (
            p.sem(n) for n in ("loaded", "counted", "sig", "clipped", "lned", "ready", "squared", "rooted"))
        block = ctx.enter_context(nc.Block())

        @block.sync
        def _(sp):
            sp.dma_start(dl[:, :], col(a("decay_logit"))).then_inc(loaded, 16)
            sp.dma_start(al[:, :], col(a("alpha_logit"))).then_inc(loaded, 16)
            sp.dma_start(dlb[:, :], row(a("decay_logit")).to_broadcast([P, R])).then_inc(loaded, 16)
            sp.dma_start(gate[:, :], row(a("k_base_gate_logit")).to_broadcast([P, 1])).then_inc(loaded, 16)
            sp.dma_start(g[:, :], row(a("k_base_kernel")).to_broadcast([P, K])).then_inc(loaded, 16)

        @block.gpsimd
        def _(pool):
            io = dict(base=0, channel_multiplier=0, allow_small_or_imprecise_dtypes=True)
            nc.gpsimd.iota(tQ[:, :], pattern=[[0, NB], [1, SUB]], **io)
            nc.gpsimd.iota(tQ2[:, :], pattern=[[1, P]], **io)
            nc.gpsimd.iota(tK[:, :, :], pattern=[[SUB, NB], [-1, P]], **io)
            nc.gpsimd.memset(gP[:, :], float(P))
            nc.gpsimd.iota(jcol[:, :], pattern=[[0, 1]], base=P, channel_multiplier=-1,
                           allow_small_or_imprecise_dtypes=True)
            nc.gpsimd.memset(causal[:, :], 1.0).then_inc(counted, 1)
            pool.wait_ge(counted, 1)
            nc.gpsimd.affine_select(out=causal[:, :], in_=causal[:, :], compare_op=ALU.is_ge, fill=0.0,
                                    base=0, pattern=[[1, P]], channel_multiplier=-1).then_inc(counted, 1)

        @block.scalar
        def _(act):
            act.wait_ge(loaded, 80)
            act.wait_ge(squared, 1)
            nc.scalar.activation(rn[:, :, :], rn[:, :, :], ACT.Sqrt).then_inc(rooted, 1)
            for t in (dl, al, dlb, gate):
                last = nc.scalar.activation(t[:, :], t[:, :], ACT.Sigmoid)
            last.then_inc(sig, 1)
            act.wait_ge(clipped, 1)
            nc.scalar.activation(dl[:, :], dl[:, :], ACT.Ln)
            nc.scalar.activation(dlb[:, :], dlb[:, :], ACT.Ln).then_inc(lned, 1)
            act.wait_ge(ready, 1)
            act.drain()
            for t in (tQ[:, :], tQ2[:, :], tK[:, :, :], gP[:, :]):
                nc.scalar.activation(t, t, ACT.Exp, scale=dl[:, :])
            nc.scalar.activation(tK2[:, :], tK2[:, :], ACT.Exp)
            act.drain()
            for t in (tQ, tQ2):
                nc.scalar.activation(t[:, :], t[:, :], ACT.Copy, scale=al[:, :])

        @block.vector
        def _(v):
            nc.vector.tensor_tensor(sq[:, :, :], qk[:, :, :], qk[:, :, :], ALU.mult)
            v.drain()
            nc.vector.tensor_reduce(rn[:, :, :], sq[:, :, :].rearrange("p t (s r) -> p t s r", s=2), AX.X,
                                    ALU.add).then_inc(squared, 1)
            v.wait_ge(sig, 1)
            for t in (dl, dlb):
                last = nc.vector.tensor_scalar(t[:, :], t[:, :], 0.15, 1.0, ALU.max, ALU.min)
            last.then_inc(clipped, 1)
            v.wait_ge(counted, 2)
            nc.vector.tensor_scalar(tK[:, :, :], tK[:, :, :], float(1 - SUB), None, ALU.max)
            v.wait_ge(lned, 1)
            nc.vector.tensor_scalar(tK2[:, :], dlb[:, :], jcol[:, :], None, ALU.mult).then_inc(ready, 1)
            nc.vector.tensor_scalar(g[:, :], g[:, :], gate[:, :], None, ALU.mult)
            v.wait_ge(rooted, 1)
            nc.vector.tensor_scalar(rn[:, :, :], rn[:, :, :], 1e-8, None, ALU.max)
            v.drain()
            nc.vector.reciprocal(rn[:, :, :], rn[:, :, :])


def decay_mix(nc, net, a, R, K, SUB, h, hn, qk, rn, g, tQ, tQ2, tK, gP, tK2, causal):
    NB = P // SUB
    with ExitStack() as ctx:
        p = Scope(nc, ctx, "a3x")
        two = lambda n, s, q=P: [p.sb(f"{n}{i}", [q, *s]) for i in range(2)]
        proj, pb, mb = p.sb("proj", [P, D]), p.sb("pb", [P, D]), p.sb("mb", [P, D])
        hc, qc, kk = two("hc", [TC, D]), two("qc", [TC, 2 * R]), two("kk", [TC, R])
        Qp, Qpp, Kp = two("Qp", [S], R), two("Qpp", [S], R), two("Kp", [NB, S], R)
        AT, SS, T = two("AT", [S]), two("SS", [TC, D], R), two("T", [S])
        tq, tk, aps, sps = p.ps("tq"), p.ps("tk"), p.ps("aps"), p.ps("sps", [P, TC, D])
        dps, ops = [p.ps(f"dps{i}") for i in range(2)], [p.ps(f"ops{i}") for i in range(2)]
        loaded, bias_added, hc_done, qc_done, t_ready, tab_done = (
            p.sem(n) for n in ("loaded", "bias_added", "hc_done", "qc_done", "t_ready", "tab_done"))
        a_done, am_done, dec_done, conv_done, proj_done, add_done = (
            p.sem(n) for n in ("a_done", "am_done", "dec_done", "conv_done", "proj_done", "add_done"))
        block = ctx.enter_context(nc.Block())

        @block.sync
        def _(sp):
            sp.dma_start(proj[:, :], a("proj_w")).then_inc(loaded, 16)
            sp.dma_start(pb[:, :], row(a("proj_b")).to_broadcast([P, D])).then_inc(loaded, 16)
            sp.dma_start(mb[:, :], row(a("mlp_b2")).to_broadcast([P, D])).then_inc(loaded, 16)

        @block.gpsimd
        def _(pool):
            pool.wait_ge(loaded, 48)
            nc.gpsimd.tensor_tensor(h[:, :, :], h[:, :, :], over_tiles(pb[:, :], NT), ALU.add).then_inc(bias_added, 1)
            nc.gpsimd.tensor_tensor(net.x[:, :, :], net.x[:, :, :], over_tiles(mb[:, :], NT), ALU.add).then_inc(bias_added, 1)
            pool.wait_ge(bias_added, 2)
            with pool.Fori(0, B) as c:
                pool.wait_ge(add_done, c + 3)
                xt = net.x[:, bass.ts(c, 4), :]
                nc.gpsimd.tensor_tensor(xt, xt, h[:, bass.ts(c, 4), :], ALU.add)

        @block.scalar
        def _(act):
            with act.Fori(0, B // 2) as i:
                for par in range(2):
                    c = 2 * i + par
                    act.wait_ge(dec_done, c + 1)
                    nc.scalar.activation(hc[par][:, :, :], hn[:, bass.ts(c, 4), :], ACT.Copy).then_inc(hc_done, 1)

        @block.tensor
        def _(pe):
            pe.wait_ge(loaded, 48)
            pe.sem_inc(t_ready, 2)
            pe.sem_inc(a_done, 2)
            pe.sem_inc(dec_done, 2)
            pe.sem_inc(proj_done, 2)

            def turn(c, par):
                pe.wait_ge(qc_done, c + 1)
                pe.wait_ge(tab_done, c + 1)
                for k in range(TC):
                    tok = slice(k * P, (k + 1) * P)
                    nc.tensor.transpose(tq[0:R, tok], qc[par][:, k, 0:R], net.ident[:, :])
                    last = nc.tensor.transpose(tk[0:R, tok], qc[par][:, k, R:2 * R], net.ident[:, :])
                last.then_inc(t_ready, 1)

            def inside(c, par):
                pe.wait_ge(hc_done, c + 1)
                pe.wait_ge(am_done, c + 1)
                pe.wait_ge(tab_done, c + 2)
                for k in range(TC - 1):
                    nc.tensor.matmul(sps[0:R, k, :], kk[par][:, k, :], hc[par][:, k, :], start=True, stop=True)
                for k in range(TC):
                    for b in range(NB):
                        sub = slice(k * P + b * SUB, k * P + (b + 1) * SUB)
                        last = nc.tensor.matmul(aps[:, sub], Kp[par][0:R, b, k * P:(k + 1) * P], Qp[par][0:R, sub],
                                                start=True, stop=True)
                last.then_inc(a_done, 1)

            def across(c, par):
                pe.wait_ge(am_done, c + 2)
                pe.wait_ge(conv_done, c + 1)
                for k in range(TC):
                    tok = slice(k * P, (k + 1) * P)
                    last = nc.tensor.matmul(dps[par][:, tok], hc[par][:, k, :], AT[par][:, tok], start=True, stop=(k == 0))
                    if k > 0:
                        last = nc.tensor.matmul(dps[par][:, tok], SS[par][0:R, k, :], Qpp[par][0:R, tok],
                                                start=False, stop=True)
                last.then_inc(dec_done, 1)

            def project(c, par):
                pe.wait_ge(conv_done, c + 3)
                pe.wait_ge(add_done, c + 1)
                for k in range(TC):
                    tok = slice(k * P, (k + 1) * P)
                    last = nc.tensor.matmul(ops[par][:, tok], T[par][:, tok], proj[:, :], start=True, stop=True)
                last.then_inc(proj_done, 1)

            skewed(pe, (across, 0), (project, -1), (turn, 2), (inside, 1))

        @block.vector
        def _(v):
            tt, stt = nc.vector.tensor_tensor, nc.vector.scalar_tensor_tensor
            v.sem_inc(tab_done, 1)
            v.sem_inc(am_done, 1)
            v.sem_inc(conv_done, 2)
            v.sem_inc(add_done, 2)

            def unit_norm(c, par):
                v.wait_ge(t_ready, c + 1)
                tt(qc[par][:, :, :].rearrange("p t (s r) -> p (t s) r", s=2),
                   qk[:, bass.ts(c, 4), :].rearrange("p t (s r) -> p (t s) r", s=2),
                   bcast(rn[:, bass.ts(c, 4), :].rearrange("p t s -> p (t s)"), R), ALU.mult).then_inc(qc_done, 1)
                v.drain()

            def factors(c, par):
                v.wait_ge(a_done, c + 1)
                tt(kk[par][:, :, :], qc[par][:, :, R:2 * R], over_tiles(tK2[:, :], TC), ALU.mult)
                v.wait_ge(t_ready, c + 3)
                v.wait_ge(dec_done, c + 1)
                tiles = lambda t: t.rearrange("r (t i) -> r t i", i=P)
                tt(tiles(Qp[par][:, :]), tiles(tq[0:R, :]), over_tiles(tQ[:, :], TC), ALU.mult)
                tt(tiles(Qpp[par][:, :]), tiles(tq[0:R, :]), over_tiles(tQ2[:, :], TC), ALU.mult)
                for b in range(NB):
                    last = tt(tiles(Kp[par][:, b, :]), tiles(tk[0:R, :]), over_tiles(tK[:, b, :], TC), ALU.mult)
                last.then_inc(tab_done, 1)

            def inside(c, par):
                v.wait_ge(a_done, c + 3)
                tt(AT[par][:, :].rearrange("j (t i) -> j t i", i=P), aps[:, :].rearrange("j (t i) -> j t i", i=P),
                   over_tiles(causal[:, :], TC), ALU.mult)
                nc.vector.tensor_copy(SS[par][:, 1, :], sps[0:R, 0, :])
                v.drain()
                stt(SS[par][:, 2, :], SS[par][:, 1, :], gP[:, :], sps[0:R, 1, :], ALU.mult, ALU.add)
                v.drain()
                stt(SS[par][:, 3, :], SS[par][:, 2, :], gP[:, :], sps[0:R, 2, :], ALU.mult, ALU.add).then_inc(am_done, 1)

            def across(c, par):
                v.wait_ge(dec_done, c + 3)
                v.wait_ge(proj_done, c + 1)
                t = T[par]
                stt(t[:, :], net.xT[:, bass.ts(c, S)], g[:, 0:1], dps[par][:, :], ALU.mult, ALU.add)
                v.drain()
                for j in range(1, K):
                    last = stt(t[:, j:], net.xT[:, bass.ds(c * S, S - j)], g[:, j:j + 1], t[:, j:], ALU.mult, ALU.add)
                    if j == K - 1:
                        last.then_inc(conv_done, 1)
                    v.drain()

            def add_output(c, par):
                v.wait_ge(proj_done, c + 3)
                v.wait_ge(bias_added, 2)
                ht = h[:, bass.ts(c, 4), :].rearrange("p a b -> p (a b)")
                tt(ht, ht, ops[par][:, :], ALU.add).then_inc(add_done, 1)

            skewed(v, (unit_norm, 2), (factors, 1), (across, 0), (inside, 1), (add_output, -1))


def moe_linear(nc, net, d):
    E = d["L3_ffn_b"].shape[0]
    with ExitStack() as ctx:
        r = Router(nc, ctx, "m3", E)
        normalise_and_route(nc, net, "m3", d["L3_ffn_wg"], E, r.lg)
        top1_prob(nc, r, "m3")
        capacity_by_order(nc, net, r, B * S // E, "m3")
        moe_linear_products(nc, net, d, r, E)
        gated_bias(nc, net, "m3", r.gate, d["L3_ffn_b"])


def moe_linear_products(nc, net, d, r, E):
    with ExitStack() as ctx:
        p = Scope(nc, ctx, "m3e")
        WT = p.sb("WT", [P, E, D])
        xc = [p.sb(f"xc{i}", [P, S]) for i in range(2)]
        yps = [p.ps(f"yps{i}", [P, E, D]) for i in range(TC)]
        loaded = p.sem("loaded")
        xc_done = p.sem("xc_done")
        y_done = p.sem("y_done")
        y_used = p.sem("y_used")
        block = ctx.enter_context(nc.Block())

        @block.sync
        def _(sp):
            sp.dma_start(WT[:, :, :], d["L3_ffn_W"]).then_inc(loaded, 16)

        @block.tensor
        def _(pe):
            pe.wait_ge(loaded, 16)
            pe.sem_inc(y_done, 5)

            def products(c, par):
                pe.wait_ge(xc_done, c + 1)
                for k in range(TC):
                    pe.wait_ge(y_used, 4 * c + k + 1)
                    for q in range(2):
                        last = nc.tensor.matmul(yps[k][:, 4 * q:4 * q + 4, :].rearrange("p e d -> p (e d)"),
                                                xc[par][:, k * P:(k + 1) * P],
                                                WT[:, 4 * q:4 * q + 4, :].rearrange("p e d -> p (e d)"),
                                                start=True, stop=True)
                    last.then_inc(y_done, 1)

            with pe.Fori(0, B // 2) as i:
                for par in range(2):
                    products(2 * i + par, par)

        @block.scalar
        def _(act):
            with act.Fori(0, B // 2) as i:
                for par in range(2):
                    c = 2 * i + par
                    act.wait_ge(y_done, 4 * c + 1)
                    nc.scalar.activation(xc[par][:, :], net.xT[:, bass.ts(c, S)], ACT.Copy).then_inc(xc_done, 1)

        @block.vector
        def _(v):
            v.sem_inc(y_used, TC)
            with v.Fori(0, B) as c:
                for k in range(0, TC, 2):
                    v.wait_ge(y_done, 4 * c + k + 7)
                    for e in range(E):
                        for t in (k, k + 1):
                            xt = net.x[:, 4 * c + t, :]
                            last = nc.vector.scalar_tensor_tensor(xt, yps[t][:, e, :], r.gate[:, 4 * c + t, e:e + 1],
                                                                  xt, ALU.mult, ALU.add)
                            if e == E - 1:
                                last.then_inc(y_used, 1)
                        v.drain()


def program(nc, d, out):
    Scope.used = []
    with ExitStack() as ctx:
        net = Net(nc, ctx)
        load_and_measure(nc, net, d["L0_attn_x"])
        relative_attention(nc, net, d)
        renew_semaphores(nc)
        moe_capacity_relu(nc, net, d)
        renew_semaphores(nc)
        phase_memory(nc, net, d)
        renew_semaphores(nc)
        moe_grouped_swiglu(nc, net, d)
        renew_semaphores(nc)
        causal_attention(nc, net, d)
        renew_semaphores(nc)
        moe_top1_gelu(nc, net, d)
        renew_semaphores(nc)
        decay_attention(nc, net, d)
        renew_semaphores(nc)
        moe_linear(nc, net, d)
        store(nc, net, out)


def tables():
    import numpy as np
    HD = 8
    div = np.exp(np.arange(0, HD, 2, dtype=np.float64) * (-np.log(10000.0) / HD))
    angle = np.arange(512)[None, :] * div[:, None]
    t = np.stack([np.sin(angle), np.cos(angle)], axis=1).reshape(HD, 512)
    m1, m2 = np.zeros((HD, HD)), np.zeros((HD, HD))
    for m in range(HD // 2):
        s, c = 2 * m, 2 * m + 1
        m1[s, c] = m1[c, c] = 1
        m2[s, s], m2[c, s] = 1, -1
    return {"rel_t": t.astype(np.float32), "rel_m1": m1.astype(np.float32), "rel_m2": m2.astype(np.float32)}


def laid_out(name, a):
    import numpy as np
    if name in ("L0_ffn_router_w", "L1_ffn_gate_w", "L3_attn_proj_w"):
        a = a.T
    elif name in ("L0_attn_w_qkv", "L0_attn_b_qkv"):
        a = a.reshape(a.shape[:-1] + (3, 16, 8))
        a = np.stack([np.swapaxes(a[..., 0, :, :], -1, -2).reshape(a.shape[:-3] + (128,)),
                      np.swapaxes(a[..., 1, :, :], -1, -2).reshape(a.shape[:-3] + (128,)),
                      a[..., 2, :, :].reshape(a.shape[:-3] + (128,))], axis=-2)
    elif name == "L3_ffn_W":
        a = a.transpose(2, 0, 1)
    elif name == "L2_ffn_b1":
        a = a.reshape(a.shape[0], -1, 128).transpose(0, 2, 1)
    elif name == "L3_attn_mlp_b1":
        a = a.reshape(-1, 128).T
    elif a.ndim == 0:
        a = a.reshape(1)
    return np.ascontiguousarray(a)


def kernel(**inputs):
    import numpy as _np
    import concourse.bacc as _bacc
    from concourse import mybir as _mybir
    from concourse.bass_utils import run_bass_kernel_spmd as _run

    nc = _bacc.Bacc("TRN2", target_bir_lowering=False, num_devices=1)
    arrays, dram = {}, {}
    for name in inputs:
        a = laid_out(name, _np.asarray(inputs[name]))
        arrays[f"in_{name}"] = a
        dram[name] = nc.dram_tensor(f"in_{name}", a.shape, _mybir.dt.from_np(a.dtype), kind="ExternalInput").ap()
    for name, a in tables().items():
        arrays[f"tab_{name}"] = a
        dram[name] = nc.dram_tensor(f"tab_{name}", a.shape, _mybir.dt.from_np(a.dtype), kind="ExternalInput").ap()
    out = nc.dram_tensor("out_x", (B, S, D), _mybir.dt.float32, kind="ExternalOutput").ap()
    program(nc, dram, out)
    return _run(nc, [arrays], core_ids=[0]).results[0]["out_x"]
```
